# Optimizing a Trainium2 kernel written in Bass

```python
import numpy as np
import jax
import jax.numpy as jnp

def _softmax(x, axis=-1):
    return jax.nn.softmax(x, axis=axis)

def _gelu(x):
    return jax.nn.gelu(x, approximate=True)

def _silu(x):
    return jax.nn.silu(x)

def _sigmoid(x):
    return jax.nn.sigmoid(x)

def _layernorm(x, axis=-1, eps=1e-05):
    m = jnp.mean(x, axis=axis, keepdims=True)
    v = jnp.var(x, axis=axis, keepdims=True)
    return (x - m) / jnp.sqrt(v + eps)

def _scatter_add(tgt, idx, src, axis=0):
    return tgt.at[idx].add(src)

def _segment_sum(src, seg, n):
    return jax.ops.segment_sum(src, seg, n)
kernel_name = 'mk_adaln_d2_jaxref_r8_7258cf'

def setup_inputs(seed: int=0):
    np.random.seed(seed)
    _w = jnp.asarray

    def _L0_attn_setup():
        import jax, jax.numpy as jnp
        import numpy as np
        B, L, D = (2, 256, 128)
        H, HD = (16, 64)
        LD = 32
        key = jax.random.key(seed)
        ks = jax.random.split(key, 6)
        s = lambda fan_in: 1.0 / np.sqrt(fan_in)
        x_bld = jax.random.normal(ks[0], (B, L, D), dtype=jnp.float32)
        Wq = jax.random.normal(ks[1], (D, H, HD), dtype=jnp.float32) * s(D)
        Wkv_down = jax.random.normal(ks[2], (D, LD), dtype=jnp.float32) * s(D)
        Wk_up = jax.random.normal(ks[3], (LD, H, HD), dtype=jnp.float32) * s(LD)
        Wv_up = jax.random.normal(ks[4], (LD, H, HD), dtype=jnp.float32) * s(LD)
        Wout = jax.random.normal(ks[5], (H, HD, D), dtype=jnp.float32) * s(H * HD)
        return {'x_bld': x_bld, 'Wq': Wq, 'Wkv_down': Wkv_down, 'Wk_up': Wk_up, 'Wv_up': Wv_up, 'Wout': Wout}
    _L0_attn_in = _L0_attn_setup()

    def _L0_ffn_setup():
        import jax, jax.numpy as jnp
        import numpy as np
        B, S, D = (8, 512, 128)
        E, R, K = (6, 16, 2)
        key = jax.random.key(seed)
        ks = jax.random.split(key, 9)
        sc = 0.02
        return {'x': jax.random.normal(ks[0], (B, S, D), jnp.float32), 'base_W': jax.random.normal(ks[1], (D, D), jnp.float32) * sc, 'base_b': jax.random.normal(ks[2], (D,), jnp.float32) * sc, 'shared_A': jax.random.normal(ks[3], (R, D), jnp.float32) * sc, 'shared_B': jax.random.normal(ks[4], (D, R), jnp.float32) * sc, 'routed_A': jax.random.normal(ks[5], (E, R, D), jnp.float32) * sc, 'routed_B': jax.random.normal(ks[6], (E, D, R), jnp.float32) * sc, 'router_W': jax.random.normal(ks[7], (E, D), jnp.float32) * sc, 'router_b': jax.random.normal(ks[8], (E,), jnp.float32) * sc}
    _L0_ffn_in = _L0_ffn_setup()
    _L0_c = _w((lambda *s: np.random.randn(*s).astype(np.float32) * 0.05)(2, 128))
    _L0_wmod = _w((lambda *s: np.random.randn(*s).astype(np.float32) * 0.05)(128, 6 * 128) * 128 ** (-0.5))

    def _L1_attn_setup():
        import jax, jax.numpy as jnp
        import numpy as np
        WINDOW = 64
        SHIFT = 32
        HEADS = 8
        key = jax.random.key(seed)
        k1, k2, k3 = jax.random.split(key, 3)
        B, L, D = (8, 512, 128)
        scale = 0.02
        return {'x': jax.random.normal(k1, (B, L, D), dtype=jnp.float32), 'in_proj_w': jax.random.normal(k2, (3 * D, D), dtype=jnp.float32) * scale, 'in_proj_b': jnp.zeros((3 * D,), dtype=jnp.float32), 'out_w': jax.random.normal(k3, (D, D), dtype=jnp.float32) * scale, 'out_b': jnp.zeros((D,), dtype=jnp.float32)}
    _L1_attn_in = _L1_attn_setup()

    def _L1_ffn_setup():
        import jax, jax.numpy as jnp
        import numpy as np
        LOOPS = 2
        NUM_GROUPS = 4
        EXPERTS_PER_GROUP = 2
        NUM_EXPERTS = NUM_GROUPS * EXPERTS_PER_GROUP
        GROUPS_TOP_K = 2
        TOP_K = 1
        RMS_EPS = 1e-06
        EPS = 1e-09

        def _rmsnorm(x, w):
            return x * jax.lax.rsqrt(jnp.mean(x * x, axis=-1, keepdims=True) + RMS_EPS) * w

        def _combine_weights(x_flat, w_macro, w_micro):
            T = x_flat.shape[0]
            macro = jax.nn.softmax(x_flat @ w_macro.T, axis=-1)
            mvals, midx = jax.lax.top_k(macro, GROUPS_TOP_K)
            mvals = mvals / (jnp.sum(mvals, axis=-1, keepdims=True) + EPS)
            micro = jax.nn.softmax(jnp.einsum('td,ged->tge', x_flat, w_micro), axis=-1)
            uvals, uidx = jax.lax.top_k(micro, TOP_K)
            uvals = uvals / (jnp.sum(uvals, axis=-1, keepdims=True) + EPS)
            tok = jnp.arange(T)
            combine = jnp.zeros((T, NUM_EXPERTS), x_flat.dtype)
            for s in range(GROUPS_TOP_K):
                g = midx[:, s]
                wg = mvals[:, s:s + 1]
                li = uidx[tok, g]
                lv = uvals[tok, g]
                eidx = g[:, None] * EXPERTS_PER_GROUP + li
                combine = combine.at[tok[:, None], eidx].add(lv * wg)
            return combine
        key = jax.random.key(seed)
        ks = jax.random.split(key, 6)
        B, S, D, F = (2, 128, 128, 256)
        return {'z': jax.random.normal(ks[0], (B, S, D), jnp.float32), 'norm_w': jnp.ones((D,), jnp.float32), 'w_macro': jax.random.normal(ks[1], (NUM_GROUPS, D), jnp.float32) * D ** (-0.5), 'w_micro': jax.random.normal(ks[2], (NUM_GROUPS, EXPERTS_PER_GROUP, D), jnp.float32) * D ** (-0.5), 'w1': jax.random.normal(ks[3], (NUM_EXPERTS, F, D), jnp.float32) * D ** (-0.5), 'w2': jax.random.normal(ks[4], (NUM_EXPERTS, D, F), jnp.float32) * F ** (-0.5)}
    _L1_ffn_in = _L1_ffn_setup()
    _L1_c = _w((lambda *s: np.random.randn(*s).astype(np.float32) * 0.05)(2, 128))
    _L1_wmod = _w((lambda *s: np.random.randn(*s).astype(np.float32) * 0.05)(128, 6 * 128) * 128 ** (-0.5))
    _d = {'L0_attn_x_bld': _L0_attn_in['x_bld'], 'L0_attn_Wq': _L0_attn_in['Wq'], 'L0_attn_Wkv_down': _L0_attn_in['Wkv_down'], 'L0_attn_Wk_up': _L0_attn_in['Wk_up'], 'L0_attn_Wv_up': _L0_attn_in['Wv_up'], 'L0_attn_Wout': _L0_attn_in['Wout'], 'L0_ffn_base_W': _L0_ffn_in['base_W'], 'L0_ffn_base_b': _L0_ffn_in['base_b'], 'L0_ffn_shared_A': _L0_ffn_in['shared_A'], 'L0_ffn_shared_B': _L0_ffn_in['shared_B'], 'L0_ffn_routed_A': _L0_ffn_in['routed_A'], 'L0_ffn_routed_B': _L0_ffn_in['routed_B'], 'L0_ffn_router_W': _L0_ffn_in['router_W'], 'L0_ffn_router_b': _L0_ffn_in['router_b'], 'L0_c': _L0_c, 'L0_wmod': _L0_wmod, 'L1_attn_in_proj_w': _L1_attn_in['in_proj_w'], 'L1_attn_in_proj_b': _L1_attn_in['in_proj_b'], 'L1_attn_out_w': _L1_attn_in['out_w'], 'L1_attn_out_b': _L1_attn_in['out_b'], 'L1_ffn_norm_w': _L1_ffn_in['norm_w'], 'L1_ffn_w_macro': _L1_ffn_in['w_macro'], 'L1_ffn_w_micro': _L1_ffn_in['w_micro'], 'L1_ffn_w1': _L1_ffn_in['w1'], 'L1_ffn_w2': _L1_ffn_in['w2'], 'L1_c': _L1_c, 'L1_wmod': _L1_wmod}
    _x0 = _d['L0_attn_x_bld']
    _d['L0_attn_x_bld'] = jax.random.normal(jax.random.fold_in(jax.random.key(seed), 1), (2, 1024, 128), dtype=_x0.dtype)
    del _x0
    return _d

def reference(L0_attn_x_bld, L0_attn_Wq, L0_attn_Wkv_down, L0_attn_Wk_up, L0_attn_Wv_up, L0_attn_Wout, L0_ffn_base_W, L0_ffn_base_b, L0_ffn_shared_A, L0_ffn_shared_B, L0_ffn_routed_A, L0_ffn_routed_B, L0_ffn_router_W, L0_ffn_router_b, L0_c, L0_wmod, L1_attn_in_proj_w, L1_attn_in_proj_b, L1_attn_out_w, L1_attn_out_b, L1_ffn_norm_w, L1_ffn_w_macro, L1_ffn_w_micro, L1_ffn_w1, L1_ffn_w2, L1_c, L1_wmod):

    def _L0_attn_ref(x_bld, Wq, Wkv_down, Wk_up, Wv_up, Wout):
        import jax, jax.numpy as jnp
        import numpy as np
        B, L, D = (2, 256, 128)
        H, HD = (16, 64)
        LD = 32
        q_blhd = jnp.einsum('bld,dhk->blhk', x_bld, Wq)
        latent_bll = jnp.einsum('bld,dc->blc', x_bld, Wkv_down)
        k_blhd = jnp.einsum('blc,chk->blhk', latent_bll, Wk_up)
        v_blhd = jnp.einsum('blc,chk->blhk', latent_bll, Wv_up)
        attn = jnp.einsum('bqhd,bkhd->bhqk', q_blhd, k_blhd) / jnp.sqrt(jnp.asarray(HD, dtype=x_bld.dtype))
        l = x_bld.shape[1]
        mask = (jnp.arange(l)[None, :] <= jnp.arange(l)[:, None])[None, None]
        neg_inf = jnp.finfo(attn.dtype).min
        attn = jax.nn.softmax(jnp.where(mask, attn, neg_inf), axis=-1)
        y_blhd = jnp.einsum('bhqk,bkhd->bqhd', attn, v_blhd)
        return jnp.einsum('bqhd,hdo->bqo', y_blhd, Wout)

    def _L0_ffn_ref(x, base_W, base_b, shared_A, shared_B, routed_A, routed_B, router_W, router_b):
        import jax, jax.numpy as jnp
        import numpy as np
        B, S, D = (8, 512, 128)
        E, R, K = (6, 16, 2)
        base_out = jax.lax.stop_gradient(jnp.einsum('bsi,oi->bso', x, base_W) + base_b)
        shared_out = jnp.einsum('bsr,or->bso', jnp.einsum('bsi,ri->bsr', x, shared_A), shared_B)
        logits = jnp.einsum('bsi,ei->bse', x, router_W) + router_b
        gate = jax.nn.softmax(logits, axis=-1)
        topk_w, topk_i = jax.lax.top_k(gate, K)
        sparse_w = jnp.sum(jax.nn.one_hot(topk_i, E, dtype=gate.dtype) * topk_w[..., None], axis=-2)
        sparse_w = sparse_w / (jnp.sum(sparse_w, axis=-1, keepdims=True) + 1e-06)
        h = jnp.einsum('bsi,eri->bser', x, routed_A)
        routed_outs = jnp.einsum('bser,eor->bseo', h, routed_B)
        routed_out = jnp.einsum('bseo,bse->bso', routed_outs, sparse_w)
        return base_out + shared_out + routed_out

    def _L1_attn_ref(x, in_proj_w, in_proj_b, out_w, out_b):
        import jax, jax.numpy as jnp
        import numpy as np
        WINDOW = 64
        SHIFT = 32
        HEADS = 8
        B, L, D = x.shape
        H, W, S = (HEADS, WINDOW, SHIFT)
        hd = D // H
        xs = jnp.roll(x, -S, axis=1)
        nw = L // W
        xw = xs.reshape(B * nw, W, D)
        qkv = xw @ in_proj_w.T + in_proj_b
        q, k, v = jnp.split(qkv, 3, axis=-1)

        def to_heads(t):
            return t.reshape(-1, W, H, hd).transpose(0, 2, 1, 3)
        q, k, v = (to_heads(q), to_heads(k), to_heads(v))
        scores = jnp.einsum('nhqd,nhkd->nhqk', q, k) * (1.0 / np.sqrt(hd))
        attn = jax.nn.softmax(scores, axis=-1)
        o = jnp.einsum('nhqk,nhkd->nhqd', attn, v)
        o = o.transpose(0, 2, 1, 3).reshape(-1, W, D)
        o = o @ out_w.T + out_b
        o = o.reshape(B, L, D)
        o = jnp.roll(o, S, axis=1)
        return o + o

    def _L1_ffn_ref(z, norm_w, w_macro, w_micro, w1, w2):
        import jax, jax.numpy as jnp
        import numpy as np
        LOOPS = 2
        NUM_GROUPS = 4
        EXPERTS_PER_GROUP = 2
        NUM_EXPERTS = NUM_GROUPS * EXPERTS_PER_GROUP
        GROUPS_TOP_K = 2
        TOP_K = 1
        RMS_EPS = 1e-06
        EPS = 1e-09

        def _rmsnorm(x, w):
            return x * jax.lax.rsqrt(jnp.mean(x * x, axis=-1, keepdims=True) + RMS_EPS) * w

        def _combine_weights(x_flat, w_macro, w_micro):
            T = x_flat.shape[0]
            macro = jax.nn.softmax(x_flat @ w_macro.T, axis=-1)
            mvals, midx = jax.lax.top_k(macro, GROUPS_TOP_K)
            mvals = mvals / (jnp.sum(mvals, axis=-1, keepdims=True) + EPS)
            micro = jax.nn.softmax(jnp.einsum('td,ged->tge', x_flat, w_micro), axis=-1)
            uvals, uidx = jax.lax.top_k(micro, TOP_K)
            uvals = uvals / (jnp.sum(uvals, axis=-1, keepdims=True) + EPS)
            tok = jnp.arange(T)
            combine = jnp.zeros((T, NUM_EXPERTS), x_flat.dtype)
            for s in range(GROUPS_TOP_K):
                g = midx[:, s]
                wg = mvals[:, s:s + 1]
                li = uidx[tok, g]
                lv = uvals[tok, g]
                eidx = g[:, None] * EXPERTS_PER_GROUP + li
                combine = combine.at[tok[:, None], eidx].add(lv * wg)
            return combine
        B, S, D = z.shape
        T = B * S
        for _ in range(LOOPS):
            zn = _rmsnorm(z, norm_w)
            x = zn.reshape(T, D)
            combine = _combine_weights(x, w_macro, w_micro)
            h = jax.nn.silu(jnp.einsum('td,efd->tef', x, w1))
            y = jnp.einsum('tef,edf->ted', h, w2)
            mixed = jnp.einsum('ted,te->td', y, combine)
            z = z + mixed.reshape(B, S, D)
        return z
    x = L0_attn_x_bld
    mod = (_silu(L0_c) @ L0_wmod).reshape(L0_c.shape[0], 6, 1, -1)
    sa, ca, ga, sb, cb, gb = (mod[:, 0], mod[:, 1], mod[:, 2], mod[:, 3], mod[:, 4], mod[:, 5])
    ga = (2 * (ga >= 0) - 1) * jnp.maximum(jnp.abs(ga), 0.25)
    gb = (2 * (gb >= 0) - 1) * jnp.maximum(jnp.abs(gb), 0.25)
    h = _layernorm(x, axis=-1) * (1 + ca) + sa
    x = x + ga * _L0_attn_ref(h, L0_attn_Wq, L0_attn_Wkv_down, L0_attn_Wk_up, L0_attn_Wv_up, L0_attn_Wout)
    h = _layernorm(x, axis=-1) * (1 + cb) + sb
    x = x + gb * _L0_ffn_ref(h, L0_ffn_base_W, L0_ffn_base_b, L0_ffn_shared_A, L0_ffn_shared_B, L0_ffn_routed_A, L0_ffn_routed_B, L0_ffn_router_W, L0_ffn_router_b)
    mod = (_silu(L1_c) @ L1_wmod).reshape(L1_c.shape[0], 6, 1, -1)
    sa, ca, ga, sb, cb, gb = (mod[:, 0], mod[:, 1], mod[:, 2], mod[:, 3], mod[:, 4], mod[:, 5])
    ga = (2 * (ga >= 0) - 1) * jnp.maximum(jnp.abs(ga), 0.25)
    gb = (2 * (gb >= 0) - 1) * jnp.maximum(jnp.abs(gb), 0.25)
    h = _layernorm(x, axis=-1) * (1 + ca) + sa
    x = x + ga * _L1_attn_ref(h, L1_attn_in_proj_w, L1_attn_in_proj_b, L1_attn_out_w, L1_attn_out_b)
    h = _layernorm(x, axis=-1) * (1 + cb) + sb
    x = x + gb * _L1_ffn_ref(h, L1_ffn_norm_w, L1_ffn_w_macro, L1_ffn_w_micro, L1_ffn_w1, L1_ffn_w2)
    return x

_drawn_inputs = setup_inputs


def setup_inputs(seed=0):
    import zlib

    import numpy as np

    out = dict(_drawn_inputs(seed))
    spreads = {'L1_attn_in_proj_b': (0.0, 0.366),
     'L1_attn_out_b': (0.0, 0.1),
     'L1_ffn_norm_w': (1.0, 0.2)}
    factors = {'L0_ffn_base_b': 4.571,
     'L0_ffn_shared_A': 6.121,
     'L0_ffn_shared_B': 4.641,
     'L0_ffn_routed_A': 6.886,
     'L0_ffn_routed_B': 4.893,
     'L0_ffn_router_W': 7.342,
     'L0_ffn_router_b': 8.0,
     'L1_attn_in_proj_w': 5.936,
     'L1_attn_out_w': 2.756}
    for name, (base, spread) in spreads.items():
        noise = np.random.default_rng([zlib.crc32(name.encode()), seed]).standard_normal(out[name].shape)
        drawn = base * np.exp(spread * noise) if base else spread * noise
        out[name] = jnp.asarray(drawn.astype(out[name].dtype))
    for name, factor in factors.items():
        out[name] = (out[name] * factor).astype(out[name].dtype)
    return out
```

```python
from contextlib import ExitStack

import numpy as np

import concourse.bass as bass
from concourse import mybir

F32 = mybir.dt.float32
F16 = mybir.dt.float16
BF16 = mybir.dt.bfloat16
ALU = mybir.AluOpType
ACT = mybir.ActivationFunctionType
AX = mybir.AxisListType

P = 128
B, L, D = 2, 1024, 128
T = B * L
NT = T // P
CH = 512
NC = T // CH
H0, C0, HD0 = 16, 32, 64
GR = 4
NG = B * H0 // GR
QB = L // P
NH, HD1, WIN, SHIFT = 8, 16, 64, 32
NGR, E1, F1 = 4, 8, 256
UP = 64.0
NEG = -1e30
LN_EPS = 1e-5

TILES = [
    (0, [(0, 0, 0), (1, 128, 512)]),
    (0, [(2, 256, 0), (3, 384, 256)]),
    (1, [(0, 0, 0), (1, 0, 512)]),
    (1, [(2, 0, 0), (3, 0, 512)]),
    (1, [(4, 0, 0), (5, 128, 512)]),
    (1, [(6, 256, 0), (7, 384, 256)]),
]
NTL = len(TILES)
MASKED = {0: 0, 1: 1, 4: 2, 5: 3}
SUB = 2 * NTL
CHUNK_END = {1: 0, 5: 1}
FILLS = [(j, i, h) for j in range(GR) for i in range(QB) for h in range(1 + (i >= 4))]
NF = len(FILLS)
PER = 5


def fills_of(k):
    return list(range(PER * k, min(PER * k + PER, NF)))


def program(nc, a, out):
    with ExitStack() as ctx:
        def sb(name, shape, dt=F32):
            return ctx.enter_context(nc.sbuf_tensor(name, shape, dt))

        def sem(name):
            return ctx.enter_context(nc.semaphore(name))

        bank = [ctx.enter_context(nc.psum_tensor(f"bank{i}", [P, CH], F32)) for i in range(2)]
        stT = ctx.enter_context(nc.psum_tensor("stT", [P, 2, 2 * CH], F32))
        bankY = ctx.enter_context(nc.psum_tensor("bankY", [P, CH], F32))
        bankM = ctx.enter_context(nc.psum_tensor("bankM", [P, CH], F32))
        quad = [stT[:, i // 2, (i % 2) * CH:(i % 2 + 1) * CH] for i in range(4)]

        identf = sb("identf", [P, P])
        identb = sb("identb", [P, P], BF16)
        maskb = sb("maskb", [P, P], BF16)
        mean_w = sb("mean_w", [P, P])
        epsc = sb("epsc", [P, 2])
        x_rows = sb("x_rows", [P, NT, P])
        xT = sb("xT", [P, T])
        xc = sb("xc", [P, T])
        sq = sb("sq", [P, T])
        rstd = sb("rstd", [P, T])
        hT = sb("hT", [P, T])
        cT = sb("cT", [P, 2, B])
        csil = sb("csil", [P, 3, 2 * B])
        wmod = sb("wmod", [P, 2, 6 * D])
        mod = sb("mod", [P, 2, 6, B])
        sgn = sb("sgn", [P, 2, 2, B])
        E0, R0 = 6, 16
        NR = R0 * (E0 + 1)
        bwT = sb("bwT", [P, D])
        downT = sb("downT", [P, NR])
        up = sb("up", [NR, D])
        rw = sb("rw", [P, E0])
        rb = sb("rb", [P, E0])
        bb = sb("bb", [P, 1])
        earlier = sb("earlier", [P, E0, E0])
        wqkv = sb("wqkv", [P, 3 * D])
        bqkv = sb("bqkv", [P, 3])
        owT = sb("owT", [P, D])
        ob = sb("ob", [P, 1])
        head_of = sb("head_of", [P, NH])
        wv_eo = sb("wv_eo", [P, 2, NH // 2, 2 * HD1])
        bq_s = sb("bq_s", [P, 1])
        ga2 = sb("ga2", [P, B])
        nw = sb("nw", [P, 1])
        wrT = sb("wrT", [P, NGR + E1])
        spread = sb("spread", [104, E1, P], F16)

        attn = ExitStack()

        def sa(name, shape, dt=F32):
            return attn.enter_context(nc.sbuf_tensor(name, shape, dt))

        wqT = sa("wqT", [HD0, H0, D])
        wkT = sa("wkT", [HD0, H0, C0])
        wvT = sa("wvT", [HD0, H0, C0])
        wo = sa("wo", [HD0, H0, D])
        wkv = sa("wkv", [P, 3, C0])
        qk = sa("qk", [P, H0 * C0])
        vo = sa("vo", [P, H0 // GR, D])
        vo_now = sa("vo_now", [P, D])
        lat = sa("lat", [97, T], F16)
        latO = sa("latO", [P, NT, 2 * C0])
        q_hi = sa("q_hi", [P, 2, L], F16)
        q_lo = sa("q_lo", [P, 2, L], F16)
        q_st = sa("q_st", [97, B * H0, L], F16)
        probs = sa("probs", [P, 2, 2, 2 * CH])
        part_max = sa("part_max", [P, 2, GR, QB])
        row_max = sa("row_max", [P, GR * QB])
        neg_max = sa("neg_max", [GR * QB, P], F16)
        y_raw = sa("y_raw", [P, 2, CH])
        ln_sum = sa("ln_sum", [P, 2, CH])
        inv_sum = sa("inv_sum", [P, 2, CH])
        y_n = sa("y_n", [P, 2, CH])

        attn.close()

        lg = sb("lg", [P, NT, 12])
        pr = sb("pr", [P, NT, 12])
        st = sb("st", [P, 6, NT, 4])
        gt = sb("gt", [P, NT, 36])
        eq = sb("eq", [P, NT, 36])
        rank = sb("rank", [P, NT, 6])
        wts = sb("wts", [P, NT, 8])
        wx = sb("wx", [P, NT, NR])
        wxT = sb("wxT", [NR, T])
        lowr = sb("lowr", [NR, 2, CH])
        ffn = sb("ffn", [P, 2, CH])
        hwin = sb("hwin", [P, 2, P])
        qw = sb("qw", [P, 2, P])
        kw = sb("kw", [P, 2, P])
        kx = sb("kx", [P, 2, 2, NH, WIN])
        vw = sb("vw", [P, 2, 2, P])
        mx = sb("mx", [P, 2, NH])
        sub = sb("sub", [P, 2, NH, WIN])
        pw = sb("pw", [P, 2, NH, WIN])
        sm = sb("sm", [P, 2, NH])
        rs = sb("rs", [P, 2, NH])
        pn = sb("pn", [P, 2, NH * WIN])
        pT = sb("pT", [P, NH // 2 * P])
        w1 = sb("w1", [P, E1 * F1])
        w2 = sb("w2", [P, E1 * F1])
        w1h = sb("w1h", [P, 2, E1 * F1], F16)
        w2h = sb("w2h", [P, 2, E1 * F1], F16)
        xnh = sb("xnh", [P, 2, T], F16)
        cT16 = sb("cT16", [104, T], F16)
        hid = sb("hid", [P, 2, 2 * CH])
        hidh = sb("hidh", [P, 2, 2, 2 * CH], F16)
        cw = sb("cw", [P, 2, CH])
        yw = sb("yw", [P, 2, CH])

        S = {n: sem(n) for n in (
            "c_loaded", "w_attn_loaded", "consts", "csil_step", "silu_ready", "mod_product", "mod_ready",
            "gate_step", "x_turned", "xT_ready", "qk_product", "qk_ready", "vo_product", "vo_ready", "lat_product",
            "lat_hi", "lat_ready", "latO_product", "latO_ready", "q_product", "q_hi_ready", "q_lo_ready",
            "scores_ready", "max_taken", "row_max_ready", "max_turned", "neg_max_ready", "max_placed",
            "st_ready", "exp_done", "masked", "pv_done", "y_done", "ln_done", "y_copied", "inv_ready", "y_n_ready",
            "vo_now_ready", "pool_passed", "proj_done", "x_updated", "out_turned", "out_rows", "stored")}
        x_loaded = [sem(f"x_loaded{c}") for c in range(NC)]
        q_placed = [sem(f"q_placed{i}") for i in range(2)]
        N = {n: sem("n_" + n) for n in ("mean", "centred", "squared", "var", "ln", "rstd", "scaled", "h")}

        W = {n: sem("w_" + n) for n in (
            "small_loaded", "w12_loaded", "consts_b", "logits", "logit_ready", "exp_in", "exp_out", "weights_ready",
            "wx_turned", "wxT_ready", "low_product", "low_ready", "ffn_product", "ffn_ready", "x_ffn",
            "prep", "hwin_ready", "q_product", "k_product", "v_product", "q_ready", "k_biased", "k_ready", "v_ready", "s_product", "max_ready",
            "sub_ready", "exp_ready", "sum_ready", "inv_ready", "p_ready", "p_turned", "pT_ready", "o_product",
            "o_ready", "att_product", "att_ready", "x_att",
            "w_hi", "w_lo", "dchain", "pchain")}
        E = {n: sem("e_" + n) for n in (
            "xn_scaled", "xn", "xn_hi", "xn_lo", "logits", "exp_in", "exp_out", "weights_ready", "cw_turned", "c_hi", "c_lo", "pre", "act",
            "hid_hi", "hid_lo", "y", "cb", "cw", "yw", "z")}
        x_final = sem("x_final")

        x_dram = a["x"].rearrange("b (n p) d -> p (b n) d", p=P)
        out_dram = out.rearrange("b (n p) d -> p (b n) d", p=P)

        block = ctx.enter_context(nc.Block())

        def steps(eng, body):
            body(0, 0, None, None)
            body(1, 0, 0, None)
            with eng.Fori(2, 4) as s:
                body(s, 0, 0, 0)
            body(4, 1, 0, 0)
            body(5, 1, 1, 0)
            with eng.Fori(6, 8) as s:
                body(s, 1, 1, 1)
            body(8, None, 1, 1)
            body(9, None, None, 1)

        def norm_count(k, name, v):
            if name in ("squared", "var", "ln", "rstd"):
                return NC * k + v
            return NC * min(k, 3) + (2 if name == "h" and k == 3 else 0) + v

        def loop_count(k, name, v):
            once = ("exp_in", "exp_out", "logits", "weights_ready")
            return k * (1 if name in once else NC if name in per_chunk else NC * E1) + v

        per_chunk = ("xn", "xn_hi", "xn_lo", "cw_turned", "c_hi", "c_lo")

        def need(eng, s, v):
            if not isinstance(v, int) or v > 0:
                eng.wait_ge(s, v)

        def windows(eng, body):
            body(0, True, False, False, 0)
            body(1, True, True, False, 1)
            body(2, True, True, True, 0)
            body(3, True, True, True, 1)
            with eng.Fori(2, NT // 2) as n:
                body(2 * n, True, True, True, 0)
                body(2 * n + 1, True, True, True, 1)
            body(NT, False, True, True, 0)
            body(NT + 1, False, False, True, 1)

        def experts(eng, ahead, unit):
            def chunk(c, last):
                for e in range(E1):
                    if e < E1 - 1:
                        ahead(c, e + 1)
                    elif not last:
                        ahead(c + 1, 0)
                    unit(c, e)
            ahead(0, 0)
            chunk(0, False)
            with eng.Fori(1, NC - 1) as c:
                chunk(c, False)
            chunk(NC - 1, True)

        def shifted_pieces(c):
            b, at = c // 2, (c % 2) * CH
            if at == 0:
                return [((b + 1) * L - SHIFT, b * L, SHIFT), (b * L, b * L + SHIFT, CH - SHIFT)]
            return [(b * L + at - SHIFT, b * L + at, CH)]

        h2_count = sum(len(shifted_pieces(c)) for c in range(NC))
        oT = rstd
        z = hT

        @block.sync
        def _(sp):
            sp.dma_start(cT[:, 0, :], a["c0T"]).then_inc(S["c_loaded"], 16)
            sp.dma_start(cT[:, 1, :], a["c1T"]).then_inc(S["c_loaded"], 16)
            for c in range(NC):
                sp.dma_start(x_rows[:, 4 * c:4 * c + 4, :], x_dram[:, 4 * c:4 * c + 4, :]).then_inc(x_loaded[c], 16)
                if c == 0:
                    sp.dma_start(wmod[:, 0, :], a["wmod0"]).then_inc(S["c_loaded"], 16)
                    sp.dma_start(wmod[:, 1, :], a["wmod1"]).then_inc(S["c_loaded"], 16)
            sp.dma_start(wqT[:], a["wqT"]).then_inc(S["w_attn_loaded"], 16)
            sp.dma_start(wkT[:], a["wkT"]).then_inc(S["w_attn_loaded"], 16)
            sp.dma_start(wvT[:], a["wvT"]).then_inc(S["w_attn_loaded"], 16)
            sp.dma_start(wo[:], a["wo"]).then_inc(S["w_attn_loaded"], 16)
            for r in range(3):
                sp.dma_start(wkv[:, r, :], a["wkv"]).then_inc(S["w_attn_loaded"], 16)
            for dst, name in ((bwT, "bwT"), (downT, "downT"), (up, "up"), (rw, "rw"), (bb, "bb"), (wqkv, "wqkv"),
                              (bqkv, "bqkv"), (owT, "owT"), (ob, "ob"), (nw, "nw"), (wrT, "wrT")):
                sp.dma_start(dst[:], a[name]).then_inc(W["small_loaded"], 16)
            sp.dma_start(rb[:], a["rb"].partition_broadcast(P)).then_inc(W["small_loaded"], 16)
            for g in range(NG):
                sp.wait_ge(S["q_hi_ready"], 2 * (g + 1))
                sp.wait_ge(S["q_lo_ready"], 2 * (g + 1))
                for row, src in ((0, q_hi), (C0, q_lo), (2 * C0, q_hi)):
                    for j in range(GR):
                        sp.dma_start(q_st[row:row + C0, GR * g + j, :], src[C0 * j:C0 * j + C0, g % 2, :])\
                          .then_inc(q_placed[g % 2], 16)

            def body(s, bm, be, bp):
                if bm is not None:
                    sp.wait_ge(S["neg_max_ready"], s + 1)
                    sp.dma_start(q_st[96:97, bass.ds(GR * s, GR), :].rearrange("o j (i t) -> o (j i) t", t=P),
                                 neg_max[:, :]).then_inc(S["max_placed"], 16)
            steps(sp, body)
            sp.wait_ge(S["x_updated"], 2 * NG)
            sp.dma_start(w1[:], a["w1"]).then_inc(W["w12_loaded"], 16)
            sp.dma_start(w2[:], a["w2"]).then_inc(W["w12_loaded"], 16)
            for c in range(NC):
                sp.wait_ge(S["out_rows"], c + 1)
                sp.dma_start(out_dram[:, 4 * c:4 * c + 4, :], x_rows[:, 4 * c:4 * c + 4, :]).then_inc(S["stored"], 16)
            sp.wait_ge(S["stored"], 16 * NC)

        @block.gpsimd
        def _(pool):
            pool.memset(identf[:], 0.0).then_inc(S["consts"], 1)
            pool.memset(mean_w[:], 1.0 / D).then_inc(S["consts"], 1)
            pool.memset(maskb[:], 0.0).then_inc(S["consts"], 1)
            pool.memset(identb[:], 0.0).then_inc(S["consts"], 1)
            pool.wait_ge(S["consts"], 4)
            for m in (identf, identb):
                pool.affine_select(out=m[:], in_=m[:], compare_op=ALU.not_equal, fill=1.0, base=0,
                                   pattern=[[-1, P]], channel_multiplier=1).then_inc(S["consts"], 1)
            pool.affine_select(out=maskb[:], in_=maskb[:], compare_op=ALU.is_ge, fill=NEG, base=0,
                               pattern=[[-1, P]], channel_multiplier=1).then_inc(S["consts"], 1)
            pool.memset(epsc[:, 0:1], LN_EPS).then_inc(S["consts"], 1)
            pool.memset(epsc[:, 1:2], 1e-6).then_inc(S["consts"], 1)
            pool.wait_ge(S["consts"], 9)
            pool.memset(lat[96:97, :], 1.0).then_inc(S["consts"], 1)
            pool.wait_ge(S["consts"], 10)
            pool.memset(latO[:, :, C0:2 * C0], 1.0).then_inc(S["consts"], 1)
            pool.memset(part_max[:], -3e38).then_inc(S["consts"], 1)
            pool.memset(earlier[:], 1.0).then_inc(W["pchain"], 1)
            pool.memset(head_of[:], 1.0).then_inc(W["pchain"], 1)
            pool.memset(spread[:], 0.0).then_inc(W["pchain"], 1)
            pool.memset(wv_eo[:], 0.0).then_inc(W["pchain"], 1)
            pool.wait_ge(W["pchain"], 4)
            pool.affine_select(out=earlier[:], in_=earlier[:], compare_op=ALU.is_ge, fill=0.0, base=-1,
                               pattern=[[1, E0], [-1, E0]], channel_multiplier=0).then_inc(W["pchain"], 1)
            pool.affine_select(out=head_of[:], in_=head_of[:], compare_op=ALU.is_ge, fill=0.0, base=0,
                               pattern=[[-HD1, NH]], channel_multiplier=1).then_inc(W["pchain"], 1)
            pool.affine_select(out=spread[:], in_=spread[:], compare_op=ALU.not_equal, fill=1.0 / UP, base=0,
                               pattern=[[-1, E1], [0, P]], channel_multiplier=1).then_inc(W["pchain"], 1)
            pool.wait_ge(W["pchain"], 7)
            pool.affine_select(out=head_of[:], in_=head_of[:], compare_op=ALU.is_ge, fill=0.0, base=HD1 - 1,
                               pattern=[[HD1, NH]], channel_multiplier=-1).then_inc(W["pchain"], 1)
            pool.affine_select(out=spread[:], in_=spread[:], compare_op=ALU.not_equal, fill=1.0 / UP, base=-96,
                               pattern=[[-1, E1], [0, P]], channel_multiplier=1).then_inc(W["pchain"], 1)
            pool.wait_ge(W["small_loaded"], 16 * 12)
            wv = wqkv[:, 2 * D:3 * D].rearrange("p (n e k) -> p n e k", e=2, k=HD1)
            for e in range(2):
                pool.tensor_copy(wv_eo[:, e, :, e * HD1:(e + 1) * HD1], wv[:, :, e, :]).then_inc(W["pchain"], 1)

            def body(s, bm, be, bp):
                if bp is not None:
                    pool.tensor_copy(vo_now[:], vo[:, bass.ds(s - 2 - GR * bp, 1), :].rearrange("p o d -> p (o d)"))\
                        .then_inc(S["vo_now_ready"], 1)
                if be is None:
                    return

                def normalise(c):
                    pool.wait_ge(S["inv_ready"], 2 * (s - 1) + c + 1)
                    pool.wait_ge(S["y_copied"], 8 * (s - 1) + (6 if c == 0 else 8))
                    if not (isinstance(s, int) and s == 1):
                        pool.wait_ge(S["proj_done"], 2 * (s - 2) + c + 1)
                    pool.tensor_tensor(y_n[:, c, :], y_raw[:, c, :], inv_sum[:, c, :], ALU.mult)\
                        .then_inc(S["y_n_ready"], 1)

                for k in range(SUB):
                    t = k % NTL
                    if t in MASKED:
                        n = SUB * (s - 1) + k
                        second = TILES[t][1][1][2]
                        for x in range(2):
                            pool.wait_ge(S["exp_done"], 2 * n + x + 1)
                            pool.sem_inc(S["pool_passed"], 1)
                            tri = probs[:, k % 2, x, 0:2 * second].rearrange("p (u q) -> p u q", u=2)[:, :, 0:P]
                            pool.affine_select(out=tri, in_=tri, compare_op=ALU.is_ge, fill=0.0, base=0,
                                               pattern=[[0, 2], [1, P]], channel_multiplier=-1)\
                                .then_inc(S["masked"], 1)
                    if k == NTL + 3:
                        normalise(0)
                if bp is not None:
                    pool.wait_ge(S["proj_done"], 2 * (s - 1))
                normalise(1)
            steps(pool, body)

            pool.wait_ge(S["x_updated"], 2 * NG)
            pool.memset(wx[:, :, 0:R0], 1.0).then_inc(W["consts_b"], 1)
            pool.memset(cT16[0:96, :], 0.0).then_inc(W["consts_b"], 1)

            def window(j, first, second, third, par):
                if first:
                    need(pool, W["v_product"], j - 1)
                    pool.wait_ge(N["h"], norm_count(2, "h", h2_count))
                    pool.tensor_copy(hwin[:, par, :], hT[:, bass.ds(j * P, P)]).then_inc(W["hwin_ready"], 1)
                if second:
                    i, q = j - 1, 1 - par
                    pool.wait_ge(W["inv_ready"], i + 1)
                    need(pool, W["p_turned"], i - 1)
                    pool.tensor_tensor(pn[:, q, :].rearrange("p (h k) -> p h k", h=NH), pw[:, q],
                                       rs[:, q, :].unsqueeze(2).broadcast_to([P, NH, WIN]), ALU.mult)\
                        .then_inc(W["p_ready"], 1)
            windows(pool, window)

            for k in range(2):

                def unit(c, e):
                    u = E1 * c + e
                    pool.wait_ge(E["yw"], loop_count(k, "yw", u + 1))
                    need(pool, E["z"], loop_count(k, "z", u))
                    pool.sem_inc(S["pool_passed"], 1)
                    zc = z[:, bass.ds(c * CH, CH)]
                    pool.tensor_tensor(zc, zc, yw[:, e % 2, :], ALU.add).then_inc(E["z"], 1)
                experts(pool, lambda c, e: None, unit)

        @block.tensor
        def _(pe):
            mm = pe.matmul

            pe.wait_ge(S["consts"], 12)
            for c in range(NC):
                pe.wait_ge(x_loaded[c], 16)
                for i in range(4):
                    m = pe.transpose(quad[c][:, i * P:(i + 1) * P], x_rows[:, 4 * c + i, :], identf[:])
                m.then_inc(S["x_turned"], 1)
            pe.wait_ge(S["c_loaded"], 64)
            pe.wait_ge(S["silu_ready"], 1)
            for l in range(2):
                for j in range(6):
                    m = mm(bankM[:, (6 * l + j) * B:(6 * l + j + 1) * B], wmod[:, l, j * D:(j + 1) * D],
                           csil[:, 2, l * B:l * B + B], start=True, stop=True)
            m.then_inc(S["mod_product"], 1)
            pe.wait_ge(S["w_attn_loaded"], 16 * 7)
            for h in range(H0):
                m = mm(bank[0][:, h * C0:(h + 1) * C0], wqT[:, h, :], wkT[:, h, :], start=True, stop=True)
            m.then_inc(S["qk_product"], 1)
            for g in range(H0 // GR):
                for j in range(GR):
                    h = GR * g + j
                    m = mm(bank[1][C0 * j:C0 * j + C0, g * D:(g + 1) * D], wvT[:, h, :], wo[:, h, :],
                           start=True, stop=True)
            m.then_inc(S["vo_product"], 1)

            def norm(k, x_ready, centre):

                def mean(c):
                    x_ready(pe, c)
                    if c >= 2:
                        pe.wait_ge(N["centred"], norm_count(k, "centred", c - 1))
                    mm(quad[c % 2], mean_w[:], xT[:, c * CH:(c + 1) * CH], start=True, stop=True)\
                        .then_inc(N["mean"], 1)

                def var(c):
                    pe.wait_ge(N["squared"], norm_count(k, "squared", c + 1))
                    if c >= 2:
                        pe.wait_ge(N["ln"], norm_count(k, "ln", c - 1))
                    mm(quad[2 + c % 2], mean_w[:], sq[:, c * CH:(c + 1) * CH], start=True, stop=True)\
                        .then_inc(N["var"], 1)
                for i in range(NC + 1):
                    if i < NC and centre:
                        mean(i)
                    if i >= 1:
                        var(i - 1)

            pe.wait_ge(S["xT_ready"], NC)
            norm(0, lambda e, c: None, True)
            pe.wait_ge(S["qk_ready"], 1)
            pe.wait_ge(S["vo_ready"], 1)
            for c in range(NC):
                pe.wait_ge(N["h"], norm_count(0, "h", c + 1))
                if c >= 2:
                    pe.wait_ge(S["lat_ready"], c - 1)
                mm(bank[c % 2][0:96, :], wkv[:].rearrange("p r c -> p (r c)"), hT[:, c * CH:(c + 1) * CH],
                   start=True, stop=True).then_inc(S["lat_product"], 1)
            for i in range(NT):
                m = mm(bankY[:, i * C0:(i + 1) * C0], hT[:, i * P:(i + 1) * P], wkv[:, 0, :], start=True, stop=True)
            m.then_inc(S["latO_product"], 1)
            for n in range(2 * NG):
                g, c = n // 2, n % 2
                b = g // GR
                if n >= 4:
                    pe.wait_ge(S["q_lo_ready"], n - 3)
                else:
                    pe.wait_ge(N["rstd"], norm_count(0, "rstd", NC))
                mm(quad[n % 4], qk[:, (g % GR) * P:(g % GR + 1) * P],
                   hT[:, b * L + c * CH:b * L + (c + 1) * CH], start=True, stop=True).then_inc(S["q_product"], 1)

            def body(s, bm, be, bp):
                first = isinstance(s, int) and s == 0

                def fill(f):
                    j, i, half = FILLS[f]
                    n = NF * s + f
                    if first and f < 2:
                        if f == 0:
                            pe.wait_ge(S["lat_ready"], NC)
                    else:
                        pe.wait_ge(S["max_taken"], n - 1)
                    width = min(CH, (i + 1) * P - half * CH)
                    diag = (i // 4 == half)
                    o = bank[f % 2]
                    m = mm(o[:, 0:width], q_st[0:96, bass.ds(GR * s + j, 1), i * P:(i + 1) * P]
                           .rearrange("p o t -> p (o t)"),
                           lat[0:96, bm * L + half * CH:bm * L + half * CH + width], start=True, stop=not diag)
                    if diag:
                        m = mm(o[:, width - P:width], identb[:], maskb[:], start=False, stop=True)
                    m.then_inc(S["scores_ready"], 1)

                def turn_max():
                    pe.wait_ge(S["row_max_ready"], s + 1)
                    if bp is not None:
                        pe.wait_ge(S["x_updated"], 2 * (s - 1))
                    pe.transpose(bankM[0:GR * QB, 0:P], row_max[:], identf[:]).then_inc(S["max_turned"], 1)

                def scores_t(k):
                    n = SUB * (s - 1) + k
                    c, segs = TILES[k % NTL]
                    for x in range(2):
                        if not (isinstance(s, int) and s == 1 and k == 0):
                            pe.wait_ge(S["exp_done"], 2 * n - 1 + x)
                        h = GR * (s - 1) + 2 * (k // NTL) + x
                        for kb, q0, at in segs:
                            m = mm(stT[:, x, at:at + CH - q0], lat[0:97, be * L + kb * P:be * L + (kb + 1) * P],
                                   q_st[0:97, bass.ds(h, 1), c * CH + q0:(c + 1) * CH].rearrange("p o t -> p (o t)"),
                                   start=True, stop=True)
                        m.then_inc(S["st_ready"], 1)

                def values(k):
                    n = SUB * (s - 1) + k
                    c, segs = TILES[k % NTL]
                    t = k % NTL
                    if t in MASKED:
                        pe.wait_ge(S["masked"], 16 * (s - 1) + 8 * (k // NTL) + 2 * MASKED[t] + 2)
                    else:
                        pe.wait_ge(S["exp_done"], 2 * n + 2)
                    if segs[0][0] == 0 and not (isinstance(s, int) and s == 1 and k == 0):
                        v = 4 * (s - 1) + 2 * (k // NTL) + c
                        pe.wait_ge(S["y_copied"], 2 * v)
                        pe.wait_ge(S["ln_done"], 2 * v)
                    for kb, q0, at in segs:
                        for x in range(2):
                            m = mm(bankY[64 * x:64 * x + 64, q0:CH], latO[:, be * QB + kb, :],
                                   probs[:, k % 2, x, at:at + CH - q0],
                                   start=(kb == 0), stop=(kb == 4 * c + 3))
                    m.then_inc(S["pv_done"], 1)

                def project(c):
                    pe.wait_ge(S["y_n_ready"], 2 * (s - 2) + c + 1)
                    if c == 0:
                        pe.wait_ge(S["vo_now_ready"], s - 1)
                        if be is not None:
                            pe.wait_ge(S["neg_max_ready"], s if bm is not None else NG)
                    else:
                        pe.wait_ge(S["x_updated"], 2 * (s - 2) + 1)
                    mm(bankM[:, :], vo_now[:], y_n[:, c, :], start=True, stop=True).then_inc(S["proj_done"], 1)

                if bm is not None:
                    g_now = s
                    if isinstance(s, int):
                        pe.wait_ge(q_placed[s % 2], 192 * (s // 2 + 1))
                    else:
                        pe.wait_ge(q_placed[0], 192 * 2 if bm == 0 else 192 * 4)
                        pe.wait_ge(q_placed[1], 192 * 2 if bm == 0 else 192 * 4)
                if be is not None:
                    pe.wait_ge(S["max_placed"], 16 * s)
                    if isinstance(s, int) and s == 1:
                        pe.wait_ge(S["q_lo_ready"], 2 * NG)
                        pe.wait_ge(S["latO_ready"], 1)
                for k in range(SUB):
                    if be is not None:
                        scores_t(k)
                    fl = fills_of(k) if bm is not None else []
                    for f in fl[:2]:
                        fill(f)
                    if be is not None and k >= 1:
                        values(k - 1)
                    for f in fl[2:]:
                        fill(f)
                    if bp is not None and k in (2, 4):
                        project(k // 2 - 1)
                if bm is not None:
                    turn_max()
                if be is not None:
                    values(SUB - 1)
            steps(pe, body)

            pe.wait_ge(S["x_updated"], 2 * NG)
            norm(1, lambda e, c: None, True)
            pe.wait_ge(W["small_loaded"], 16 * 12)
            for i in range(NT):
                if i % 4 == 0:
                    pe.wait_ge(N["h"], norm_count(1, "h", i // 4 + 1))
                m = mm(bank[0][:, i * E0:(i + 1) * E0], hT[:, i * P:(i + 1) * P], rw[:], start=True, stop=True)
            m.then_inc(W["logits"], 1)
            lowb, outb = (bank[1], bankY), (bankM, bank[0])

            def low(c):
                if c >= 2:
                    pe.wait_ge(W["low_ready"], c - 1)
                mm(lowb[c % 2][0:NR, :], downT[:], hT[:, c * CH:(c + 1) * CH], start=True, stop=True)\
                    .then_inc(W["low_product"], 1)
            low(0)
            low(1)
            pe.wait_ge(W["weights_ready"], 1)
            for c in range(NC):
                for i in range(4):
                    m = pe.transpose(quad[c][0:NR, i * P:(i + 1) * P], wx[:, 4 * c + i, :], identf[:])
                m.then_inc(W["wx_turned"], 1)
            for c in range(NC):
                if c >= 2:
                    pe.wait_ge(W["ffn_ready"], c - 1)
                mm(outb[c % 2][:], bwT[:], hT[:, c * CH:(c + 1) * CH], start=True, stop=False)
                pe.wait_ge(W["low_ready"], c + 1)
                mm(outb[c % 2][:], up[:], lowr[:, c % 2, :], start=False, stop=True).then_inc(W["ffn_product"], 1)
                if c + 2 < NC:
                    low(c + 2)

            norm(2, lambda e, c: e.wait_ge(W["x_ffn"], c + 1), True)
            pe.wait_ge(W["pchain"], 11)

            def window(j, first, second, third, par):
                if first:
                    pe.wait_ge(W["hwin_ready"], j + 1)
                    need(pe, W["q_ready"], j)
                    mm(bank[0][:, 0:P], wqkv[:, 0:D], hwin[:, par, :], start=True, stop=True)\
                        .then_inc(W["q_product"], 1)
                    need(pe, W["k_biased"], j)
                    mm(bankM[:, 0:P], wqkv[:, D:2 * D], hwin[:, par, :], start=True, stop=True)\
                        .then_inc(W["k_product"], 1)
                    need(pe, W["v_ready"], j)
                    for w in range(2):
                        for e in range(2):
                            m = mm(bank[1][WIN * e:WIN * e + WIN, w * P:(w + 1) * P],
                                   hwin[:, par, WIN * w:WIN * w + WIN],
                                   wv_eo[:, e].rearrange("p n c -> p (n c)"), start=True, stop=True)
                    m.then_inc(W["v_product"], 1)
                if third:
                    n = j - 2
                    pe.wait_ge(W["p_ready"], n + 1)
                    need(pe, W["pT_ready"], n)
                    for r in range(NH // 2):
                        m = pe.transpose(quad[2][:, r * P:(r + 1) * P], pn[:, par, r * P:(r + 1) * P], identf[:])
                    m.then_inc(W["p_turned"], 1)
                if second:
                    i, q = j - 1, 1 - par
                    pe.wait_ge(W["q_ready"], i + 1)
                    pe.wait_ge(W["k_ready"], i + 1)
                    need(pe, W["sub_ready"], i - 1)
                    for w in range(2):
                        m = mm(quad[q][WIN * w:WIN * w + WIN, :], qw[:, q, WIN * w:WIN * w + WIN],
                               kx[:, q, w].rearrange("p h k -> p (h k)"), start=True, stop=True)
                    m.then_inc(W["s_product"], 1)
                if third:
                    pe.wait_ge(W["v_ready"], n + 1)
                    pe.wait_ge(W["pT_ready"], n + 1)
                    need(pe, W["o_ready"], n)
                    for w in range(2):
                        for r in range(NH // 2):
                            m = mm(quad[3][32 * r:32 * r + 32, w * WIN:(w + 1) * WIN],
                                   vw[:, par, w, 32 * r:32 * r + 32],
                                   pT[:, r * P + w * WIN:r * P + (w + 1) * WIN], start=True, stop=True)
                    m.then_inc(W["o_product"], 1)
            windows(pe, window)
            for c in range(NC):
                pe.wait_ge(W["o_ready"], 4 * (c + 1))
                if c >= 2:
                    pe.wait_ge(W["att_ready"], c - 1)
                mm(outb[c % 2][:], owT[:], oT[:, c * CH:(c + 1) * CH], start=True, stop=True)\
                    .then_inc(W["att_product"], 1)

            norm(3, lambda e, c: e.wait_ge(W["x_att"], 6), True)
            for k in range(2):
                norm(4 + k, lambda e, c: None, False)
                for i in range(NT):
                    if i % 4 == 0:
                        pe.wait_ge(E["xn"], loop_count(k, "xn", i // 4 + 1))
                    m = mm(bank[0][:, i * 12:(i + 1) * 12], xc[:, i * P:(i + 1) * P], wrT[:], start=True, stop=True)
                m.then_inc(E["logits"], 1)
                pe.wait_ge(E["weights_ready"], loop_count(k, "weights_ready", 1))
                for c in range(NC):
                    for i in range(4):
                        m = pe.transpose(quad[c][0:E1, i * P:(i + 1) * P], wts[:, 4 * c + i, :], identf[:])
                    m.then_inc(E["cw_turned"], 1)
                pe.wait_ge(E["xn_lo"], loop_count(k, "xn_lo", NC))
                pe.wait_ge(W["w_lo"], 2)
                pe.wait_ge(E["c_lo"], loop_count(k, "c_lo", NC))

                def ahead(c, e):
                    u = E1 * c + e
                    need(pe, E["act"], loop_count(k, "act", u - 1))
                    for f in range(2):
                        at = e * F1 + f * P
                        for t, (wp, xp) in enumerate(((0, 0), (0, 1), (1, 0))):
                            m = mm(stT[:, e % 2, f * CH:(f + 1) * CH], w1h[:, wp, at:at + P],
                                   xnh[:, xp, bass.ds(c * CH, CH)], start=(t == 0), stop=(t == 2))
                    m.then_inc(E["pre"], 1)

                def unit(c, e):
                    u = E1 * c + e
                    need(pe, E["cw"], loop_count(k, "cw", u - 1))
                    mm((bankY, bankM)[e % 2][:], spread[:, e, :], cT16[:, bass.ds(c * CH, CH)],
                       start=True, stop=True).then_inc(E["cb"], 1)
                    pe.wait_ge(E["hid_lo"], loop_count(k, "hid_lo", u + 1))
                    need(pe, E["yw"], loop_count(k, "yw", u - 1))
                    for n, (f, wp, hp) in enumerate([(f, *q) for f in range(2) for q in ((0, 0), (0, 1), (1, 0))]):
                        at = (2 * e + f) * P
                        m = mm(bank[e % 2][:], w2h[:, wp, at:at + P], hidh[:, e % 2, hp, f * CH:(f + 1) * CH],
                               start=(n == 0), stop=(n == 5))
                    m.then_inc(E["y"], 1)
                experts(pe, ahead, unit)
            for c in range(NC):
                pe.wait_ge(x_final, c + 1)
                for i in range(4):
                    m = pe.transpose(quad[c][:, i * P:(i + 1) * P], xT[:, (4 * c + i) * P:(4 * c + i + 1) * P],
                                     identf[:])
                m.then_inc(S["out_turned"], 1)

        @block.scalar
        def _(act):
            A = nc.scalar.activation
            act.preload_act_table_set("natural_log_exp_and_others")
            act.wait_ge(S["c_loaded"], 64)
            A(csil[:, 0, :], cT[:].rearrange("p l b -> p (l b)"), ACT.Exp, scale=-1.0).then_inc(S["csil_step"], 1)
            for c in range(NC):
                act.wait_ge(S["x_turned"], c + 1)
                A(xT[:, c * CH:(c + 1) * CH], quad[c], ACT.Copy).then_inc(S["xT_ready"], 1)
            act.wait_ge(S["qk_product"], 1)
            A(qk[:], bank[0][:], ACT.Copy, scale=HD0 ** -0.5).then_inc(S["qk_ready"], 1)

            def norm(k, eps, centre):
                src = xc if centre else z
                for i in range(NC + 1):
                    if i < NC:
                        cs = slice(i * CH, (i + 1) * CH)
                        if centre:
                            act.wait_ge(N["centred"], norm_count(k, "centred", i + 1))
                        elif k == 4:
                            act.wait_ge(N["h"], norm_count(3, "h", i + 1))
                        else:
                            act.wait_ge(E["z"], loop_count(0, "z", E1 * (i + 1)))
                        A(sq[:, cs], src[:, cs], ACT.Square).then_inc(N["squared"], 1)
                    if i >= 1:
                        cs = slice((i - 1) * CH, i * CH)
                        act.wait_ge(N["var"], norm_count(k, "var", i))
                        A(rstd[:, cs], quad[2 + (i - 1) % 2], ACT.Ln, bias=epsc[:, eps:eps + 1]).then_inc(N["ln"], 1)
                        act.wait_ge(N["ln"], norm_count(k, "ln", i))
                        A(rstd[:, cs], rstd[:, cs], ACT.Exp, scale=-0.5).then_inc(N["rstd"], 1)

            norm(0, 0, True)
            for c in range(NC):
                act.wait_ge(S["lat_product"], c + 1)
                A(lat[0:96, c * CH:(c + 1) * CH], bank[c % 2][0:96, :], ACT.Copy).then_inc(S["lat_hi"], 1)
            for n in range(2 * NG):
                g, c = n // 2, n % 2
                act.wait_ge(S["q_product"], n + 1)
                if g >= 2 and c == 0:
                    act.wait_ge(q_placed[g % 2], 192 * (g // 2))
                A(q_hi[:, g % 2, c * CH:(c + 1) * CH], quad[n % 4], ACT.Copy).then_inc(S["q_hi_ready"], 1)

            def body(s, bm, be, bp):
                def exps(k):
                    n = SUB * (s - 1) + k
                    c, segs = TILES[k % NTL]
                    width = segs[1][2] + CH - segs[1][1]
                    for x in range(2):
                        act.wait_ge(S["st_ready"], 2 * n + x + 1)
                        if x == 0 and not (isinstance(s, int) and s == 1 and k < 2):
                            act.wait_ge(S["pv_done"], n - 1)
                        A(probs[:, k % 2, x, 0:width], stT[:, x, 0:width], ACT.Exp).then_inc(S["exp_done"], 1)

                def logs(pair, c):
                    act.wait_ge(S["pv_done"], SUB * (s - 1) + NTL * pair + (2 if c == 0 else NTL))
                    for x in range(2):
                        j = 2 * pair + x
                        A(ln_sum[C0 * j:C0 * j + C0, c, :], bankY[64 * x + C0:64 * x + 2 * C0, :], ACT.Ln)\
                            .then_inc(S["ln_done"], 1)
                    if pair == 1:
                        act.wait_ge(S["ln_done"], 8 * (s - 1) + (6 if c == 0 else 8))
                        if not (isinstance(s, int) and s == 1):
                            act.wait_ge(S["y_n_ready"], 2 * (s - 2) + c + 1)
                        A(inv_sum[:, c, :], ln_sum[:, c, :], ACT.Exp, scale=-1.0).then_inc(S["inv_ready"], 1)

                for k in range(SUB):
                    if be is not None:
                        exps(k)
                        if k == 2:
                            logs(0, 0)
                        if k == NTL:
                            logs(0, 1)
                        if k == NTL + 2:
                            logs(1, 0)
                if bm is not None:
                    act.wait_ge(S["max_turned"], s + 1)
                    if not (isinstance(s, int) and s == 0):
                        act.wait_ge(S["max_placed"], 16 * s)
                    A(neg_max[:], bankM[0:GR * QB, 0:P], ACT.Copy, scale=-1.0).then_inc(S["neg_max_ready"], 1)
                if be is not None:
                    logs(1, 1)
            steps(act, body)

            norm(1, 0, True)
            act.wait_ge(W["exp_in"], 1)
            A(pr[:, :, 0:E0], lg[:, :, 0:E0], ACT.Exp).then_inc(W["exp_out"], 1)
            for c in range(NC):
                act.wait_ge(W["wx_turned"], c + 1)
                A(wxT[:, c * CH:(c + 1) * CH], quad[c][0:NR, :], ACT.Copy).then_inc(W["wxT_ready"], 1)
            outb = (bankM, bank[0])
            for c in range(NC):
                act.wait_ge(W["ffn_product"], c + 1)
                if c >= 2:
                    act.wait_ge(W["x_ffn"], c - 1)
                A(ffn[:, c % 2, :], outb[c % 2][:], ACT.Identity, bias=bb[:]).then_inc(W["ffn_ready"], 1)

            norm(2, 0, True)
            act.wait_ge(W["prep"], 1)

            def window(j, first, second, third, par):
                if first:
                    act.wait_ge(W["q_product"], j + 1)
                    need(act, W["s_product"], j - 1)
                    A(qw[:, par, :], bank[0][:, 0:P], ACT.Identity, bias=bq_s[:], scale=HD1 ** -0.5)\
                        .then_inc(W["q_ready"], 1)
                    act.wait_ge(W["k_product"], j + 1)
                    need(act, W["k_ready"], j - 1)
                    A(kw[:, par, :], bankM[:, 0:P], ACT.Identity, bias=bqkv[:, 1:2]).then_inc(W["k_biased"], 1)
                if third:
                    n = j - 2
                    act.wait_ge(W["p_turned"], n + 1)
                    need(act, W["o_product"], n)
                    A(pT[:], quad[2][:], ACT.Copy).then_inc(W["pT_ready"], 1)
                if second:
                    i, q = j - 1, 1 - par
                    act.wait_ge(W["sub_ready"], i + 1)
                    need(act, W["p_ready"], i - 1)
                    A(pw[:, q], sub[:, q], ACT.Exp).then_inc(W["exp_ready"], 1)
                if third:
                    act.wait_ge(W["o_product"], n + 1)
                    A(oT[:, bass.ds(n * P, P)], quad[3][:, 0:P], ACT.Identity, bias=bqkv[:, 2:3])\
                        .then_inc(W["o_ready"], 1)
                if first:
                    act.wait_ge(W["v_product"], j + 1)
                    need(act, W["o_product"], j - 1)
                    A(vw[:, par].rearrange("p w c -> p (w c)"), bank[1][:, 0:2 * P], ACT.Copy)\
                        .then_inc(W["v_ready"], 1)
            windows(act, window)
            for c in range(NC):
                act.wait_ge(W["att_product"], c + 1)
                if c >= 2:
                    act.wait_ge(W["x_att"], (0, 1, 3, 4)[c - 1])
                A(ffn[:, c % 2, :], outb[c % 2][:], ACT.Identity, bias=ob[:]).then_inc(W["att_ready"], 1)

            norm(3, 0, True)
            act.wait_ge(W["w12_loaded"], 32)
            for dst, src in ((w1h, w1), (w2h, w2)):
                A(dst[:, 0, :], src[:], ACT.Copy, scale=UP).then_inc(W["w_hi"], 1)
            for k in range(2):
                act.preload_act_table_set("natural_log_exp_and_others")
                norm(4 + k, 1, False)
                for c in range(NC):
                    act.wait_ge(E["xn"], loop_count(k, "xn", c + 1))
                    if k:
                        act.wait_ge(E["pre"], loop_count(k - 1, "pre", NC * E1))
                    A(xnh[:, 0, c * CH:(c + 1) * CH], xc[:, c * CH:(c + 1) * CH], ACT.Copy).then_inc(E["xn_hi"], 1)
                act.wait_ge(E["exp_in"], loop_count(k, "exp_in", 1))
                A(pr[:], lg[:], ACT.Exp).then_inc(E["exp_out"], 1)
                act.wait_ge(W["consts_b"], 2)
                for c in range(NC):
                    act.wait_ge(E["cw_turned"], loop_count(k, "cw_turned", c + 1))
                    A(cT16[0:E1, c * CH:(c + 1) * CH], quad[c][0:E1, :], ACT.Copy).then_inc(E["c_hi"], 1)

                def ahead(c, e):
                    u = E1 * c + e
                    act.wait_ge(E["pre"], loop_count(k, "pre", u + 1))
                    need(act, E["hid_lo"], loop_count(k, "hid_lo", u - 1))
                    A(hid[:, e % 2, :], stT[:, e % 2, :], ACT.Silu, scale=1.0 / UP).then_inc(E["act"], 1)

                def unit(c, e):
                    u = E1 * c + e
                    act.wait_ge(E["cb"], loop_count(k, "cb", u + 1))
                    need(act, E["yw"], loop_count(k, "yw", u - 1))
                    A(cw[:, e % 2, :], (bankY, bankM)[e % 2][:], ACT.Copy).then_inc(E["cw"], 1)
                experts(act, ahead, unit)

        def add_ffn(dve, V, c):
            dve.wait_ge(W["ffn_ready"], c + 1)
            cs = slice(c * CH, (c + 1) * CH)
            V.scalar_tensor_tensor(out=xT[:, cs], in0=ffn[:, c % 2, :], scalar=mod[:, 0, 5, c // 2:c // 2 + 1],
                                   in1=xT[:, cs], op0=ALU.mult, op1=ALU.add).then_inc(W["x_ffn"], 1)

        def shifted_pieces_back(c):
            b = c // 2
            if c % 2 == 0:
                return [(b * L + SHIFT, 0, CH)]
            return [(b * L + CH + SHIFT, 0, CH - SHIFT), (b * L, CH - SHIFT, SHIFT)]

        @block.vector
        def _(dve):
            chain = [0]
            dch = S["gate_step"]

            def link(ins):
                chain[0] += 1
                ins.then_inc(dch, 1)
                dve.wait_ge(dch, chain[0])

            V = nc.vector
            dve.wait_ge(S["csil_step"], 1)
            link(V.tensor_scalar(csil[:, 1, :], csil[:, 0, :], 1.0, None, ALU.add))
            link(V.reciprocal(csil[:, 1, :], csil[:, 1, :]))
            V.tensor_tensor(csil[:, 2, :], cT[:].rearrange("p l b -> p (l b)"), csil[:, 1, :], ALU.mult)\
                .then_inc(S["silu_ready"], 1)
            dve.wait_ge(S["mod_product"], 1)
            link(V.tensor_copy(mod[:].rearrange("p l j b -> p (l j b)"), bankM[:, 0:12 * B]))
            for j in (1, 4):
                link(V.tensor_scalar(mod[:, :, j, :], mod[:, :, j, :], 1.0, None, ALU.add))
            for n, j in enumerate((2, 5)):
                gate = mod[:, :, j, :]
                link(V.tensor_scalar(sgn[:, n], gate, 0.0, 2.0, ALU.is_ge, ALU.mult))
                link(V.tensor_scalar(sgn[:, n], sgn[:, n], -1.0, None, ALU.add))
                link(V.tensor_tensor(gate, gate, sgn[:, n], ALU.mult))
                link(V.tensor_scalar(gate, gate, 0.25, None, ALU.max))
                link(V.tensor_tensor(gate, gate, sgn[:, n], ALU.mult))
            dve.wait_ge(S["vo_product"], 1)
            V.tensor_copy(vo[:].rearrange("p g d -> p (g d)"), bank[1][:]).then_inc(S["vo_ready"], 1)

            def norm(k, l, sh, sc, shifted=False):
                for c in range(NC):
                    cs = slice(c * CH, (c + 1) * CH)
                    dve.wait_ge(N["mean"], norm_count(k, "mean", c + 1))
                    V.tensor_tensor(xc[:, cs], xT[:, cs], quad[c % 2], ALU.subtract).then_inc(N["centred"], 1)
                for c in range(NC):
                    cs = slice(c * CH, (c + 1) * CH)
                    b = c // 2
                    dve.wait_ge(N["rstd"], norm_count(k, "rstd", c + 1))
                    V.scalar_tensor_tensor(out=xc[:, cs], in0=xc[:, cs], scalar=mod[:, l, sc, b:b + 1],
                                           in1=rstd[:, cs], op0=ALU.mult, op1=ALU.mult).then_inc(N["scaled"], 1)
                    dve.wait_ge(N["scaled"], norm_count(k, "scaled", c + 1))
                    for to, at, m in shifted_pieces(c) if shifted else [(c * CH, c * CH, CH)]:
                        V.tensor_scalar(hT[:, to:to + m], xc[:, at:at + m], mod[:, l, sh, b:b + 1], None, ALU.add)\
                            .then_inc(N["h"], 1)

            dve.wait_ge(S["xT_ready"], NC)
            norm(0, 0, 0, 1)
            for c in range(NC):
                cs = slice(c * CH, (c + 1) * CH)
                dve.wait_ge(S["lat_hi"], c + 1)
                V.tensor_tensor(lat[64:96, cs], bank[c % 2][64:96, :], lat[64:96, cs], ALU.subtract)\
                    .then_inc(S["lat_ready"], 1)
            dve.wait_ge(S["latO_product"], 1)
            V.tensor_copy(latO[:, :, 0:C0], bankY[:].rearrange("p (n c) -> p n c", c=C0)).then_inc(S["latO_ready"], 1)
            for n in range(2 * NG):
                g, c = n // 2, n % 2
                dve.wait_ge(S["q_hi_ready"], n + 1)
                if g >= 2 and c == 0:
                    dve.wait_ge(q_placed[g % 2], 192 * (g // 2))
                V.tensor_tensor(q_lo[:, g % 2, c * CH:(c + 1) * CH], quad[n % 4],
                                q_hi[:, g % 2, c * CH:(c + 1) * CH], ALU.subtract).then_inc(S["q_lo_ready"], 1)

            dve.wait_ge(S["consts"], 12)

            def body(s, bm, be, bp):
                def take(f):
                    j, i, half = FILLS[f]
                    width = min(CH, (i + 1) * P - half * CH)
                    dve.wait_ge(S["scores_ready"], NF * s + f + 1)
                    V.tensor_reduce(part_max[:, half, j, i:i + 1], bank[f % 2][:, 0:width], AX.X, ALU.max)\
                        .then_inc(S["max_taken"], 1)

                def copy_y(pair, c):
                    dve.wait_ge(S["pv_done"], SUB * (s - 1) + NTL * pair + (2 if c == 0 else NTL))
                    if pair == 0 and not (isinstance(s, int) and s == 1):
                        dve.wait_ge(S["y_n_ready"], 2 * (s - 2) + c + 1)
                    for x in range(2):
                        j = 2 * pair + x
                        V.tensor_copy(y_raw[C0 * j:C0 * j + C0, c, :], bankY[64 * x:64 * x + C0, :])\
                            .then_inc(S["y_copied"], 1)

                def update(c):
                    dve.wait_ge(S["proj_done"], 2 * (s - 2) + c + 1)
                    cs = slice(bp * L + c * CH, bp * L + (c + 1) * CH)
                    V.scalar_tensor_tensor(out=xT[:, cs], in0=bankM[:, :], scalar=mod[:, 0, 2, bp:bp + 1],
                                           in1=xT[:, cs], op0=ALU.mult, op1=ALU.add).then_inc(S["x_updated"], 1)

                for k in range(SUB):
                    if bm is not None:
                        for f in fills_of(k):
                            take(f)
                    if be is not None:
                        if k == 2:
                            copy_y(0, 0)
                        if k == NTL:
                            copy_y(0, 1)
                        if k == NTL + 2:
                            copy_y(1, 0)
                    if bp is not None and k in (2, 4):
                        update(k // 2 - 1)
                if bp is not None:
                    dve.wait_ge(S["x_updated"], 2 * (s - 1))
                if bm is not None:
                    dve.wait_ge(S["max_taken"], NF * (s + 1))
                    if not (isinstance(s, int) and s == 0):
                        dve.wait_ge(S["max_turned"], s)
                    V.tensor_tensor(row_max[:].rearrange("p (j i) -> p j i", j=GR), part_max[:, 0], part_max[:, 1],
                                    ALU.max).then_inc(S["row_max_ready"], 1)
                if be is not None:
                    copy_y(1, 1)
            steps(dve, body)

            chain2 = [0]

            def then(ins):
                chain2[0] += 1
                ins.then_inc(W["dchain"], 1)
                dve.wait_ge(W["dchain"], chain2[0])

            def softmax_in(x, k):
                g, n = x.shape[2], x.shape[3]
                m = st[:, k, :, 0:g]
                then(V.tensor_reduce(m, x, AX.X, ALU.max))
                then(V.tensor_tensor(x, x, m.unsqueeze(3).broadcast_to([P, NT, g, n]), ALU.subtract))

            def softmax_out(x, k):
                g, n = x.shape[2], x.shape[3]
                m = st[:, k, :, 0:g]
                then(V.tensor_reduce(m, x, AX.X, ALU.add))
                then(V.reciprocal(m, m))
                then(V.tensor_tensor(x, x, m.unsqueeze(3).broadcast_to([P, NT, g, n]), ALU.mult))

            def top_two(x, w, tiny):
                n = x.shape[2]
                g = gt[:, :, 0:n * n].rearrange("p t (e f) -> p t e f", e=n)
                q = eq[:, :, 0:n * n].rearrange("p t (e f) -> p t e f", e=n)
                other = x.unsqueeze(2).broadcast_to([P, NT, n, n])
                own = x.unsqueeze(3).broadcast_to([P, NT, n, n])
                then(V.tensor_tensor(g, other, own, ALU.is_gt))
                then(V.tensor_tensor(q, other, own, ALU.is_equal))
                then(V.tensor_tensor(q, q, earlier[:, 0:n, 0:n].unsqueeze(1).broadcast_to([P, NT, n, n]), ALU.mult))
                then(V.tensor_tensor(g, g, q, ALU.add))
                r = rank[:, :, 0:n]
                then(V.tensor_reduce(r, g, AX.X, ALU.add))
                then(V.tensor_scalar(r, r, 1.5, None, ALU.is_lt))
                then(V.tensor_tensor(w, x, r, ALU.mult))
                s1 = st[:, 4, :, 0:1]
                then(V.tensor_reduce(s1, w.unsqueeze(2), AX.X, ALU.add))
                then(V.tensor_scalar(s1, s1, tiny, None, ALU.add))
                then(V.reciprocal(s1, s1))
                then(V.tensor_tensor(w, w, s1.broadcast_to([P, NT, n]), ALU.mult))

            norm(1, 0, 3, 4)
            dve.wait_ge(W["logits"], 1)
            l0 = lg[:, :, 0:E0]
            then(V.tensor_tensor(l0, bank[0][:, 0:NT * E0].rearrange("p (t e) -> p t e", e=E0),
                                 rb[:].unsqueeze(1).broadcast_to([P, NT, E0]), ALU.add))
            softmax_in(l0.unsqueeze(2), 0)
            V.tensor_copy(st[:, 5, :, 0:1], st[:, 0, :, 0:1]).then_inc(W["exp_in"], 1)
            dve.wait_ge(W["exp_out"], 1)
            dve.wait_ge(W["pchain"], 11)
            softmax_out(pr[:, :, 0:E0].unsqueeze(2), 1)
            top_two(pr[:, :, 0:E0], wts[:, :, 0:E0], 1e-6)
            dve.wait_ge(W["consts_b"], 1)
            V.tensor_copy(wx[:, :, R0:NR].rearrange("p t (e r) -> p t e r", r=R0),
                          wts[:, :, 0:E0].unsqueeze(3).broadcast_to([P, NT, E0, R0])).then_inc(W["weights_ready"], 1)
            lowb = (bank[1], bankY)
            for c in range(NC):
                dve.wait_ge(W["low_product"], c + 1)
                dve.wait_ge(W["wxT_ready"], c + 1)
                if c >= 2:
                    dve.wait_ge(W["ffn_product"], c - 1)
                V.tensor_tensor(lowr[:, c % 2, :], lowb[c % 2][0:NR, :], wxT[:, c * CH:(c + 1) * CH], ALU.mult)\
                    .then_inc(W["low_ready"], 1)
                if c >= 1:
                    add_ffn(dve, V, c - 1)
            add_ffn(dve, V, NC - 1)
            then(V.tensor_scalar(bq_s[:], bqkv[:, 0:1], HD1 ** -0.5, None, ALU.mult))
            V.tensor_scalar(ga2[:], mod[:, 1, 2, :], 2.0, None, ALU.mult).then_inc(W["prep"], 1)

            norm(2, 1, 0, 1, shifted=True)

            def window(j, first, second, third, par):
                if first:
                    dve.wait_ge(W["k_biased"], j + 1)
                    need(dve, W["s_product"], j - 1)
                    shape = [P, 2, NH, WIN]
                    V.tensor_tensor(
                        kx[:, par], kw[:, par, :].rearrange("p (w k) -> p w k", w=2).unsqueeze(2).broadcast_to(shape),
                        head_of[:].unsqueeze(1).unsqueeze(3).broadcast_to(shape), ALU.mult).then_inc(W["k_ready"], 1)
                if second:
                    i, q = j - 1, 1 - par
                    s4 = quad[q].rearrange("p (h k) -> p h k", h=NH)
                    dve.wait_ge(W["s_product"], i + 1)
                    V.tensor_reduce(mx[:, q, :], s4, AX.X, ALU.max).then_inc(W["max_ready"], 1)
                    dve.wait_ge(W["max_ready"], i + 1)
                    need(dve, W["exp_ready"], i - 1)
                    V.tensor_tensor(sub[:, q], s4, mx[:, q, :].unsqueeze(2).broadcast_to([P, NH, WIN]),
                                    ALU.subtract).then_inc(W["sub_ready"], 1)
                    dve.wait_ge(W["exp_ready"], i + 1)
                    V.tensor_reduce(sm[:, q, :], pw[:, q], AX.X, ALU.add).then_inc(W["sum_ready"], 1)
                    dve.wait_ge(W["sum_ready"], i + 1)
                    need(dve, W["p_ready"], i - 1)
                    V.reciprocal(rs[:, q, :], sm[:, q, :]).then_inc(W["inv_ready"], 1)
            windows(dve, window)
            for c in range(NC):
                dve.wait_ge(W["att_ready"], c + 1)
                b = c // 2
                for to, at, m in shifted_pieces_back(c):
                    V.scalar_tensor_tensor(out=xT[:, to:to + m], in0=ffn[:, c % 2, at:at + m],
                                           scalar=ga2[:, b:b + 1], in1=xT[:, to:to + m], op0=ALU.mult,
                                           op1=ALU.add).then_inc(W["x_att"], 1)

            norm(3, 1, 3, 4)
            for n, (dst, src) in enumerate(((w1h, w1), (w2h, w2))):
                dve.wait_ge(W["w_hi"], n + 1)
                V.scalar_tensor_tensor(out=dst[:, 1, :], in0=src[:], scalar=UP, in1=dst[:, 0, :],
                                       op0=ALU.mult, op1=ALU.subtract).then_inc(W["w_lo"], 1)
            for k in range(2):
                for c in range(NC):
                    cs = slice(c * CH, (c + 1) * CH)
                    dve.wait_ge(N["rstd"], norm_count(4 + k, "rstd", c + 1))
                    V.scalar_tensor_tensor(out=xc[:, cs], in0=z[:, cs], scalar=nw[:], in1=rstd[:, cs],
                                           op0=ALU.mult, op1=ALU.mult).then_inc(E["xn"], 1)
                for c in range(NC):
                    cs = slice(c * CH, (c + 1) * CH)
                    dve.wait_ge(E["xn_hi"], loop_count(k, "xn_hi", c + 1))
                    V.tensor_tensor(xnh[:, 1, cs], xc[:, cs], xnh[:, 0, cs], ALU.subtract).then_inc(E["xn_lo"], 1)
                dve.wait_ge(E["logits"], loop_count(k, "logits", 1))
                then(V.tensor_copy(lg[:], bank[0][:, 0:NT * 12].rearrange("p (t e) -> p t e", e=12)))
                softmax_in(lg[:, :, 0:NGR].unsqueeze(2), 0)
                softmax_in(lg[:, :, NGR:12].rearrange("p t (g e) -> p t g e", e=2), 1)
                V.tensor_copy(st[:, 5, :, 0:1], st[:, 0, :, 0:1]).then_inc(E["exp_in"], 1)
                dve.wait_ge(E["exp_out"], loop_count(k, "exp_out", 1))
                macro = pr[:, :, 0:NGR]
                micro = pr[:, :, NGR:12].rearrange("p t (g e) -> p t g e", e=2)
                softmax_out(macro.unsqueeze(2), 0)
                softmax_out(micro, 1)
                wg = rank[:, :, 0:NGR]
                top_two(macro, macro, 1e-9)
                best = st[:, 2]
                then(V.tensor_reduce(best, micro, AX.X, ALU.max))
                then(V.tensor_scalar(st[:, 3], best, 1e-9, None, ALU.add))
                then(V.reciprocal(st[:, 3], st[:, 3]))
                then(V.tensor_tensor(best, best, st[:, 3], ALU.mult))
                then(V.tensor_tensor(best, best, macro, ALU.mult))
                then(V.tensor_tensor(st[:, 3], micro[:, :, :, 0], micro[:, :, :, 1], ALU.is_ge))
                w4 = wts[:].rearrange("p t (g e) -> p t g e", e=2)
                then(V.tensor_tensor(w4[:, :, :, 0], best, st[:, 3], ALU.mult))
                V.tensor_tensor(w4[:, :, :, 1], best, w4[:, :, :, 0], ALU.subtract).then_inc(E["weights_ready"], 1)
                for c in range(NC):
                    cs = slice(c * CH, (c + 1) * CH)
                    dve.wait_ge(E["c_hi"], loop_count(k, "c_hi", c + 1))
                    if c == 0:
                        dve.wait_ge(W["consts_b"], 2)
                    V.tensor_tensor(cT16[96:104, cs], quad[c][0:E1, :], cT16[0:E1, cs], ALU.subtract)\
                        .then_inc(E["c_lo"], 1)

                def ahead(c, e):
                    u = E1 * c + e
                    dve.wait_ge(E["act"], loop_count(k, "act", u + 1))
                    need(dve, E["y"], loop_count(k, "y", u - 1))
                    V.tensor_copy(hidh[:, e % 2, 0, :], hid[:, e % 2, :]).then_inc(E["hid_hi"], 1)
                    dve.wait_ge(E["hid_hi"], loop_count(k, "hid_hi", u + 1))
                    V.tensor_tensor(hidh[:, e % 2, 1, :], hid[:, e % 2, :], hidh[:, e % 2, 0, :], ALU.subtract)\
                        .then_inc(E["hid_lo"], 1)

                def unit(c, e):
                    u = E1 * c + e
                    dve.wait_ge(E["y"], loop_count(k, "y", u + 1))
                    dve.wait_ge(E["cw"], loop_count(k, "cw", u + 1))
                    need(dve, E["z"], loop_count(k, "z", u - 1))
                    V.tensor_tensor(yw[:, e % 2, :], bank[e % 2][:], cw[:, e % 2, :], ALU.mult).then_inc(E["yw"], 1)
                experts(dve, ahead, unit)
            dve.wait_ge(E["z"], loop_count(1, "z", NC * E1))
            for c in range(NC):
                cs = slice(c * CH, (c + 1) * CH)
                V.scalar_tensor_tensor(out=xT[:, cs], in0=z[:, cs], scalar=mod[:, 1, 5, c // 2:c // 2 + 1],
                                       in1=xT[:, cs], op0=ALU.mult, op1=ALU.add).then_inc(x_final, 1)
            for c in range(NC):
                dve.wait_ge(S["out_turned"], c + 1)
                V.tensor_copy(x_rows[:, 4 * c:4 * c + 4, :].rearrange("p n d -> p (n d)"), quad[c])\
                    .then_inc(S["out_rows"], 1)


def kernel(**inputs):
    import concourse.bacc as _bacc
    from concourse.bass_utils import run_bass_kernel_spmd as _run

    v = {k: np.asarray(x) for k, x in inputs.items()}
    lay = {
        "x": v["L0_attn_x_bld"],
        "c0T": v["L0_c"].T, "c1T": v["L1_c"].T, "wmod0": v["L0_wmod"], "wmod1": v["L1_wmod"],
        "wqT": v["L0_attn_Wq"].transpose(2, 1, 0), "wkT": v["L0_attn_Wk_up"].transpose(2, 1, 0),
        "wvT": v["L0_attn_Wv_up"].transpose(2, 1, 0), "wo": v["L0_attn_Wout"].transpose(1, 0, 2),
        "wkv": v["L0_attn_Wkv_down"],
        "bwT": v["L0_ffn_base_W"].T, "bb": v["L0_ffn_base_b"][:, None],
        "downT": np.concatenate([v["L0_ffn_shared_A"][None], v["L0_ffn_routed_A"]]).reshape(-1, D).T,
        "up": np.concatenate([v["L0_ffn_shared_B"][None], v["L0_ffn_routed_B"]]).transpose(0, 2, 1).reshape(-1, D),
        "rw": v["L0_ffn_router_W"].T, "rb": v["L0_ffn_router_b"],
        "wqkv": v["L1_attn_in_proj_w"].T, "bqkv": v["L1_attn_in_proj_b"].reshape(3, D).T,
        "owT": v["L1_attn_out_w"].T, "ob": v["L1_attn_out_b"][:, None],
        "nw": v["L1_ffn_norm_w"][:, None],
        "wrT": np.concatenate([v["L1_ffn_w_macro"], v["L1_ffn_w_micro"].reshape(E1, D)]).T,
        "w1": v["L1_ffn_w1"].transpose(2, 0, 1).reshape(D, E1 * F1),
        "w2": v["L1_ffn_w2"].reshape(E1, D, F1 // P, P).transpose(3, 0, 2, 1).reshape(P, E1 * F1),
    }
    nc = _bacc.Bacc("TRN2", target_bir_lowering=False, num_devices=1)
    arrays, args = {}, {}
    for name, x in lay.items():
        x = np.ascontiguousarray(x)
        arrays[f"in_{name}"] = x
        args[name] = nc.dram_tensor(f"in_{name}", x.shape, mybir.dt.from_np(x.dtype), kind="ExternalInput").ap()
    out = nc.dram_tensor("out", (B, L, D), F32, kind="ExternalOutput").ap()
    program(nc, args, out)
    r = _run(nc, [arrays], core_ids=[0])
    return r.results[0]["out"]
```

```python
from contextlib import ExitStack

import numpy as np

import concourse.bass as bass
from concourse import mybir

F32 = mybir.dt.float32
F16 = mybir.dt.float16
BF16 = mybir.dt.bfloat16
ALU = mybir.AluOpType
ACT = mybir.ActivationFunctionType
AX = mybir.AxisListType

P = 128
B, L, D = 2, 1024, 128
T = B * L
NT = T // P
CH = 512
NC = T // CH
H0, C0, HD0 = 16, 32, 64
GR = 4
NG = B * H0 // GR
QB = L // P
NH, HD1, WIN, SHIFT = 8, 16, 64, 32
NGR, E1, F1 = 4, 8, 256
UP = 64.0
NEG = -1e30
LN_EPS = 1e-5

TILES = [
    (0, [(0, 0, 0), (1, 128, 512)]),
    (0, [(2, 256, 0), (3, 384, 256)]),
    (1, [(0, 0, 0), (1, 0, 512)]),
    (1, [(2, 0, 0), (3, 0, 512)]),
    (1, [(4, 0, 0), (5, 128, 512)]),
    (1, [(6, 256, 0), (7, 384, 256)]),
]
NTL = len(TILES)
MASKED = {0: 0, 1: 1, 4: 2, 5: 3}
SUB = 2 * NTL
CHUNK_END = {1: 0, 5: 1}
FILLS = [(j, i, h) for j in range(GR) for i in range(QB) for h in range(1 + (i >= 4))]
NF = len(FILLS)
SHARE = [4, 5, 4, 6, 6, 4, 4, 5, 5, 5, 0, 0]
assert sum(SHARE) == NF and len(SHARE) == SUB
TURN = SUB - 3
Q_LOTS = [(0, 1), (1, 2), (2, GR), (GR, NG)]
LAST_STAGE = 5
LATER_Q = [(n // 2, n % 2) for n in range(2, 2 * NG)]


def fills_of(k):
    return list(range(sum(SHARE[:k]), sum(SHARE[:k + 1])))


def later_q_of(k):
    return LATER_Q[2 * k:2 * k + 2]


def program(nc, a, out):
    with ExitStack() as ctx:
        def sb(name, shape, dt=F32):
            return ctx.enter_context(nc.sbuf_tensor(name, shape, dt))

        def sem(name):
            return ctx.enter_context(nc.semaphore(name))

        bank = [ctx.enter_context(nc.psum_tensor(f"bank{i}", [P, CH], F32)) for i in range(2)]
        stT = ctx.enter_context(nc.psum_tensor("stT", [P, 2, 2 * CH], F32))
        bankY = ctx.enter_context(nc.psum_tensor("bankY", [P, CH], F32))
        bankM = ctx.enter_context(nc.psum_tensor("bankM", [P, CH], F32))
        quad = [stT[:, i // 2, (i % 2) * CH:(i % 2 + 1) * CH] for i in range(4)]

        identf = sb("identf", [P, P])
        identb = sb("identb", [P, P], BF16)
        maskb = sb("maskb", [P, P], BF16)
        mean_w = sb("mean_w", [P, P])
        epsc = sb("epsc", [P, 2])
        x_rows = sb("x_rows", [P, NT, P])
        xT = sb("xT", [P, T])
        xc = sb("xc", [P, T])
        sq = sb("sq", [P, T])
        rstd = sb("rstd", [P, T])
        hT = sb("hT", [P, T])
        cT = sb("cT", [P, 2, B])
        csil = sb("csil", [P, 3, 2 * B])
        wmod = sb("wmod", [P, 2, 6 * D])
        mod = sb("mod", [P, 2, 6, B])
        sgn = sb("sgn", [P, 2, 2, B])
        E0, R0 = 6, 16
        NR = R0 * (E0 + 1)
        bwT = sb("bwT", [P, D])
        downT = sb("downT", [P, NR])
        up = sb("up", [NR, D])
        rw = sb("rw", [P, E0])
        rb = sb("rb", [P, E0])
        bb = sb("bb", [P, 1])
        earlier = sb("earlier", [P, E0, E0])
        wqkv = sb("wqkv", [P, 3 * D])
        bqkv = sb("bqkv", [P, 3])
        owT = sb("owT", [P, D])
        ob = sb("ob", [P, 1])
        head_of = sb("head_of", [P, NH])
        wv_eo = sb("wv_eo", [P, 2, NH // 2, 2 * HD1])
        bq_s = sb("bq_s", [P, 1])
        ga2 = sb("ga2", [P, B])
        ob_v = sb("ob_v", [P, 1])
        ones_eo = sb("ones_eo", [P, 2 * HD1])
        nw = sb("nw", [P, 1])
        wrT = sb("wrT", [P, NGR + E1])
        spread = sb("spread", [104, E1, P], F16)

        attn = ExitStack()

        def sa(name, shape, dt=F32):
            return attn.enter_context(nc.sbuf_tensor(name, shape, dt))

        wqT = sa("wqT", [HD0, H0, D])
        wkT = sa("wkT", [HD0, H0, C0])
        wvT = sa("wvT", [HD0, H0, C0])
        wo = sa("wo", [HD0, H0, D])
        wkv = sa("wkv", [P, 3, C0])
        qk = sa("qk", [P, H0 * C0])
        vo = sa("vo", [P, H0 // GR, D])
        vo_now = sa("vo_now", [P, D])
        lat = sa("lat", [97, T], F16)
        latO = sa("latO", [P, NT, 2 * C0])
        q_hi0 = sa("q_hi0", [P, NG // 2, L], F16)
        q_lo0 = sa("q_lo0", [P, NG // 2, L], F16)
        q_hi = [q_hi0[:], xc[:].bitcast(F16).rearrange("p (g t) -> p g t", t=L)]
        q_lo = [q_lo0[:], sq[:].bitcast(F16).rearrange("p (g t) -> p g t", t=L)]
        q_st = sa("q_st", [97, B * H0, L], F16)
        probs = sa("probs", [P, 2, 2, 2 * CH])
        part_max = sa("part_max", [P, 2, GR, QB])
        row_max = sa("row_max", [P, GR * QB])
        neg_max = sa("neg_max", [GR * QB, P], F16)
        y_raw = x_rows[:, 0:NT // 2, :].rearrange("p (c n) d -> p c (n d)", c=2)
        ln_sum = x_rows[:, NT // 2:NT, :].rearrange("p (c n) d -> p c (n d)", c=2)
        y_part = rstd[:, 0:2 * CH].rearrange("p (v t) -> p v t", v=2)
        inv_sum = sa("inv_sum", [P, 2, CH])
        y_n = sa("y_n", [P, 2, CH])

        attn.close()

        lg = sb("lg", [P, NT, 12])
        pr = sb("pr", [P, NT, 12])
        st = sb("st", [P, 6, NT, 4])
        gt = sb("gt", [P, NT, 36])
        eq = sb("eq", [P, NT, 36])
        rank = sb("rank", [P, NT, 6])
        wts = sb("wts", [P, NT, 8])
        wx = sb("wx", [P, NT, NR])
        wxT = sb("wxT", [NR, T])
        lowr = sb("lowr", [NR, 2, CH])
        ffn = sb("ffn", [P, 2, CH])
        hwin = sb("hwin", [P, 2, P])
        qw = sb("qw", [P, 2, P])
        kx = sb("kx", [P, 2, 2, NH, WIN])
        vw = sb("vw", [P, 2, 2, P])
        mx = sb("mx", [P, 2, NH])
        sub = sb("sub", [P, 2, NH, WIN])
        pw = sb("pw", [P, 2, NH, WIN])
        pT = sb("pT", [P, 2, NH // 2 * P])
        inv_w = sb("inv_w", [P, 2, P])
        w1 = sb("w1", [P, E1 * F1])
        w2 = sb("w2", [P, E1 * F1])
        w1h = sb("w1h", [P, 2, E1 * F1], F16)
        w2h = sb("w2h", [P, 2, E1 * F1], F16)
        xnh = sb("xnh", [P, 2, T], F16)
        cT16 = sb("cT16", [104, T], F16)
        hid = sb("hid", [P, 2, 2 * CH])
        hidh = sb("hidh", [P, 2, 2, 2 * CH], F16)
        cw = sb("cw", [P, 2, CH])
        yw = sb("yw", [P, 2, CH])

        S = {n: sem(n) for n in (
            "c_loaded", "w_attn_loaded", "ident_step", "consts", "csil_step", "silu_ready", "mod_product", "mod_ready",
            "gate_step", "x_turned", "xT_ready", "qk_product", "qk_ready", "vo_product", "vo_ready", "lat_product",
            "lat_hi", "lat_ready", "latO_product", "latO_ready", "q_product", "q_hi_ready", "q_lo_ready",
            "scores_ready", "max_taken", "row_max_ready", "max_turned", "neg_max_ready", "max_placed",
            "st_ready", "exp_done", "masked", "pv_done", "y_done", "ln_done", "y_copied", "y_moved", "inv_ready", "y_n_ready",
            "vo_now_ready", "pool_passed", "proj_done", "x_updated", "out_turned", "out_rows", "stored")}
        x_loaded = [sem(f"x_loaded{c}") for c in range(NC)]
        q_placed = [sem(f"q_placed{i}") for i in range(len(Q_LOTS))]
        N = {n: sem("n_" + n) for n in ("mean", "centred", "squared", "var", "ln", "rstd", "scaled", "h")}

        W = {n: sem("w_" + n) for n in (
            "small_loaded", "w12_loaded", "consts_b", "logits", "logit_ready", "exp_in", "exp_out", "weights_ready",
            "wx_turned", "wxT_ready", "low_product", "low_ready", "ffn_product", "ffn_ready", "x_ffn",
            "prep", "bias_product", "k_product", "k_biased", "hwin_ready", "q_product", "v_product", "q_ready", "k_ready",
            "v_ready", "s_product", "max_ready",
            "sub_ready", "exp_ready", "p_turned", "pT_ready", "o_product", "inv_ready",
            "o_ready", "att_product", "att_ready", "x_att",
            "w_hi", "w_lo", "dchain", "pchain")}
        E = {n: sem("e_" + n) for n in (
            "xn_scaled", "xn", "xn_hi", "xn_lo", "logits", "exp_in", "exp_out", "weights_ready", "cw_turned", "c_hi", "c_lo", "pre", "act",
            "hid_hi", "hid_lo", "y", "cb", "cw", "yw", "z")}
        x_final = sem("x_final")

        x_dram = a["x"].rearrange("b (n p) d -> p (b n) d", p=P)
        out_dram = out.rearrange("b (n p) d -> p (b n) d", p=P)

        block = ctx.enter_context(nc.Block())

        def steps(eng, body):
            body(0, 0, None, None)
            body(1, 0, 0, None)
            with eng.Fori(2, 4) as s:
                body(s, 0, 0, 0)
            body(4, 1, 0, 0)
            body(5, 1, 1, 0)
            with eng.Fori(6, 8) as s:
                body(s, 1, 1, 1)
            body(8, None, 1, 1)
            body(9, None, None, 1)

        def norm_count(k, name, v):
            if name in ("squared", "var", "ln", "rstd"):
                return NC * k + v
            return NC * min(k, 3) + (2 if name == "h" and k == 3 else 0) + v

        def loop_count(k, name, v):
            once = ("exp_in", "exp_out", "logits", "weights_ready")
            return k * (1 if name in once else NC if name in per_chunk else NC * E1) + v

        per_chunk = ("xn", "xn_hi", "xn_lo", "cw_turned", "c_hi", "c_lo")

        def need(eng, s, v):
            if not isinstance(v, int) or v > 0:
                eng.wait_ge(s, v)

        def windows(eng, body):
            def slot(j):
                body(j, lambda d: (j - d, (j - d) % 2) if 0 <= j - d < NT else None)
            for j in range(6):
                slot(j)
            with eng.Fori(3, NT // 2) as n:
                for p in range(2):
                    body(2 * n + p, lambda d: (2 * n + p - d, (p + d) % 2))
            for j in range(NT, NT + LAST_STAGE):
                slot(j)

        def experts(eng, ahead, unit):
            def chunk(c, last):
                for e in range(E1):
                    if e < E1 - 1:
                        ahead(c, e + 1)
                    elif not last:
                        ahead(c + 1, 0)
                    unit(c, e)
            ahead(0, 0)
            chunk(0, False)
            with eng.Fori(1, NC - 1) as c:
                chunk(c, False)
            chunk(NC - 1, True)

        def shifted_pieces(c):
            b, at = c // 2, (c % 2) * CH
            if at == 0:
                return [((b + 1) * L - SHIFT, b * L, SHIFT), (b * L, b * L + SHIFT, CH - SHIFT)]
            return [(b * L + at - SHIFT, b * L + at, CH)]

        h2_count = sum(len(shifted_pieces(c)) for c in range(NC))
        kT = sq
        oT = rstd
        z = hT

        @block.sync
        def _(sp):
            for c in range(NC):
                sp.dma_start(x_rows[:, 4 * c:4 * c + 4, :], x_dram[:, 4 * c:4 * c + 4, :]).then_inc(x_loaded[c], 16)
                if c == 0:
                    sp.dma_start(cT[:, 0, :], a["c0T"]).then_inc(S["c_loaded"], 16)
                    sp.dma_start(cT[:, 1, :], a["c1T"]).then_inc(S["c_loaded"], 16)
                if c == 1:
                    sp.dma_start(wmod[:, 0, :], a["wmod0"]).then_inc(S["c_loaded"], 16)
                    sp.dma_start(wmod[:, 1, :], a["wmod1"]).then_inc(S["c_loaded"], 16)
            sp.dma_start(wqT[:], a["wqT"]).then_inc(S["w_attn_loaded"], 16)
            sp.dma_start(wkT[:], a["wkT"]).then_inc(S["w_attn_loaded"], 16)
            sp.dma_start(wvT[:], a["wvT"]).then_inc(S["w_attn_loaded"], 16)
            sp.dma_start(wo[:], a["wo"]).then_inc(S["w_attn_loaded"], 16)
            for r in range(3):
                sp.dma_start(wkv[:, r, :], a["wkv"]).then_inc(S["w_attn_loaded"], 16)
            for dst, name in ((bwT, "bwT"), (downT, "downT"), (up, "up"), (rw, "rw"), (bb, "bb"), (wqkv, "wqkv"),
                              (bqkv, "bqkv"), (owT, "owT"), (ob, "ob"), (nw, "nw"), (wrT, "wrT")):
                sp.dma_start(dst[:], a[name]).then_inc(W["small_loaded"], 16)
            sp.dma_start(rb[:], a["rb"].partition_broadcast(P)).then_inc(W["small_loaded"], 16)
            for lot, (g0, g1) in enumerate(Q_LOTS):
                sp.wait_ge(S["q_hi_ready"], 2 * g1)
                sp.wait_ge(S["q_lo_ready"], 2 * g1)
                bq, g2, g3 = g0 // GR, g0 % GR, g0 % GR + g1 - g0
                for row, src in ((0, q_hi), (C0, q_lo), (2 * C0, q_hi)):
                    for j in range(GR):
                        sp.dma_start(q_st[row:row + C0, GR * g0 + j:GR * g1:GR, :],
                                     src[bq][C0 * j:C0 * j + C0, g2:g3, :]).then_inc(q_placed[lot], 16)

            def body(s, bm, be, bp):
                if bm is not None:
                    sp.wait_ge(S["neg_max_ready"], s + 1)
                    sp.dma_start(q_st[96:97, bass.ds(GR * s, GR), :].rearrange("o j (i t) -> o (j i) t", t=P),
                                 neg_max[:, :]).then_inc(S["max_placed"], 16)
            steps(sp, body)
            sp.wait_ge(S["x_updated"], 2 * NG)
            sp.dma_start(w1[:], a["w1"]).then_inc(W["w12_loaded"], 16)
            sp.dma_start(w2[:], a["w2"]).then_inc(W["w12_loaded"], 16)
            for c in range(NC):
                sp.wait_ge(S["out_rows"], c + 1)
                sp.dma_start(out_dram[:, 4 * c:4 * c + 4, :], x_rows[:, 4 * c:4 * c + 4, :]).then_inc(S["stored"], 16)
            sp.wait_ge(S["stored"], 16 * NC)

        @block.gpsimd
        def _(pool):
            pool.memset(identf[:], 0.0).then_inc(S["ident_step"], 1)
            pool.wait_ge(S["ident_step"], 1)
            pool.affine_select(out=identf[:], in_=identf[:], compare_op=ALU.not_equal, fill=1.0, base=0,
                               pattern=[[-1, P]], channel_multiplier=1).then_inc(S["ident_step"], 1)
            pool.memset(mean_w[:], 1.0 / D).then_inc(S["ident_step"], 1)
            pool.memset(epsc[:, 0:1], LN_EPS).then_inc(S["ident_step"], 1)
            pool.memset(epsc[:, 1:2], 1e-6).then_inc(S["ident_step"], 1)
            pool.memset(maskb[:], 0.0).then_inc(S["consts"], 1)
            pool.memset(identb[:], 0.0).then_inc(S["consts"], 1)
            pool.wait_ge(S["consts"], 2)
            pool.affine_select(out=identb[:], in_=identb[:], compare_op=ALU.not_equal, fill=1.0, base=0,
                               pattern=[[-1, P]], channel_multiplier=1).then_inc(S["consts"], 1)
            pool.affine_select(out=maskb[:], in_=maskb[:], compare_op=ALU.is_ge, fill=NEG, base=0,
                               pattern=[[-1, P]], channel_multiplier=1).then_inc(S["consts"], 1)
            pool.wait_ge(S["consts"], 4)
            pool.memset(lat[96:97, :], 1.0).then_inc(S["consts"], 1)
            pool.wait_ge(S["consts"], 5)
            pool.memset(latO[:, :, C0:2 * C0], 1.0).then_inc(S["consts"], 1)
            pool.memset(part_max[:], -3e38).then_inc(S["consts"], 1)
            pool.memset(earlier[:], 1.0).then_inc(W["pchain"], 1)
            pool.memset(head_of[:], 1.0).then_inc(W["pchain"], 1)
            pool.memset(spread[:], 0.0).then_inc(W["pchain"], 1)
            pool.memset(wv_eo[:], 0.0).then_inc(W["pchain"], 1)
            pool.memset(ones_eo[:], 1.0).then_inc(W["pchain"], 1)
            pool.wait_ge(W["pchain"], 5)
            pool.affine_select(out=earlier[:], in_=earlier[:], compare_op=ALU.is_ge, fill=0.0, base=-1,
                               pattern=[[1, E0], [-1, E0]], channel_multiplier=0).then_inc(W["pchain"], 1)
            pool.affine_select(out=head_of[:], in_=head_of[:], compare_op=ALU.is_ge, fill=0.0, base=0,
                               pattern=[[-HD1, NH]], channel_multiplier=1).then_inc(W["pchain"], 1)
            pool.affine_select(out=spread[:], in_=spread[:], compare_op=ALU.not_equal, fill=1.0 / UP, base=0,
                               pattern=[[-1, E1], [0, P]], channel_multiplier=1).then_inc(W["pchain"], 1)
            pool.affine_select(out=ones_eo[:], in_=ones_eo[:], compare_op=ALU.is_ge, fill=0.0, base=0,
                               pattern=[[-WIN, 2], [0, HD1]], channel_multiplier=1).then_inc(W["pchain"], 1)
            pool.wait_ge(W["pchain"], 9)
            pool.affine_select(out=head_of[:], in_=head_of[:], compare_op=ALU.is_ge, fill=0.0, base=HD1 - 1,
                               pattern=[[HD1, NH]], channel_multiplier=-1).then_inc(W["pchain"], 1)
            pool.affine_select(out=spread[:], in_=spread[:], compare_op=ALU.not_equal, fill=1.0 / UP, base=-96,
                               pattern=[[-1, E1], [0, P]], channel_multiplier=1).then_inc(W["pchain"], 1)
            pool.affine_select(out=ones_eo[:], in_=ones_eo[:], compare_op=ALU.is_ge, fill=0.0, base=WIN - 1,
                               pattern=[[WIN, 2], [0, HD1]], channel_multiplier=-1).then_inc(W["pchain"], 1)
            pool.wait_ge(W["small_loaded"], 16 * 12)
            wv = wqkv[:, 2 * D:3 * D].rearrange("p (n e k) -> p n e k", e=2, k=HD1)
            for e in range(2):
                pool.tensor_copy(wv_eo[:, e, :, e * HD1:(e + 1) * HD1], wv[:, :, e, :]).then_inc(W["pchain"], 1)

            def body(s, bm, be, bp):
                if bp is not None:
                    pool.tensor_copy(vo_now[:], vo[:, bass.ds(s - 2 - GR * bp, 1), :].rearrange("p o d -> p (o d)"))\
                        .then_inc(S["vo_now_ready"], 1)
                def normalise(c, g):
                    pool.wait_ge(S["inv_ready"], 2 * g + c + 1)
                    pool.wait_ge(S["y_moved"], 8 * g + (6 if c == 0 else 8))
                    if not (isinstance(g, int) and g == 0):
                        pool.wait_ge(S["proj_done"], 2 * (g - 1) + c + 1)
                    pool.tensor_tensor(y_n[:, c, :], y_raw[:, c, :], inv_sum[:, c, :], ALU.mult)\
                        .then_inc(S["y_n_ready"], 1)

                for k in range(SUB):
                    t = k % NTL
                    if be is not None and t in MASKED:
                        n = SUB * (s - 1) + k
                        second = TILES[t][1][1][2]
                        for x in range(2):
                            pool.wait_ge(S["exp_done"], 2 * n + x + 1)
                            pool.sem_inc(S["pool_passed"], 1)
                            tri = probs[:, k % 2, x, 0:2 * second].rearrange("p (u q) -> p u q", u=2)[:, :, 0:P]
                            pool.affine_select(out=tri, in_=tri, compare_op=ALU.is_ge, fill=0.0, base=0,
                                               pattern=[[0, 2], [1, P]], channel_multiplier=-1)\
                                .then_inc(S["masked"], 1)
                    if k == 0 and bp is not None:
                        normalise(1, s - 2)
                    if be is not None and k == NTL + 3:
                        normalise(0, s - 1)
                if bp is not None:
                    pool.wait_ge(S["proj_done"], 2 * (s - 1))
            steps(pool, body)

            pool.wait_ge(S["x_updated"], 2 * NG)
            pool.memset(wx[:, :, 0:R0], 1.0).then_inc(W["consts_b"], 1)
            pool.memset(cT16[0:96, :], 0.0).then_inc(W["consts_b"], 1)

            pool.wait_ge(N["h"], norm_count(2, "h", h2_count))
            pool.wait_ge(W["k_biased"], NC)

            def window(j, stage):
                if stage(2):
                    i, q = stage(2)
                    need(pool, W["v_product"], i - 1)
                    pool.sem_inc(S["pool_passed"], 1)
                    pool.tensor_copy(hwin[:, q, :], hT[:, bass.ds(i * P, P)]).then_inc(W["hwin_ready"], 1)
                if stage(0):
                    i, q = stage(0)
                    need(pool, W["s_product"], i - 1)
                    pool.sem_inc(S["pool_passed"], 1)
                    shape = [P, NH, WIN]
                    for w in range(2):
                        pool.tensor_tensor(kx[:, q, w],
                                           kT[:, bass.ds(i * P + w * WIN, WIN)].unsqueeze(1).broadcast_to(shape),
                                           head_of[:].unsqueeze(2).broadcast_to(shape), ALU.mult)\
                            .then_inc(W["k_ready"], 1)
            windows(pool, window)

            for k in range(2):

                def unit(c, e):
                    u = E1 * c + e
                    pool.wait_ge(E["yw"], loop_count(k, "yw", u + 1))
                    need(pool, E["z"], loop_count(k, "z", u))
                    pool.sem_inc(S["pool_passed"], 1)
                    zc = z[:, bass.ds(c * CH, CH)]
                    pool.tensor_tensor(zc, zc, yw[:, e % 2, :], ALU.add).then_inc(E["z"], 1)
                experts(pool, lambda c, e: None, unit)

        @block.tensor
        def _(pe):
            mm = pe.matmul

            pe.wait_ge(S["ident_step"], 5)
            for c in range(NC):
                pe.wait_ge(x_loaded[c], 16)
                for i in range(4):
                    m = pe.transpose(quad[c][:, i * P:(i + 1) * P], x_rows[:, 4 * c + i, :], identf[:])
                m.then_inc(S["x_turned"], 1)
            pe.wait_ge(S["c_loaded"], 64)
            pe.wait_ge(S["silu_ready"], 1)
            for l in range(2):
                for j in range(6):
                    m = mm(bankM[:, (6 * l + j) * B:(6 * l + j + 1) * B], wmod[:, l, j * D:(j + 1) * D],
                           csil[:, 2, l * B:l * B + B], start=True, stop=True)
            m.then_inc(S["mod_product"], 1)
            def norm(k, x_ready, centre):

                def mean(c):
                    x_ready(pe, c)
                    if c >= 2:
                        pe.wait_ge(N["centred"], norm_count(k, "centred", c - 1))
                    mm(quad[c % 2], mean_w[:], xT[:, c * CH:(c + 1) * CH], start=True, stop=True)\
                        .then_inc(N["mean"], 1)

                def var(c):
                    pe.wait_ge(N["squared"], norm_count(k, "squared", c + 1))
                    if c >= 2:
                        pe.wait_ge(N["ln"], norm_count(k, "ln", c - 1))
                    mm(quad[2 + c % 2], mean_w[:], sq[:, c * CH:(c + 1) * CH], start=True, stop=True)\
                        .then_inc(N["var"], 1)
                for i in range(NC + 1):
                    if i < NC and centre:
                        mean(i)
                    if i >= 1:
                        var(i - 1)

            norm(0, lambda e, c: e.wait_ge(S["xT_ready"], c + 1), True)
            pe.wait_ge(S["w_attn_loaded"], 16 * 7)
            for h in range(H0):
                m = mm(bank[0][:, h * C0:(h + 1) * C0], wqT[:, h, :], wkT[:, h, :], start=True, stop=True)
            m.then_inc(S["qk_product"], 1)
            for g in range(H0 // GR):
                for j in range(GR):
                    h = GR * g + j
                    m = mm(bank[1][C0 * j:C0 * j + C0, g * D:(g + 1) * D], wvT[:, h, :], wo[:, h, :],
                           start=True, stop=True)
            m.then_inc(S["vo_product"], 1)

            pe.wait_ge(S["qk_ready"], 1)
            pe.wait_ge(S["vo_ready"], 1)

            def latents(c):
                pe.wait_ge(N["h"], norm_count(0, "h", c + 1))
                if c >= 2:
                    pe.wait_ge(S["lat_ready"], c - 1)
                mm(bank[c % 2][0:96, :], wkv[:].rearrange("p r c -> p (r c)"), hT[:, c * CH:(c + 1) * CH],
                   start=True, stop=True).then_inc(S["lat_product"], 1)

            def queries(g, c):
                n = 2 * g + c
                b = g // GR
                if n >= 4:
                    pe.wait_ge(S["q_lo_ready"], n - 3)
                mm(quad[n % 4], qk[:, (g % GR) * P:(g % GR + 1) * P],
                   hT[:, b * L + c * CH:b * L + (c + 1) * CH], start=True, stop=True).then_inc(S["q_product"], 1)

            latents(0)
            latents(1)
            pe.wait_ge(N["ln"], norm_count(0, "ln", NC))
            queries(0, 0)
            queries(0, 1)
            latents(2)
            latents(3)
            for i in range(NT):
                m = mm(bankY[:, i * C0:(i + 1) * C0], hT[:, i * P:(i + 1) * P], wkv[:, 0, :], start=True, stop=True)
            m.then_inc(S["latO_product"], 1)

            def body(s, bm, be, bp):
                first = isinstance(s, int) and s == 0

                def fill(f):
                    j, i, half = FILLS[f]
                    n = NF * s + f
                    if first and f < 2:
                        if f == 0:
                            pe.wait_ge(S["lat_ready"], NC)
                            pe.wait_ge(S["consts"], 7)
                    else:
                        pe.wait_ge(S["max_taken"], n - 1)
                    width = min(CH, (i + 1) * P - half * CH)
                    diag = (i // 4 == half)
                    o = bank[f % 2]
                    m = mm(o[:, 0:width], q_st[0:96, bass.ds(GR * s + j, 1), i * P:(i + 1) * P]
                           .rearrange("p o t -> p (o t)"),
                           lat[0:96, bm * L + half * CH:bm * L + half * CH + width], start=True, stop=not diag)
                    if diag:
                        m = mm(o[:, width - P:width], identb[:], maskb[:], start=False, stop=True)
                    m.then_inc(S["scores_ready"], 1)

                def turn_max():
                    pe.wait_ge(S["row_max_ready"], s + 1)
                    if bp is not None:
                        pe.wait_ge(S["x_updated"], 2 * (s - 1))
                    pe.transpose(bankM[0:GR * QB, 0:P], row_max[:], identf[:]).then_inc(S["max_turned"], 1)

                def scores_t(k, x):
                    n = SUB * (s - 1) + k
                    c, segs = TILES[k % NTL]
                    if k == 0 and x == 0:
                        pe.wait_ge(S["max_placed"], 16 * s)
                    if True:
                        if not (isinstance(s, int) and s == 1 and k == 0):
                            pe.wait_ge(S["exp_done"], 2 * n - 1 + x)
                        h = GR * (s - 1) + 2 * (k // NTL) + x
                        for kb, q0, at in segs:
                            m = mm(stT[:, x, at:at + CH - q0], lat[0:97, be * L + kb * P:be * L + (kb + 1) * P],
                                   q_st[0:97, bass.ds(h, 1), c * CH + q0:(c + 1) * CH].rearrange("p o t -> p (o t)"),
                                   start=True, stop=True)
                        m.then_inc(S["st_ready"], 1)

                def values(k, g, bg, part):
                    n = SUB * g + k
                    c, segs = TILES[k % NTL]
                    t = k % NTL
                    if part == 0:
                        if t in MASKED:
                            pe.wait_ge(S["masked"], 16 * g + 8 * (k // NTL) + 2 * MASKED[t] + 2)
                        else:
                            pe.wait_ge(S["exp_done"], 2 * n + 2)
                        if segs[0][0] == 0 and not (isinstance(g, int) and g == 0 and k == 0):
                            v = 4 * g + 2 * (k // NTL) + c
                            pe.wait_ge(S["y_copied"], v)
                    kb, q0, at = segs[part]
                    for x in range(2):
                        m = mm(bankY[64 * x:64 * x + 64, q0:CH], latO[:, bg * QB + kb, :],
                               probs[:, k % 2, x, at:at + CH - q0], start=(kb == 0), stop=(kb == 4 * c + 3))
                    if part == 1:
                        m.then_inc(S["pv_done"], 1)

                def project(c):
                    pe.wait_ge(S["y_n_ready"], 2 * (s - 2) + c + 1)
                    if c == 0:
                        pe.wait_ge(S["vo_now_ready"], s - 1)
                        if be is not None:
                            pe.wait_ge(S["neg_max_ready"], s if bm is not None else NG)
                    else:
                        pe.wait_ge(S["x_updated"], 2 * (s - 2) + 1)
                    mm(bankM[:, :], vo_now[:], y_n[:, c, :], start=True, stop=True).then_inc(S["proj_done"], 1)

                if bm is not None:
                    lots = {0: [0], 1: [1], 4: [3]}.get(s, []) if isinstance(s, int) else [2] if bm == 0 else []
                    for i in lots:
                        pe.wait_ge(q_placed[i], 16 * 3 * GR)
                if be is not None and isinstance(s, int) and s == 1:
                    pe.wait_ge(S["q_lo_ready"], 2 * NG)
                    pe.wait_ge(S["latO_ready"], 1)
                for k in range(SUB if bm is not None or be is not None else 5):
                    before = (k - 1, s - 1, be) if k else (SUB - 1, s - 2, bp)
                    if k and be is None:
                        before = None
                    if before and before[2] is None:
                        before = None
                    work = []
                    if be is not None:
                        work += [lambda: scores_t(k, 0), lambda: scores_t(k, 1)]
                    if before:
                        work += [lambda: values(*before, 0), lambda: values(*before, 1)]
                    if first:
                        work += [lambda q=q: queries(*q) for q in later_q_of(k)]
                    fl = fills_of(k) if bm is not None else []
                    done = 0
                    for n, w in enumerate(work):
                        upto = len(fl) * (n + 1) // (len(work) + 1)
                        for f in fl[done:upto]:
                            fill(f)
                        done = upto
                        w()
                    for f in fl[done:]:
                        fill(f)
                    if bp is not None and k in (2, 4):
                        project(k // 2 - 1)
                    if bm is not None and k == TURN:
                        turn_max()
            steps(pe, body)

            pe.wait_ge(S["x_updated"], 2 * NG)
            norm(1, lambda e, c: None, True)
            pe.wait_ge(W["small_loaded"], 16 * 12)
            for i in range(NT):
                if i % 4 == 0:
                    pe.wait_ge(N["h"], norm_count(1, "h", i // 4 + 1))
                m = mm(bank[0][:, i * E0:(i + 1) * E0], hT[:, i * P:(i + 1) * P], rw[:], start=True, stop=True)
            m.then_inc(W["logits"], 1)
            lowb, outb = (bank[1], bankY), (bankM, bank[0])

            def low(c):
                if c >= 2:
                    pe.wait_ge(W["low_ready"], c - 1)
                mm(lowb[c % 2][0:NR, :], downT[:], hT[:, c * CH:(c + 1) * CH], start=True, stop=True)\
                    .then_inc(W["low_product"], 1)
            low(0)
            low(1)
            pe.wait_ge(W["weights_ready"], 1)
            for c in range(NC):
                for i in range(4):
                    m = pe.transpose(quad[c][0:NR, i * P:(i + 1) * P], wx[:, 4 * c + i, :], identf[:])
                m.then_inc(W["wx_turned"], 1)
            for c in range(NC):
                if c >= 2:
                    pe.wait_ge(W["ffn_ready"], c - 1)
                mm(outb[c % 2][:], bwT[:], hT[:, c * CH:(c + 1) * CH], start=True, stop=False)
                pe.wait_ge(W["low_ready"], c + 1)
                mm(outb[c % 2][:], up[:], lowr[:, c % 2, :], start=False, stop=True).then_inc(W["ffn_product"], 1)
                if c + 2 < NC:
                    low(c + 2)

            norm(2, lambda e, c: e.wait_ge(W["x_ffn"], c + 1), True)
            pe.wait_ge(W["pchain"], 14)
            mm(bank[0][:, 2 * P:2 * P + 1], owT[:], bqkv[:, 2:3], start=True, stop=True)\
                .then_inc(W["bias_product"], 1)
            for c in range(NC):
                pe.wait_ge(N["h"], norm_count(2, "h", (3, 3, h2_count, h2_count)[c]))
                need(pe, W["k_biased"], c - 1)
                mm((bankY, bankM)[c % 2][:], wqkv[:, D:2 * D], hT[:, c * CH:(c + 1) * CH], start=True, stop=True)\
                    .then_inc(W["k_product"], 1)

            def out_product(c):
                pe.wait_ge(W["o_ready"], 4 * (c + 1))
                if c >= 2:
                    pe.wait_ge(W["att_ready"], c - 1)
                mm(bank[c % 2][:], owT[:], oT[:, c * CH:(c + 1) * CH], start=True, stop=True)\
                    .then_inc(W["att_product"], 1)

            def window(j, stage):
                if stage(1):
                    i, q = stage(1)
                    pe.wait_ge(W["q_ready"], i + 1)
                    pe.wait_ge(W["k_ready"], 2 * i + 2)
                    need(pe, W["sub_ready"], i - 1)
                    for w in range(2):
                        m = mm(quad[q][WIN * w:WIN * w + WIN, :], qw[:, q, WIN * w:WIN * w + WIN],
                               kx[:, q, w].rearrange("p h k -> p (h k)"), start=True, stop=True)
                    m.then_inc(W["s_product"], 1)
                if stage(0):
                    i, q = stage(0)
                    need(pe, W["q_ready"], i)
                    mm(bank[0][:, 0:P], wqkv[:, 0:D], hT[:, bass.ds(i * P, P)], start=True, stop=True)\
                        .then_inc(W["q_product"], 1)
                if stage(3):
                    i, q = stage(3)
                    pe.wait_ge(W["exp_ready"], i + 1)
                    need(pe, W["pT_ready"], i - 1)
                    for r in range(NH // 2):
                        m = pe.transpose(quad[2 + q][:, r * P:(r + 1) * P],
                                         pw[:, q, 2 * r:2 * r + 2, :].rearrange("p h k -> p (h k)"), identf[:])
                    m.then_inc(W["p_turned"], 1)
                    pe.wait_ge(W["hwin_ready"], i + 1)
                    need(pe, W["v_ready"], i)
                    for w in range(2):
                        for e in range(2):
                            m = mm(bank[1][WIN * e:WIN * e + WIN, w * P:(w + 1) * P],
                                   hwin[:, q, WIN * w:WIN * w + WIN],
                                   wv_eo[:, e].rearrange("p n c -> p (n c)"), start=True, stop=True)
                    m.then_inc(W["v_product"], 1)
                if stage(4):
                    i, q = stage(4)
                    pe.wait_ge(W["pT_ready"], i + 1)
                    pe.wait_ge(W["v_ready"], i + 1)
                    need(pe, W["o_ready"], i - 1)
                    o = (bankY, bankM)[q]
                    for w in range(2):
                        for r in range(NH // 2):
                            mm(o[32 * r:32 * r + 32, w * WIN:(w + 1) * WIN], vw[:, q, w, 32 * r:32 * r + 32],
                               pT[:, q, r * P + w * WIN:r * P + (w + 1) * WIN], start=True, stop=True)
                    for r in range(NH // 2):
                        m = mm(o[32 * r:32 * r + 32, P:2 * P], ones_eo[:], pT[:, q, r * P:(r + 1) * P],
                               start=True, stop=True)
                    m.then_inc(W["o_product"], 1)
                if isinstance(j, int) and j == NT + 2:
                    out_product(0)
                if isinstance(j, int) and j == NT + 3:
                    out_product(1)
            pe.wait_ge(W["prep"], 2)
            windows(pe, window)
            out_product(2)
            out_product(3)

            norm(3, lambda e, c: e.wait_ge(W["x_att"], 6), True)
            for k in range(2):
                norm(4 + k, lambda e, c: None, False)
                for i in range(NT):
                    if i % 4 == 0:
                        pe.wait_ge(E["xn"], loop_count(k, "xn", i // 4 + 1))
                    m = mm(bank[0][:, i * 12:(i + 1) * 12], xc[:, i * P:(i + 1) * P], wrT[:], start=True, stop=True)
                m.then_inc(E["logits"], 1)
                pe.wait_ge(E["weights_ready"], loop_count(k, "weights_ready", 1))
                for c in range(NC):
                    for i in range(4):
                        m = pe.transpose(quad[c][0:E1, i * P:(i + 1) * P], wts[:, 4 * c + i, :], identf[:])
                    m.then_inc(E["cw_turned"], 1)
                pe.wait_ge(E["xn_lo"], loop_count(k, "xn_lo", NC))
                pe.wait_ge(W["w_lo"], 2)
                pe.wait_ge(E["c_lo"], loop_count(k, "c_lo", NC))

                def ahead(c, e):
                    u = E1 * c + e
                    need(pe, E["act"], loop_count(k, "act", u - 1))
                    for f in range(2):
                        at = e * F1 + f * P
                        for t, (wp, xp) in enumerate(((0, 0), (0, 1), (1, 0))):
                            m = mm(stT[:, e % 2, f * CH:(f + 1) * CH], w1h[:, wp, at:at + P],
                                   xnh[:, xp, bass.ds(c * CH, CH)], start=(t == 0), stop=(t == 2))
                    m.then_inc(E["pre"], 1)

                def unit(c, e):
                    u = E1 * c + e
                    need(pe, E["cw"], loop_count(k, "cw", u - 1))
                    mm((bankY, bankM)[e % 2][:], spread[:, e, :], cT16[:, bass.ds(c * CH, CH)],
                       start=True, stop=True).then_inc(E["cb"], 1)
                    pe.wait_ge(E["hid_lo"], loop_count(k, "hid_lo", u + 1))
                    need(pe, E["yw"], loop_count(k, "yw", u - 1))
                    for n, (f, wp, hp) in enumerate([(f, *q) for f in range(2) for q in ((0, 0), (0, 1), (1, 0))]):
                        at = (2 * e + f) * P
                        m = mm(bank[e % 2][:], w2h[:, wp, at:at + P], hidh[:, e % 2, hp, f * CH:(f + 1) * CH],
                               start=(n == 0), stop=(n == 5))
                    m.then_inc(E["y"], 1)
                experts(pe, ahead, unit)
            for c in range(NC):
                pe.wait_ge(x_final, c + 1)
                for i in range(4):
                    m = pe.transpose(quad[c][:, i * P:(i + 1) * P], xT[:, (4 * c + i) * P:(4 * c + i + 1) * P],
                                     identf[:])
                m.then_inc(S["out_turned"], 1)

        @block.scalar
        def _(act):
            A = nc.scalar.activation
            act.preload_act_table_set("natural_log_exp_and_others")
            act.wait_ge(S["c_loaded"], 64)
            A(csil[:, 0, :], cT[:].rearrange("p l b -> p (l b)"), ACT.Exp, scale=-1.0).then_inc(S["csil_step"], 1)
            for c in range(NC):
                act.wait_ge(S["x_turned"], c + 1)
                A(xT[:, c * CH:(c + 1) * CH], quad[c], ACT.Copy).then_inc(S["xT_ready"], 1)
            def norm(k, eps, centre):
                src = xc if centre else z
                for i in range(NC + 1):
                    if i < NC:
                        cs = slice(i * CH, (i + 1) * CH)
                        if centre:
                            act.wait_ge(N["centred"], norm_count(k, "centred", i + 1))
                        elif k == 4:
                            act.wait_ge(N["h"], norm_count(3, "h", i + 1))
                        else:
                            act.wait_ge(E["z"], loop_count(0, "z", E1 * (i + 1)))
                        A(sq[:, cs], src[:, cs], ACT.Square).then_inc(N["squared"], 1)
                    if i >= 1:
                        cs = slice((i - 1) * CH, i * CH)
                        act.wait_ge(N["var"], norm_count(k, "var", i))
                        A(rstd[:, cs], quad[2 + (i - 1) % 2], ACT.Ln, bias=epsc[:, eps:eps + 1]).then_inc(N["ln"], 1)
                        act.wait_ge(N["ln"], norm_count(k, "ln", i))
                        A(rstd[:, cs], rstd[:, cs], ACT.Exp, scale=-0.5).then_inc(N["rstd"], 1)

            norm(0, 0, True)
            act.wait_ge(S["qk_product"], 1)
            A(qk[:], bank[0][:], ACT.Copy, scale=HD0 ** -0.5).then_inc(S["qk_ready"], 1)

            def latents(c):
                act.wait_ge(S["lat_product"], c + 1)
                A(lat[0:96, c * CH:(c + 1) * CH], bank[c % 2][0:96, :], ACT.Copy).then_inc(S["lat_hi"], 1)

            def queries(g, c):
                n = 2 * g + c
                act.wait_ge(S["q_product"], n + 1)
                A(q_hi[g // GR][:, g % GR, c * CH:(c + 1) * CH], quad[n % 4], ACT.Copy).then_inc(S["q_hi_ready"], 1)

            latents(0)
            latents(1)
            queries(0, 0)
            queries(0, 1)
            latents(2)
            latents(3)

            def body(s, bm, be, bp):
                def exps(k):
                    n = SUB * (s - 1) + k
                    c, segs = TILES[k % NTL]
                    width = segs[1][2] + CH - segs[1][1]
                    for x in range(2):
                        act.wait_ge(S["st_ready"], 2 * n + x + 1)
                        if x == 0 and not (isinstance(s, int) and s == 1 and k < 2):
                            act.wait_ge(S["pv_done"], n - 1)
                        A(probs[:, k % 2, x, 0:width], stT[:, x, 0:width], ACT.Exp).then_inc(S["exp_done"], 1)

                def logs(pair, c, g):
                    act.wait_ge(S["y_copied"], 4 * g + 2 * pair + c + 1)
                    if pair == 0 and not (isinstance(g, int) and g == 0):
                        act.wait_ge(S["y_n_ready"], 2 * (g - 1) + c + 1)
                    for x in range(2):
                        j = 2 * pair + x
                        A(y_raw[C0 * j:C0 * j + C0, c, :], y_part[64 * x:64 * x + C0, c, :], ACT.Copy)\
                            .then_inc(S["y_moved"], 1)
                        A(ln_sum[C0 * j:C0 * j + C0, c, :], y_part[64 * x + C0:64 * x + 2 * C0, c, :], ACT.Ln)\
                            .then_inc(S["ln_done"], 1)
                    if pair == 1:
                        act.wait_ge(S["ln_done"], 8 * g + (6 if c == 0 else 8))
                        if not (isinstance(g, int) and g == 0):
                            act.wait_ge(S["y_n_ready"], 2 * (g - 1) + c + 1)
                        A(inv_sum[:, c, :], ln_sum[:, c, :], ACT.Exp, scale=-1.0).then_inc(S["inv_ready"], 1)

                for k in range(SUB):
                    if be is not None:
                        exps(k)
                    if k == 0 and bp is not None:
                        logs(1, 1, s - 2)
                    if be is not None:
                        if k == 2:
                            logs(0, 0, s - 1)
                        if k == NTL:
                            logs(0, 1, s - 1)
                        if k == NTL + 2:
                            logs(1, 0, s - 1)
                    if isinstance(s, int) and s == 0:
                        for q in later_q_of(k):
                            queries(*q)
                    if bm is not None and k == TURN:
                        act.wait_ge(S["max_turned"], s + 1)
                        if not (isinstance(s, int) and s == 0):
                            act.wait_ge(S["max_placed"], 16 * s)
                        A(neg_max[:], bankM[0:GR * QB, 0:P], ACT.Copy, scale=-1.0).then_inc(S["neg_max_ready"], 1)
            steps(act, body)

            norm(1, 0, True)
            act.wait_ge(W["exp_in"], 1)
            A(pr[:, :, 0:E0], lg[:, :, 0:E0], ACT.Exp).then_inc(W["exp_out"], 1)
            for c in range(NC):
                act.wait_ge(W["wx_turned"], c + 1)
                A(wxT[:, c * CH:(c + 1) * CH], quad[c][0:NR, :], ACT.Copy).then_inc(W["wxT_ready"], 1)
            outb = (bankM, bank[0])
            for c in range(NC):
                act.wait_ge(W["ffn_product"], c + 1)
                if c >= 2:
                    act.wait_ge(W["x_ffn"], c - 1)
                A(ffn[:, c % 2, :], outb[c % 2][:], ACT.Identity, bias=bb[:]).then_inc(W["ffn_ready"], 1)

            norm(2, 0, True)
            act.wait_ge(W["prep"], 1)
            for c in range(NC):
                act.wait_ge(W["k_product"], c + 1)
                A(kT[:, c * CH:(c + 1) * CH], (bankY, bankM)[c % 2][:], ACT.Identity, bias=bqkv[:, 1:2])\
                    .then_inc(W["k_biased"], 1)

            def window(j, stage):
                if stage(2):
                    i, q = stage(2)
                    act.wait_ge(W["sub_ready"], i + 1)
                    need(act, W["p_turned"], i - 1)
                    A(pw[:, q], sub[:, q], ACT.Exp).then_inc(W["exp_ready"], 1)
                if stage(0):
                    i, q = stage(0)
                    act.wait_ge(W["q_product"], i + 1)
                    need(act, W["s_product"], i - 1)
                    A(qw[:, q, :], bank[0][:, 0:P], ACT.Identity, bias=bq_s[:], scale=HD1 ** -0.5)\
                        .then_inc(W["q_ready"], 1)
                if stage(3):
                    i, q = stage(3)
                    act.wait_ge(W["p_turned"], i + 1)
                    need(act, W["o_product"], i - 1)
                    A(pT[:, q], quad[2 + q][:], ACT.Copy).then_inc(W["pT_ready"], 1)
                    act.wait_ge(W["v_product"], i + 1)
                    A(vw[:, q].rearrange("p w c -> p (w c)"), bank[1][:, 0:2 * P], ACT.Copy)\
                        .then_inc(W["v_ready"], 1)
            windows(act, window)
            act.wait_ge(W["prep"], 2)
            for c in range(NC):
                act.wait_ge(W["att_product"], c + 1)
                if c >= 2:
                    act.wait_ge(W["x_att"], (0, 1, 3, 4)[c - 1])
                A(ffn[:, c % 2, :], bank[c % 2][:], ACT.Identity, bias=ob_v[:]).then_inc(W["att_ready"], 1)

            norm(3, 0, True)
            act.wait_ge(W["w12_loaded"], 32)
            for dst, src in ((w1h, w1), (w2h, w2)):
                A(dst[:, 0, :], src[:], ACT.Copy, scale=UP).then_inc(W["w_hi"], 1)
            for k in range(2):
                act.preload_act_table_set("natural_log_exp_and_others")
                norm(4 + k, 1, False)
                for c in range(NC):
                    act.wait_ge(E["xn"], loop_count(k, "xn", c + 1))
                    if k:
                        act.wait_ge(E["pre"], loop_count(k - 1, "pre", NC * E1))
                    A(xnh[:, 0, c * CH:(c + 1) * CH], xc[:, c * CH:(c + 1) * CH], ACT.Copy).then_inc(E["xn_hi"], 1)
                act.wait_ge(E["exp_in"], loop_count(k, "exp_in", 1))
                A(pr[:], lg[:], ACT.Exp).then_inc(E["exp_out"], 1)
                act.wait_ge(W["consts_b"], 2)
                for c in range(NC):
                    act.wait_ge(E["cw_turned"], loop_count(k, "cw_turned", c + 1))
                    A(cT16[0:E1, c * CH:(c + 1) * CH], quad[c][0:E1, :], ACT.Copy).then_inc(E["c_hi"], 1)

                def ahead(c, e):
                    u = E1 * c + e
                    act.wait_ge(E["pre"], loop_count(k, "pre", u + 1))
                    need(act, E["hid_lo"], loop_count(k, "hid_lo", u - 1))
                    A(hid[:, e % 2, :], stT[:, e % 2, :], ACT.Silu, scale=1.0 / UP).then_inc(E["act"], 1)

                def unit(c, e):
                    u = E1 * c + e
                    act.wait_ge(E["cb"], loop_count(k, "cb", u + 1))
                    need(act, E["yw"], loop_count(k, "yw", u - 1))
                    A(cw[:, e % 2, :], (bankY, bankM)[e % 2][:], ACT.Copy).then_inc(E["cw"], 1)
                experts(act, ahead, unit)

        def add_ffn(dve, V, c):
            dve.wait_ge(W["ffn_ready"], c + 1)
            cs = slice(c * CH, (c + 1) * CH)
            V.scalar_tensor_tensor(out=xT[:, cs], in0=ffn[:, c % 2, :], scalar=mod[:, 0, 5, c // 2:c // 2 + 1],
                                   in1=xT[:, cs], op0=ALU.mult, op1=ALU.add).then_inc(W["x_ffn"], 1)

        def shifted_pieces_back(c):
            b = c // 2
            if c % 2 == 0:
                return [(b * L + SHIFT, 0, CH)]
            return [(b * L + CH + SHIFT, 0, CH - SHIFT), (b * L, CH - SHIFT, SHIFT)]

        @block.vector
        def _(dve):
            chain = [0]
            dch = S["gate_step"]

            def link(ins):
                chain[0] += 1
                ins.then_inc(dch, 1)
                dve.wait_ge(dch, chain[0])

            V = nc.vector
            dve.wait_ge(S["csil_step"], 1)
            link(V.tensor_scalar(csil[:, 1, :], csil[:, 0, :], 1.0, None, ALU.add))
            link(V.reciprocal(csil[:, 1, :], csil[:, 1, :]))
            V.tensor_tensor(csil[:, 2, :], cT[:].rearrange("p l b -> p (l b)"), csil[:, 1, :], ALU.mult)\
                .then_inc(S["silu_ready"], 1)
            def centre(k):
                for c in range(NC):
                    cs = slice(c * CH, (c + 1) * CH)
                    dve.wait_ge(N["mean"], norm_count(k, "mean", c + 1))
                    V.tensor_tensor(xc[:, cs], xT[:, cs], quad[c % 2], ALU.subtract).then_inc(N["centred"], 1)

            centre(0)
            dve.wait_ge(S["mod_product"], 1)
            link(V.tensor_copy(mod[:].rearrange("p l j b -> p (l j b)"), bankM[:, 0:12 * B]))
            for j in (1, 4):
                link(V.tensor_scalar(mod[:, :, j, :], mod[:, :, j, :], 1.0, None, ALU.add))
            for n, j in enumerate((2, 5)):
                gate = mod[:, :, j, :]
                link(V.tensor_scalar(sgn[:, n], gate, 0.0, 2.0, ALU.is_ge, ALU.mult))
                link(V.tensor_scalar(sgn[:, n], sgn[:, n], -1.0, None, ALU.add))
                link(V.tensor_tensor(gate, gate, sgn[:, n], ALU.mult))
                link(V.tensor_scalar(gate, gate, 0.25, None, ALU.max))
                link(V.tensor_tensor(gate, gate, sgn[:, n], ALU.mult))

            def norm(k, l, sh, sc, shifted=False):
                if k:
                    centre(k)
                for c in range(NC):
                    cs = slice(c * CH, (c + 1) * CH)
                    b = c // 2
                    dve.wait_ge(N["rstd"], norm_count(k, "rstd", c + 1))
                    V.scalar_tensor_tensor(out=xc[:, cs], in0=xc[:, cs], scalar=mod[:, l, sc, b:b + 1],
                                           in1=rstd[:, cs], op0=ALU.mult, op1=ALU.mult).then_inc(N["scaled"], 1)
                    dve.wait_ge(N["scaled"], norm_count(k, "scaled", c + 1))
                    for to, at, m in shifted_pieces(c) if shifted else [(c * CH, c * CH, CH)]:
                        V.tensor_scalar(hT[:, to:to + m], xc[:, at:at + m], mod[:, l, sh, b:b + 1], None, ALU.add)\
                            .then_inc(N["h"], 1)

            norm(0, 0, 0, 1)
            dve.wait_ge(S["vo_product"], 1)
            V.tensor_copy(vo[:].rearrange("p g d -> p (g d)"), bank[1][:]).then_inc(S["vo_ready"], 1)

            def latents(c):
                cs = slice(c * CH, (c + 1) * CH)
                dve.wait_ge(S["lat_hi"], c + 1)
                V.tensor_tensor(lat[64:96, cs], bank[c % 2][64:96, :], lat[64:96, cs], ALU.subtract)\
                    .then_inc(S["lat_ready"], 1)

            def queries(g, c):
                n = 2 * g + c
                dve.wait_ge(S["q_hi_ready"], n + 1)
                cs = slice(c * CH, (c + 1) * CH)
                V.tensor_tensor(q_lo[g // GR][:, g % GR, cs], quad[n % 4], q_hi[g // GR][:, g % GR, cs],
                                ALU.subtract).then_inc(S["q_lo_ready"], 1)

            latents(0)
            latents(1)
            queries(0, 0)
            queries(0, 1)
            latents(2)
            latents(3)
            dve.wait_ge(S["latO_product"], 1)
            V.tensor_copy(latO[:, :, 0:C0], bankY[:].rearrange("p (n c) -> p n c", c=C0)).then_inc(S["latO_ready"], 1)
            dve.wait_ge(S["consts"], 7)

            def body(s, bm, be, bp):
                def take(f):
                    j, i, half = FILLS[f]
                    width = min(CH, (i + 1) * P - half * CH)
                    dve.wait_ge(S["scores_ready"], NF * s + f + 1)
                    V.tensor_reduce(part_max[:, half, j, i:i + 1], bank[f % 2][:, 0:width], AX.X, ALU.max)\
                        .then_inc(S["max_taken"], 1)

                def copy_y(pair, c, g):
                    v = 4 * g + 2 * pair + c
                    dve.wait_ge(S["pv_done"], SUB * g + NTL * pair + (2 if c == 0 else NTL))
                    if not (isinstance(g, int) and v < 2):
                        dve.wait_ge(S["ln_done"], 2 * (v - 1))
                        dve.wait_ge(S["y_moved"], 2 * (v - 1))
                    V.tensor_copy(y_part[:, c, :], bankY[:, :]).then_inc(S["y_copied"], 1)

                def update(c):
                    dve.wait_ge(S["proj_done"], 2 * (s - 2) + c + 1)
                    cs = slice(bp * L + c * CH, bp * L + (c + 1) * CH)
                    V.scalar_tensor_tensor(out=xT[:, cs], in0=bankM[:, :], scalar=mod[:, 0, 2, bp:bp + 1],
                                           in1=xT[:, cs], op0=ALU.mult, op1=ALU.add).then_inc(S["x_updated"], 1)

                for k in range(SUB):
                    fl = fills_of(k) if bm is not None else []
                    for f in fl[:-1]:
                        take(f)
                    if k == 0 and bp is not None:
                        copy_y(1, 1, s - 2)
                    if be is not None:
                        if k == 2:
                            copy_y(0, 0, s - 1)
                        if k == NTL:
                            copy_y(0, 1, s - 1)
                        if k == NTL + 2:
                            copy_y(1, 0, s - 1)
                    for f in fl[-1:]:
                        take(f)
                    if isinstance(s, int) and s == 0:
                        for q in later_q_of(k):
                            queries(*q)
                    if bp is not None and k in (2, 4):
                        update(k // 2 - 1)
                    if bm is not None and k == TURN:
                        dve.wait_ge(S["max_taken"], NF * (s + 1))
                        if not (isinstance(s, int) and s == 0):
                            dve.wait_ge(S["max_turned"], s)
                        V.tensor_tensor(row_max[:].rearrange("p (j i) -> p j i", j=GR), part_max[:, 0],
                                        part_max[:, 1], ALU.max).then_inc(S["row_max_ready"], 1)
                if bp is not None:
                    dve.wait_ge(S["x_updated"], 2 * (s - 1))
            steps(dve, body)

            chain2 = [0]

            def then(ins):
                chain2[0] += 1
                ins.then_inc(W["dchain"], 1)
                dve.wait_ge(W["dchain"], chain2[0])

            def softmax_in(x, k):
                g, n = x.shape[2], x.shape[3]
                m = st[:, k, :, 0:g]
                then(V.tensor_reduce(m, x, AX.X, ALU.max))
                then(V.tensor_tensor(x, x, m.unsqueeze(3).broadcast_to([P, NT, g, n]), ALU.subtract))

            def softmax_out(x, k):
                g, n = x.shape[2], x.shape[3]
                m = st[:, k, :, 0:g]
                then(V.tensor_reduce(m, x, AX.X, ALU.add))
                then(V.reciprocal(m, m))
                then(V.tensor_tensor(x, x, m.unsqueeze(3).broadcast_to([P, NT, g, n]), ALU.mult))

            def top_two(x, w, tiny):
                n = x.shape[2]
                g = gt[:, :, 0:n * n].rearrange("p t (e f) -> p t e f", e=n)
                q = eq[:, :, 0:n * n].rearrange("p t (e f) -> p t e f", e=n)
                other = x.unsqueeze(2).broadcast_to([P, NT, n, n])
                own = x.unsqueeze(3).broadcast_to([P, NT, n, n])
                then(V.tensor_tensor(g, other, own, ALU.is_gt))
                then(V.tensor_tensor(q, other, own, ALU.is_equal))
                then(V.tensor_tensor(q, q, earlier[:, 0:n, 0:n].unsqueeze(1).broadcast_to([P, NT, n, n]), ALU.mult))
                then(V.tensor_tensor(g, g, q, ALU.add))
                r = rank[:, :, 0:n]
                then(V.tensor_reduce(r, g, AX.X, ALU.add))
                then(V.tensor_scalar(r, r, 1.5, None, ALU.is_lt))
                then(V.tensor_tensor(w, x, r, ALU.mult))
                s1 = st[:, 4, :, 0:1]
                then(V.tensor_reduce(s1, w.unsqueeze(2), AX.X, ALU.add))
                then(V.tensor_scalar(s1, s1, tiny, None, ALU.add))
                then(V.reciprocal(s1, s1))
                then(V.tensor_tensor(w, w, s1.broadcast_to([P, NT, n]), ALU.mult))

            norm(1, 0, 3, 4)
            dve.wait_ge(W["logits"], 1)
            l0 = lg[:, :, 0:E0]
            then(V.tensor_tensor(l0, bank[0][:, 0:NT * E0].rearrange("p (t e) -> p t e", e=E0),
                                 rb[:].unsqueeze(1).broadcast_to([P, NT, E0]), ALU.add))
            softmax_in(l0.unsqueeze(2), 0)
            V.tensor_copy(st[:, 5, :, 0:1], st[:, 0, :, 0:1]).then_inc(W["exp_in"], 1)
            dve.wait_ge(W["exp_out"], 1)
            dve.wait_ge(W["pchain"], 14)
            softmax_out(pr[:, :, 0:E0].unsqueeze(2), 1)
            top_two(pr[:, :, 0:E0], wts[:, :, 0:E0], 1e-6)
            dve.wait_ge(W["consts_b"], 1)
            V.tensor_copy(wx[:, :, R0:NR].rearrange("p t (e r) -> p t e r", r=R0),
                          wts[:, :, 0:E0].unsqueeze(3).broadcast_to([P, NT, E0, R0])).then_inc(W["weights_ready"], 1)
            lowb = (bank[1], bankY)
            for c in range(NC):
                dve.wait_ge(W["low_product"], c + 1)
                dve.wait_ge(W["wxT_ready"], c + 1)
                if c >= 2:
                    dve.wait_ge(W["ffn_product"], c - 1)
                V.tensor_tensor(lowr[:, c % 2, :], lowb[c % 2][0:NR, :], wxT[:, c * CH:(c + 1) * CH], ALU.mult)\
                    .then_inc(W["low_ready"], 1)
                if c >= 1:
                    add_ffn(dve, V, c - 1)
            add_ffn(dve, V, NC - 1)
            then(V.tensor_scalar(bq_s[:], bqkv[:, 0:1], HD1 ** -0.5, None, ALU.mult))
            V.tensor_scalar(ga2[:], mod[:, 1, 2, :], 2.0, None, ALU.mult).then_inc(W["prep"], 1)

            norm(2, 1, 0, 1, shifted=True)

            dve.wait_ge(W["bias_product"], 1)
            V.tensor_tensor(ob_v[:], bank[0][:, 2 * P:2 * P + 1], ob[:], ALU.add).then_inc(W["prep"], 1)

            def window(j, stage):
                if stage(5):
                    i, q = stage(5)
                    dve.wait_ge(W["o_product"], i + 1)
                    o = (bankY, bankM)[q]
                    V.reciprocal(inv_w[:, q, :], o[:, P:2 * P]).then_inc(W["inv_ready"], 1)
                    dve.wait_ge(W["inv_ready"], i + 1)
                    V.tensor_tensor(oT[:, bass.ds(i * P, P)], o[:, 0:P], inv_w[:, q, :], ALU.mult)\
                        .then_inc(W["o_ready"], 1)
                if stage(1):
                    i, q = stage(1)
                    s4 = quad[q].rearrange("p (h k) -> p h k", h=NH)
                    dve.wait_ge(W["s_product"], i + 1)
                    V.tensor_reduce(mx[:, q, :], s4, AX.X, ALU.max).then_inc(W["max_ready"], 1)
                    dve.wait_ge(W["max_ready"], i + 1)
                    need(dve, W["exp_ready"], i - 1)
                    V.tensor_tensor(sub[:, q], s4, mx[:, q, :].unsqueeze(2).broadcast_to([P, NH, WIN]),
                                    ALU.subtract).then_inc(W["sub_ready"], 1)
            windows(dve, window)
            for c in range(NC):
                dve.wait_ge(W["att_ready"], c + 1)
                b = c // 2
                for to, at, m in shifted_pieces_back(c):
                    V.scalar_tensor_tensor(out=xT[:, to:to + m], in0=ffn[:, c % 2, at:at + m],
                                           scalar=ga2[:, b:b + 1], in1=xT[:, to:to + m], op0=ALU.mult,
                                           op1=ALU.add).then_inc(W["x_att"], 1)

            norm(3, 1, 3, 4)
            for n, (dst, src) in enumerate(((w1h, w1), (w2h, w2))):
                dve.wait_ge(W["w_hi"], n + 1)
                V.scalar_tensor_tensor(out=dst[:, 1, :], in0=src[:], scalar=UP, in1=dst[:, 0, :],
                                       op0=ALU.mult, op1=ALU.subtract).then_inc(W["w_lo"], 1)
            for k in range(2):
                for c in range(NC):
                    cs = slice(c * CH, (c + 1) * CH)
                    dve.wait_ge(N["rstd"], norm_count(4 + k, "rstd", c + 1))
                    V.scalar_tensor_tensor(out=xc[:, cs], in0=z[:, cs], scalar=nw[:], in1=rstd[:, cs],
                                           op0=ALU.mult, op1=ALU.mult).then_inc(E["xn"], 1)
                for c in range(NC):
                    cs = slice(c * CH, (c + 1) * CH)
                    dve.wait_ge(E["xn_hi"], loop_count(k, "xn_hi", c + 1))
                    V.tensor_tensor(xnh[:, 1, cs], xc[:, cs], xnh[:, 0, cs], ALU.subtract).then_inc(E["xn_lo"], 1)
                dve.wait_ge(E["logits"], loop_count(k, "logits", 1))
                then(V.tensor_copy(lg[:], bank[0][:, 0:NT * 12].rearrange("p (t e) -> p t e", e=12)))
                softmax_in(lg[:, :, 0:NGR].unsqueeze(2), 0)
                softmax_in(lg[:, :, NGR:12].rearrange("p t (g e) -> p t g e", e=2), 1)
                V.tensor_copy(st[:, 5, :, 0:1], st[:, 0, :, 0:1]).then_inc(E["exp_in"], 1)
                dve.wait_ge(E["exp_out"], loop_count(k, "exp_out", 1))
                macro = pr[:, :, 0:NGR]
                micro = pr[:, :, NGR:12].rearrange("p t (g e) -> p t g e", e=2)
                softmax_out(macro.unsqueeze(2), 0)
                softmax_out(micro, 1)
                wg = rank[:, :, 0:NGR]
                top_two(macro, macro, 1e-9)
                best = st[:, 2]
                then(V.tensor_reduce(best, micro, AX.X, ALU.max))
                then(V.tensor_scalar(st[:, 3], best, 1e-9, None, ALU.add))
                then(V.reciprocal(st[:, 3], st[:, 3]))
                then(V.tensor_tensor(best, best, st[:, 3], ALU.mult))
                then(V.tensor_tensor(best, best, macro, ALU.mult))
                then(V.tensor_tensor(st[:, 3], micro[:, :, :, 0], micro[:, :, :, 1], ALU.is_ge))
                w4 = wts[:].rearrange("p t (g e) -> p t g e", e=2)
                then(V.tensor_tensor(w4[:, :, :, 0], best, st[:, 3], ALU.mult))
                V.tensor_tensor(w4[:, :, :, 1], best, w4[:, :, :, 0], ALU.subtract).then_inc(E["weights_ready"], 1)
                for c in range(NC):
                    cs = slice(c * CH, (c + 1) * CH)
                    dve.wait_ge(E["c_hi"], loop_count(k, "c_hi", c + 1))
                    if c == 0:
                        dve.wait_ge(W["consts_b"], 2)
                    V.tensor_tensor(cT16[96:104, cs], quad[c][0:E1, :], cT16[0:E1, cs], ALU.subtract)\
                        .then_inc(E["c_lo"], 1)

                def ahead(c, e):
                    u = E1 * c + e
                    dve.wait_ge(E["act"], loop_count(k, "act", u + 1))
                    need(dve, E["y"], loop_count(k, "y", u - 1))
                    V.tensor_copy(hidh[:, e % 2, 0, :], hid[:, e % 2, :]).then_inc(E["hid_hi"], 1)
                    dve.wait_ge(E["hid_hi"], loop_count(k, "hid_hi", u + 1))
                    V.tensor_tensor(hidh[:, e % 2, 1, :], hid[:, e % 2, :], hidh[:, e % 2, 0, :], ALU.subtract)\
                        .then_inc(E["hid_lo"], 1)

                def unit(c, e):
                    u = E1 * c + e
                    dve.wait_ge(E["y"], loop_count(k, "y", u + 1))
                    dve.wait_ge(E["cw"], loop_count(k, "cw", u + 1))
                    need(dve, E["z"], loop_count(k, "z", u - 1))
                    V.tensor_tensor(yw[:, e % 2, :], bank[e % 2][:], cw[:, e % 2, :], ALU.mult).then_inc(E["yw"], 1)
                experts(dve, ahead, unit)
            dve.wait_ge(E["z"], loop_count(1, "z", NC * E1))
            for c in range(NC):
                cs = slice(c * CH, (c + 1) * CH)
                V.scalar_tensor_tensor(out=xT[:, cs], in0=z[:, cs], scalar=mod[:, 1, 5, c // 2:c // 2 + 1],
                                       in1=xT[:, cs], op0=ALU.mult, op1=ALU.add).then_inc(x_final, 1)
            for c in range(NC):
                dve.wait_ge(S["out_turned"], c + 1)
                V.tensor_copy(x_rows[:, 4 * c:4 * c + 4, :].rearrange("p n d -> p (n d)"), quad[c])\
                    .then_inc(S["out_rows"], 1)


def kernel(**inputs):
    import concourse.bacc as _bacc
    from concourse.bass_utils import run_bass_kernel_spmd as _run

    v = {k: np.asarray(x) for k, x in inputs.items()}
    lay = {
        "x": v["L0_attn_x_bld"],
        "c0T": v["L0_c"].T, "c1T": v["L1_c"].T, "wmod0": v["L0_wmod"], "wmod1": v["L1_wmod"],
        "wqT": v["L0_attn_Wq"].transpose(2, 1, 0), "wkT": v["L0_attn_Wk_up"].transpose(2, 1, 0),
        "wvT": v["L0_attn_Wv_up"].transpose(2, 1, 0), "wo": v["L0_attn_Wout"].transpose(1, 0, 2),
        "wkv": v["L0_attn_Wkv_down"],
        "bwT": v["L0_ffn_base_W"].T, "bb": v["L0_ffn_base_b"][:, None],
        "downT": np.concatenate([v["L0_ffn_shared_A"][None], v["L0_ffn_routed_A"]]).reshape(-1, D).T,
        "up": np.concatenate([v["L0_ffn_shared_B"][None], v["L0_ffn_routed_B"]]).transpose(0, 2, 1).reshape(-1, D),
        "rw": v["L0_ffn_router_W"].T, "rb": v["L0_ffn_router_b"],
        "wqkv": v["L1_attn_in_proj_w"].T, "bqkv": v["L1_attn_in_proj_b"].reshape(3, D).T,
        "owT": v["L1_attn_out_w"].T, "ob": v["L1_attn_out_b"][:, None],
        "nw": v["L1_ffn_norm_w"][:, None],
        "wrT": np.concatenate([v["L1_ffn_w_macro"], v["L1_ffn_w_micro"].reshape(E1, D)]).T,
        "w1": v["L1_ffn_w1"].transpose(2, 0, 1).reshape(D, E1 * F1),
        "w2": v["L1_ffn_w2"].reshape(E1, D, F1 // P, P).transpose(3, 0, 2, 1).reshape(P, E1 * F1),
    }
    nc = _bacc.Bacc("TRN2", target_bir_lowering=False, num_devices=1)
    arrays, args = {}, {}
    for name, x in lay.items():
        x = np.ascontiguousarray(x)
        arrays[f"in_{name}"] = x
        args[name] = nc.dram_tensor(f"in_{name}", x.shape, mybir.dt.from_np(x.dtype), kind="ExternalInput").ap()
    out = nc.dram_tensor("out", (B, L, D), F32, kind="ExternalOutput").ap()
    program(nc, args, out)
    r = _run(nc, [arrays], core_ids=[0])
    return r.results[0]["out"]
```

```python
from contextlib import ExitStack

import numpy as np

import concourse.bass as bass
from concourse import mybir

F32 = mybir.dt.float32
F16 = mybir.dt.float16
BF16 = mybir.dt.bfloat16
ALU = mybir.AluOpType
ACT = mybir.ActivationFunctionType
AX = mybir.AxisListType

P = 128
B, L, D = 2, 1024, 128
T = B * L
NT = T // P
CH = 512
NC = T // CH
H0, C0, HD0 = 16, 32, 64
GR = 4
NG = B * H0 // GR
QB = L // P
NH, HD1, WIN, SHIFT = 8, 16, 64, 32
NGR, E1, F1 = 4, 8, 256
UP = 64.0
NEG = -1e30
LN_EPS = 1e-5

TILES = [
    (0, [(0, 0, 0), (1, 128, 512)]),
    (0, [(2, 256, 0), (3, 384, 256)]),
    (1, [(0, 0, 0), (1, 0, 512)]),
    (1, [(2, 0, 0), (3, 0, 512)]),
    (1, [(4, 0, 0), (5, 128, 512)]),
    (1, [(6, 256, 0), (7, 384, 256)]),
]
NTL = len(TILES)
MASKED = {0: 0, 1: 1, 4: 2, 5: 3}
SUB = 2 * NTL
CHUNK_END = {1: 0, 5: 1}
FILLS = [(j, i, h) for j in range(GR) for i in range(QB) for h in range(1 + (i >= 4))]
NF = len(FILLS)
NFH = NF // GR
SHARE = [3, 4, 3, 5, 5, 4, 4, 3, 4, 4, 5, 4]
assert sum(SHARE) == NF and sum(SHARE[:NTL]) == NF // 2 and len(SHARE) == SUB
TURN_AT = (NTL, 1)
Q_LOTS = [(0, 1), (1, 2), (2, GR), (GR, NG)]
FFN_NORMS = [(n, c) for ns, h in (((3, 4), 0), ((3, 4), 1), ((5,), 0), ((5,), 1)) for n in ns
             for c in (2 * h, 2 * h + 1)]
UNITS = 2 * NC * E1
HALF = 2 * E1
AHEAD = 3
OUT_AT = [UNITS - 14, UNITS - 12, UNITS - 6]
ROUTE_AT = [5, 6, 8, 9, 10]
LAST_STAGE = 5
LATER_Q = [(n // 2, n % 2) for n in range(2, 2 * NG)]


def fills_of(k):
    return list(range(sum(SHARE[:k]), sum(SHARE[:k + 1])))


def later_q_of(k):
    return LATER_Q[2 * k:2 * k + 2]


def program(nc, a, out):
    with ExitStack() as ctx:
        def sb(name, shape, dt=F32):
            return ctx.enter_context(nc.sbuf_tensor(name, shape, dt))

        def sem(name):
            return ctx.enter_context(nc.semaphore(name))

        bank = [ctx.enter_context(nc.psum_tensor(f"bank{i}", [P, CH], F32)) for i in range(2)]
        stT = ctx.enter_context(nc.psum_tensor("stT", [P, 2, 2 * CH], F32))
        bankY = ctx.enter_context(nc.psum_tensor("bankY", [P, CH], F32))
        bankM = ctx.enter_context(nc.psum_tensor("bankM", [P, CH], F32))
        quad = [stT[:, i // 2, (i % 2) * CH:(i % 2 + 1) * CH] for i in range(4)]

        identf = sb("identf", [P, P])
        identb = sb("identb", [P, P], BF16)
        maskb = sb("maskb", [P, P], BF16)
        mean_w = sb("mean_w", [P, P])
        epsc = sb("epsc", [P, 2])
        x_rows = sb("x_rows", [P, NT, P])
        xT = sb("xT", [P, T])
        xc = sb("xc", [P, T])
        sq = sb("sq", [P, T])
        rstd = sb("rstd", [P, T])
        hT = sb("hT", [P, T])
        cT = sb("cT", [P, 2, B])
        csil = sb("csil", [P, 3, 2 * B])
        wmod = sb("wmod", [P, 2, 6 * D])
        mod = sb("mod", [P, 2, 6, B])
        sgn = sb("sgn", [P, 2, 2, B])
        E0, R0 = 6, 16
        NR = R0 * (E0 + 1)
        bwT = sb("bwT", [P, D])
        downT = sb("downT", [P, NR])
        up = sb("up", [NR, D])
        rw = sb("rw", [P, E0])
        rb = sb("rb", [P, E0])
        bb = sb("bb", [P, 1])
        earlier = sb("earlier", [P, E0, E0])
        wqkv = sb("wqkv", [P, 3 * D])
        bqkv = sb("bqkv", [P, 3])
        owT = sb("owT", [P, D])
        ob = sb("ob", [P, 1])
        head_of = sb("head_of", [P, NH])
        wv_eo = sb("wv_eo", [P, 2, NH // 2, 2 * HD1])
        bq_s = sb("bq_s", [P, 1])
        ga2 = sb("ga2", [P, B])
        ob_v = sb("ob_v", [P, 1])
        ones_eo = sb("ones_eo", [P, 2 * HD1])
        nw = sb("nw", [P, 1])
        wrT = sb("wrT", [P, NGR + E1])
        spread = sb("spread", [104, E1, P], F16)

        attn = ExitStack()

        def sa(name, shape, dt=F32):
            return attn.enter_context(nc.sbuf_tensor(name, shape, dt))

        wqT = sa("wqT", [HD0, H0, D])
        wkT = sa("wkT", [HD0, H0, C0])
        wvT = sa("wvT", [HD0, H0, C0])
        wo = sa("wo", [HD0, H0, D])
        wkv = sa("wkv", [P, 3, C0])
        qk = sa("qk", [P, H0 * C0])
        vo = sa("vo", [P, H0 // GR, D])
        vo_now = sa("vo_now", [P, D])
        lat = sa("lat", [97, T], F16)
        latO = sa("latO", [P, NT, 2 * C0])
        q_hi0 = sa("q_hi0", [P, NG // 2, L], F16)
        q_lo0 = sa("q_lo0", [P, NG // 2, L], F16)
        q_hi = [q_hi0[:], xc[:].bitcast(F16).rearrange("p (g t) -> p g t", t=L)]
        q_lo = [q_lo0[:], sq[:].bitcast(F16).rearrange("p (g t) -> p g t", t=L)]
        q_st = sa("q_st", [97, B * H0, L], F16)
        probs = sa("probs", [P, 2, 2, 2 * CH])
        part_max = sa("part_max", [P, 2, GR, QB])
        row_max = sa("row_max", [P, GR * QB])
        neg_max = sa("neg_max", [2 * QB, 2, P], F16)
        y_raw = x_rows[:, 0:NT // 2, :].rearrange("p (c n) d -> p c (n d)", c=2)
        ln_sum = x_rows[:, NT // 2:NT, :].rearrange("p (c n) d -> p c (n d)", c=2)
        y_part = rstd[:, 0:2 * CH].rearrange("p (v t) -> p v t", v=2)
        q_stage = [probs[:, r, 0, 0:CH] for r in range(2)]
        inv_sum = sa("inv_sum", [P, 2, CH])
        y_n = sa("y_n", [P, 2, CH])

        attn.close()

        lg = sb("lg", [P, NT, 12])
        pr = sb("pr", [P, NT, 12])
        st = sb("st", [P, 6, NT, 4])
        gt = sb("gt", [P, NT, 36])
        eq = sb("eq", [P, NT, 36])
        rank = sb("rank", [P, NT, 6])
        wts = sb("wts", [P, NT, 8])
        wx = sb("wx", [P, NT, NR])
        wxT = sb("wxT", [NR, T])
        lowr = sb("lowr", [NR, 2, CH])
        ffn = sb("ffn", [P, 2, CH])
        hwin = sb("hwin", [P, 2, P])
        qw = sb("qw", [P, 2, P])
        kx = sb("kx", [P, 2, 2, NH, WIN])
        vw = sb("vw", [P, 2, 2, P])
        mx = sb("mx", [P, 2, NH])
        sub = sb("sub", [P, 2, NH, WIN])
        pw = sb("pw", [P, 2, NH, WIN])
        pT = sb("pT", [P, 2, NH // 2 * P])
        inv_w = sb("inv_w", [P, 2, P])
        w1 = sb("w1", [P, E1 * F1])
        w2 = sb("w2", [P, E1 * F1])
        w1h = sb("w1h", [P, 2, E1 * F1], F16)
        w2h = sb("w2h", [P, 2, E1 * F1], F16)
        xnh = sb("xnh", [P, 2, T], F16)
        cT16 = sb("cT16", [104, T], F16)
        hid = sb("hid", [P, AHEAD, 2 * CH])
        hidh = sb("hidh", [P, AHEAD, 2, 2 * CH], F16)
        cw = sb("cw", [P, AHEAD, CH])

        S = {n: sem(n) for n in (
            "c_loaded", "w_attn_loaded", "ident_step", "consts", "csil_step", "silu_ready", "mod_product",
            "gate_step", "x_turned", "xT_ready", "qk_product", "qk_ready", "vo_product", "vo_ready", "lat_product",
            "lat_hi", "lat_ready", "latO_product", "latO_ready", "q_product", "q_hi_ready", "q_lo_ready", "q_staged", "q_lo_later",
            "scores_ready", "max_taken", "row_max_ready", "max_turned", "neg_max_ready",
            "st_ready", "exp_done", "masked", "pv_done", "ln_done", "y_copied", "y_moved", "inv_ready", "y_n_ready",
            "vo_now_ready", "pool_passed", "proj_done", "x_updated", "out_turned", "out_rows", "stored")}
        x_loaded = [sem(f"x_loaded{c}") for c in range(NC)]
        max_placed = [sem(f"max_placed{pair}") for pair in range(2)]
        q_first = [sem(f"q_first{j}") for j in range(GR)]
        q_placed = [sem(f"q_placed{i}") for i in range(len(Q_LOTS))]
        N = {n: sem("n_" + n) for n in ("mean", "centred", "squared", "var", "ln", "rstd", "scaled", "h")}

        W = {n: sem("w_" + n) for n in (
            "small_loaded", "w12_loaded", "consts_b", "logits", "exp_in", "exp_out", "weights_ready",
            "wx_turned", "wxT_ready", "low_product", "low_ready", "ffn_product", "ffn_ready", "x_ffn",
            "prep", "bias_product", "k_product", "k_biased", "hwin_ready", "q_product", "v_product", "q_ready", "k_ready",
            "v_ready", "s_product", "max_ready",
            "sub_ready", "exp_ready", "p_turned", "pT_ready", "o_product", "inv_ready",
            "o_ready", "att_product", "att_ready", "x_att",
            "w_hi", "w_lo", "dchain", "pchain")}
        E = {n: sem("e_" + n) for n in (
            "xn", "xn_hi", "xn_lo", "logits", "exp_in", "exp_out", "weights_ready", "cw_turned", "c_hi", "c_lo", "pre", "act",
            "hid_w", "hid_hi", "hid_lo", "y", "cb", "cw", "z")}
        x_final = sem("x_final")

        x_dram = a["x"].rearrange("b (n p) d -> p (b n) d", p=P)
        out_dram = out.rearrange("b (n p) d -> p (b n) d", p=P)

        block = ctx.enter_context(nc.Block())

        def steps(eng, body):
            body(0, 0, None, None)
            body(1, 0, 0, None)
            with eng.Fori(2, 4) as s:
                body(s, 0, 0, 0)
            body(4, 1, 0, 0)
            body(5, 1, 1, 0)
            with eng.Fori(6, 8) as s:
                body(s, 1, 1, 1)
            body(8, None, 1, 1)
            body(9, None, None, 1)

        def norm_count(k, name, v):
            if k >= 3 and name in ("squared", "var", "ln", "rstd"):
                return NC * 3 + FFN_NORMS.index((k, v - 1)) + 1
            return NC * k + (2 if name == "h" and k == 3 else 0) + v

        def next_half(u):
            g = u // HALF + 1
            return (g // 2, g % 2, u % HALF) if 0 <= u and g < 4 else (0, 0, -1)

        def need(eng, s, v):
            if not isinstance(v, int) or v > 0:
                eng.wait_ge(s, v)

        def windows(eng, body):
            def slot(j):
                body(j, lambda d: (j - d, (j - d) % 2) if 0 <= j - d < NT else None)
            for j in range(6):
                slot(j)
            with eng.Fori(3, NT // 2) as n:
                for p in range(2):
                    body(2 * n + p, lambda d: (2 * n + p - d, (p + d) % 2))
            for j in range(NT, NT + LAST_STAGE):
                slot(j)

        def shifted_pieces(c):
            b, at = c // 2, (c % 2) * CH
            if at == 0:
                return [((b + 1) * L - SHIFT, b * L, SHIFT), (b * L, b * L + SHIFT, CH - SHIFT)]
            return [(b * L + at - SHIFT, b * L + at, CH)]

        h2_count = sum(len(shifted_pieces(c)) for c in range(NC))
        kT = sq
        oT = rstd
        z = hT

        @block.sync
        def _(sp):
            for c in range(NC):
                sp.dma_start(x_rows[:, 4 * c:4 * c + 4, :], x_dram[:, 4 * c:4 * c + 4, :]).then_inc(x_loaded[c], 16)
                if c == 0:
                    sp.dma_start(cT[:, 0, :], a["c0T"]).then_inc(S["c_loaded"], 16)
                    sp.dma_start(cT[:, 1, :], a["c1T"]).then_inc(S["c_loaded"], 16)
                if c == 1:
                    sp.dma_start(wmod[:, 0, :], a["wmod0"]).then_inc(S["c_loaded"], 16)
                    sp.dma_start(wmod[:, 1, :], a["wmod1"]).then_inc(S["c_loaded"], 16)
            sp.dma_start(wqT[:], a["wqT"]).then_inc(S["w_attn_loaded"], 16)
            sp.dma_start(wkT[:], a["wkT"]).then_inc(S["w_attn_loaded"], 16)
            sp.dma_start(wvT[:], a["wvT"]).then_inc(S["w_attn_loaded"], 16)
            sp.dma_start(wo[:], a["wo"]).then_inc(S["w_attn_loaded"], 16)
            for r in range(3):
                sp.dma_start(wkv[:, r, :], a["wkv"]).then_inc(S["w_attn_loaded"], 16)
            for dst, name in ((bwT, "bwT"), (downT, "downT"), (up, "up"), (rw, "rw"), (bb, "bb"), (wqkv, "wqkv"),
                              (bqkv, "bqkv"), (owT, "owT"), (ob, "ob"), (nw, "nw"), (wrT, "wrT")):
                sp.dma_start(dst[:], a[name]).then_inc(W["small_loaded"], 16)
            sp.dma_start(rb[:], a["rb"].partition_broadcast(P)).then_inc(W["small_loaded"], 16)
            for lot, (g0, g1) in enumerate(Q_LOTS):
                sp.wait_ge(S["q_hi_ready"], 2 * g1)
                sp.wait_ge(*((S["q_lo_later"], 2 * g1 - 2) if lot else (S["q_lo_ready"], 2)))
                bq, g2, g3 = g0 // GR, g0 % GR, g0 % GR + g1 - g0
                for j in range(GR):
                    for row, src in ((0, q_hi), (C0, q_lo), (2 * C0, q_hi)):
                        sp.dma_start(q_st[row:row + C0, GR * g0 + j:GR * g1:GR, :],
                                     src[bq][C0 * j:C0 * j + C0, g2:g3, :])\
                            .then_inc(q_placed[lot] if lot else q_first[j], 16)

            def body(s, bm, be, bp):
                for pair, g, there in ((1, s - 1, be), (0, s, bm)):
                    if there is not None:
                        sp.wait_ge(S["neg_max_ready"], 2 * g + pair + 1)
                        sp.dma_start(q_st[96:97, bass.ds(GR * g + 2 * pair, 2), :].rearrange("o j (i t) -> o (j i) t", t=P),
                                     neg_max[:, pair, :]).then_inc(max_placed[pair], 16)
            steps(sp, body)
            sp.wait_ge(S["x_updated"], 2 * NG)
            sp.dma_start(w1[:], a["w1"]).then_inc(W["w12_loaded"], 16)
            sp.dma_start(w2[:], a["w2"]).then_inc(W["w12_loaded"], 16)
            for c in range(NC):
                sp.wait_ge(S["out_rows"], c + 1)
                sp.dma_start(out_dram[:, 4 * c:4 * c + 4, :], x_rows[:, 4 * c:4 * c + 4, :]).then_inc(S["stored"], 16)
            sp.wait_ge(S["stored"], 16 * NC)

        @block.gpsimd
        def _(pool):
            pool.memset(identf[:], 0.0).then_inc(S["ident_step"], 1)
            pool.wait_ge(S["ident_step"], 1)
            pool.affine_select(out=identf[:], in_=identf[:], compare_op=ALU.not_equal, fill=1.0, base=0,
                               pattern=[[-1, P]], channel_multiplier=1).then_inc(S["ident_step"], 1)
            pool.memset(mean_w[:], 1.0 / D).then_inc(S["ident_step"], 1)
            pool.memset(epsc[:, 0:1], LN_EPS).then_inc(S["ident_step"], 1)
            pool.memset(epsc[:, 1:2], 1e-6).then_inc(S["ident_step"], 1)
            pool.memset(maskb[:], 0.0).then_inc(S["consts"], 1)
            pool.memset(identb[:], 0.0).then_inc(S["consts"], 1)
            pool.wait_ge(S["consts"], 2)
            pool.affine_select(out=identb[:], in_=identb[:], compare_op=ALU.not_equal, fill=1.0, base=0,
                               pattern=[[-1, P]], channel_multiplier=1).then_inc(S["consts"], 1)
            pool.affine_select(out=maskb[:], in_=maskb[:], compare_op=ALU.is_ge, fill=NEG, base=0,
                               pattern=[[-1, P]], channel_multiplier=1).then_inc(S["consts"], 1)
            pool.wait_ge(S["consts"], 4)
            pool.memset(lat[96:97, :], 1.0).then_inc(S["consts"], 1)
            pool.wait_ge(S["consts"], 5)
            pool.memset(latO[:, :, C0:2 * C0], 1.0).then_inc(S["consts"], 1)
            pool.memset(part_max[:], -3e38).then_inc(S["consts"], 1)
            pool.memset(earlier[:], 1.0).then_inc(W["pchain"], 1)
            pool.memset(head_of[:], 1.0).then_inc(W["pchain"], 1)
            pool.memset(spread[:], 0.0).then_inc(W["pchain"], 1)
            pool.memset(wv_eo[:], 0.0).then_inc(W["pchain"], 1)
            pool.memset(ones_eo[:], 1.0).then_inc(W["pchain"], 1)
            pool.wait_ge(W["pchain"], 5)
            pool.affine_select(out=earlier[:], in_=earlier[:], compare_op=ALU.is_ge, fill=0.0, base=-1,
                               pattern=[[1, E0], [-1, E0]], channel_multiplier=0).then_inc(W["pchain"], 1)
            pool.affine_select(out=head_of[:], in_=head_of[:], compare_op=ALU.is_ge, fill=0.0, base=0,
                               pattern=[[-HD1, NH]], channel_multiplier=1).then_inc(W["pchain"], 1)
            pool.affine_select(out=spread[:], in_=spread[:], compare_op=ALU.not_equal, fill=1.0, base=0,
                               pattern=[[-1, E1], [0, P]], channel_multiplier=1).then_inc(W["pchain"], 1)
            pool.affine_select(out=ones_eo[:], in_=ones_eo[:], compare_op=ALU.is_ge, fill=0.0, base=0,
                               pattern=[[-WIN, 2], [0, HD1]], channel_multiplier=1).then_inc(W["pchain"], 1)
            pool.wait_ge(W["pchain"], 9)
            pool.affine_select(out=head_of[:], in_=head_of[:], compare_op=ALU.is_ge, fill=0.0, base=HD1 - 1,
                               pattern=[[HD1, NH]], channel_multiplier=-1).then_inc(W["pchain"], 1)
            pool.affine_select(out=spread[:], in_=spread[:], compare_op=ALU.not_equal, fill=1.0, base=-96,
                               pattern=[[-1, E1], [0, P]], channel_multiplier=1).then_inc(W["pchain"], 1)
            pool.affine_select(out=ones_eo[:], in_=ones_eo[:], compare_op=ALU.is_ge, fill=0.0, base=WIN - 1,
                               pattern=[[WIN, 2], [0, HD1]], channel_multiplier=-1).then_inc(W["pchain"], 1)
            pool.wait_ge(W["small_loaded"], 16 * 12)
            wv = wqkv[:, 2 * D:3 * D].rearrange("p (n e k) -> p n e k", e=2, k=HD1)
            for e in range(2):
                pool.tensor_copy(wv_eo[:, e, :, e * HD1:(e + 1) * HD1], wv[:, :, e, :]).then_inc(W["pchain"], 1)

            def body(s, bm, be, bp):
                if bp is not None:
                    pool.tensor_copy(vo_now[:], vo[:, bass.ds(s - 2 - GR * bp, 1), :].rearrange("p o d -> p (o d)"))\
                        .then_inc(S["vo_now_ready"], 1)
                def normalise(c, g):
                    pool.wait_ge(S["inv_ready"], 2 * g + c + 1)
                    pool.wait_ge(S["y_moved"], 4 * g + 3 + c)
                    if not (isinstance(g, int) and g == 0):
                        pool.wait_ge(S["proj_done"], 2 * (g - 1) + c + 1)
                    pool.tensor_tensor(y_n[:, c, :], y_raw[:, c, :], inv_sum[:, c, :], ALU.mult)\
                        .then_inc(S["y_n_ready"], 1)

                for k in range(SUB):
                    if isinstance(s, int) and s == 0:
                        for g, c in later_q_of(k):
                            n, cs = 2 * g + c, slice(c * CH, (c + 1) * CH)
                            pool.wait_ge(S["q_staged"], n - 1)
                            pool.tensor_tensor(q_lo[g // GR][:, g % GR, cs], q_stage[n % 2],
                                               q_hi[g // GR][:, g % GR, cs], ALU.subtract)\
                                .then_inc(S["q_lo_later"], 1)
                    t = k % NTL
                    if be is not None and t in MASKED:
                        n = SUB * (s - 1) + k
                        second = TILES[t][1][1][2]
                        for x in range(2):
                            pool.wait_ge(S["exp_done"], 2 * n + x + 1)
                            pool.sem_inc(S["pool_passed"], 1)
                            tri = probs[:, k % 2, x, 0:2 * second].rearrange("p (u q) -> p u q", u=2)[:, :, 0:P]
                            pool.affine_select(out=tri, in_=tri, compare_op=ALU.is_ge, fill=0.0, base=0,
                                               pattern=[[0, 2], [1, P]], channel_multiplier=-1)\
                                .then_inc(S["masked"], 1)
                    if k == 0 and bp is not None:
                        normalise(1, s - 2)
                    if be is not None and k == NTL + 3:
                        normalise(0, s - 1)
                if bp is not None:
                    pool.wait_ge(S["proj_done"], 2 * (s - 1))
            steps(pool, body)

            pool.wait_ge(S["x_updated"], 2 * NG)
            pool.memset(wx[:, :, 0:R0], 1.0).then_inc(W["consts_b"], 1)
            pool.memset(cT16[0:96, :], 0.0).then_inc(W["consts_b"], 1)

            pool.wait_ge(N["h"], norm_count(2, "h", h2_count))
            pool.wait_ge(W["k_biased"], NC)

            def window(j, stage):
                if stage(2):
                    i, q = stage(2)
                    need(pool, W["v_product"], i - 1)
                    pool.sem_inc(S["pool_passed"], 1)
                    pool.tensor_copy(hwin[:, q, :], hT[:, bass.ds(i * P, P)]).then_inc(W["hwin_ready"], 1)
                if stage(0):
                    i, q = stage(0)
                    need(pool, W["s_product"], i - 1)
                    pool.sem_inc(S["pool_passed"], 1)
                    shape = [P, NH, WIN]
                    for w in range(2):
                        pool.tensor_tensor(kx[:, q, w],
                                           kT[:, bass.ds(i * P + w * WIN, WIN)].unsqueeze(1).broadcast_to(shape),
                                           head_of[:].unsqueeze(2).broadcast_to(shape), ALU.mult)\
                            .then_inc(W["k_ready"], 1)
            windows(pool, window)

            for u in range(UNITS):
                pool.wait_ge(E["act"], u + 1)
                pool.wait_ge(E["cw"], u + 1)
                h2 = hid[:, u % AHEAD, :].rearrange("p (f t) -> p f t", f=2)
                pool.tensor_tensor(h2, h2, cw[:, u % AHEAD, :].unsqueeze(1).broadcast_to([P, 2, CH]), ALU.mult)\
                    .then_inc(E["hid_w"], 1)

        @block.tensor
        def _(pe):
            mm = pe.matmul

            pe.wait_ge(S["ident_step"], 5)
            for c in range(NC):
                pe.wait_ge(x_loaded[c], 16)
                for i in range(4):
                    m = pe.transpose(quad[c][:, i * P:(i + 1) * P], x_rows[:, 4 * c + i, :], identf[:])
                m.then_inc(S["x_turned"], 1)
            pe.wait_ge(S["c_loaded"], 64)
            pe.wait_ge(S["silu_ready"], 1)
            for l in range(2):
                for j in range(6):
                    m = mm(bankM[:, (6 * l + j) * B:(6 * l + j + 1) * B], wmod[:, l, j * D:(j + 1) * D],
                           csil[:, 2, l * B:l * B + B], start=True, stop=True)
            m.then_inc(S["mod_product"], 1)
            def norm(k, x_ready, centre):

                def mean(c):
                    x_ready(pe, c)
                    if c >= 2:
                        pe.wait_ge(N["centred"], norm_count(k, "centred", c - 1))
                    mm(quad[c % 2], mean_w[:], xT[:, c * CH:(c + 1) * CH], start=True, stop=True)\
                        .then_inc(N["mean"], 1)

                def var(c):
                    pe.wait_ge(N["squared"], norm_count(k, "squared", c + 1))
                    if c >= 2:
                        pe.wait_ge(N["ln"], norm_count(k, "ln", c - 1))
                    mm(quad[2 + c % 2], mean_w[:], sq[:, c * CH:(c + 1) * CH], start=True, stop=True)\
                        .then_inc(N["var"], 1)
                for i in range(NC + 1):
                    if i < NC and centre:
                        mean(i)
                    if i >= 1:
                        var(i - 1)

            norm(0, lambda e, c: e.wait_ge(S["xT_ready"], c + 1), True)
            pe.wait_ge(S["w_attn_loaded"], 16 * 7)
            for h in range(H0):
                m = mm(bank[0][:, h * C0:(h + 1) * C0], wqT[:, h, :], wkT[:, h, :], start=True, stop=True)
            m.then_inc(S["qk_product"], 1)

            pe.wait_ge(S["qk_ready"], 1)

            def latents(c):
                pe.wait_ge(N["h"], norm_count(0, "h", c + 1))
                if c >= 2:
                    pe.wait_ge(S["lat_ready"], c - 1)
                mm(bank[c % 2][0:96, :], wkv[:].rearrange("p r c -> p (r c)"), hT[:, c * CH:(c + 1) * CH],
                   start=True, stop=True).then_inc(S["lat_product"], 1)

            def queries(g, c):
                n = 2 * g + c
                b = g // GR
                if n < 2:
                    pe.wait_ge(N["h"], norm_count(0, "h", c + 1))
                if n in (4, 5):
                    pe.wait_ge(S["q_lo_ready"], n - 3)
                elif n > 5:
                    pe.wait_ge(S["q_staged"], n - 5)
                mm(quad[n % 4], qk[:, (g % GR) * P:(g % GR + 1) * P],
                   hT[:, b * L + c * CH:b * L + (c + 1) * CH], start=True, stop=True).then_inc(S["q_product"], 1)

            pe.wait_ge(N["ln"], norm_count(0, "ln", NC))
            queries(0, 0)
            queries(0, 1)
            for c in range(NC):
                latents(c)
            for i in range(NT):
                m = mm(bankY[:, i * C0:(i + 1) * C0], hT[:, i * P:(i + 1) * P], wkv[:, 0, :], start=True, stop=True)
            m.then_inc(S["latO_product"], 1)
            for g in range(H0 // GR):
                for j in range(GR):
                    h = GR * g + j
                    m = mm(bankM[C0 * j:C0 * j + C0, g * D:(g + 1) * D], wvT[:, h, :], wo[:, h, :],
                           start=True, stop=True)
            m.then_inc(S["vo_product"], 1)

            def body(s, bm, be, bp):
                first = isinstance(s, int) and s == 0

                def fill(f):
                    j, i, half = FILLS[f]
                    n = NF * s + f
                    if first and f < 2:
                        if f == 0:
                            pe.wait_ge(S["lat_ready"], NC)
                            pe.wait_ge(S["consts"], 7)
                    else:
                        pe.wait_ge(S["max_taken"], n - 1)
                    if first and f % NFH == 0:
                        pe.wait_ge(q_first[j], 16 * 3)
                    width = min(CH, (i + 1) * P - half * CH)
                    diag = (i // 4 == half)
                    o = bank[f % 2]
                    m = mm(o[:, 0:width], q_st[0:96, bass.ds(GR * s + j, 1), i * P:(i + 1) * P]
                           .rearrange("p o t -> p (o t)"),
                           lat[0:96, bm * L + half * CH:bm * L + half * CH + width], start=True, stop=not diag)
                    if diag:
                        m = mm(o[:, width - P:width], identb[:], maskb[:], start=False, stop=True)
                    m.then_inc(S["scores_ready"], 1)

                def turn_max(pair, g):
                    pe.wait_ge(S["row_max_ready"], 2 * g + pair + 1)
                    if not (isinstance(g, int) and g == 0 and pair == 0):
                        pe.wait_ge(S["neg_max_ready"], 2 * g + pair)
                    else:
                        pe.wait_ge(S["vo_ready"], 1)
                    if pair == 0 and bp is not None:
                        pe.wait_ge(S["x_updated"], 2 * (s - 1))
                    pe.transpose(bankM[0:2 * QB, 0:P], row_max[:, 2 * QB * pair:2 * QB * (pair + 1)], identf[:])\
                        .then_inc(S["max_turned"], 1)

                def scores_t(k, x):
                    n = SUB * (s - 1) + k
                    c, segs = TILES[k % NTL]
                    if k % NTL == 0 and x == 0:
                        pe.wait_ge(max_placed[k // NTL], 16 * s)
                    if not (isinstance(s, int) and s == 1 and k == 0):
                        pe.wait_ge(S["exp_done"], 2 * n - 1 + x)
                    h = GR * (s - 1) + 2 * (k // NTL) + x
                    for kb, q0, at in segs:
                        m = mm(stT[:, x, at:at + CH - q0], lat[0:97, be * L + kb * P:be * L + (kb + 1) * P],
                               q_st[0:97, bass.ds(h, 1), c * CH + q0:(c + 1) * CH].rearrange("p o t -> p (o t)"),
                               start=True, stop=True)
                    m.then_inc(S["st_ready"], 1)

                def values(k, g, bg, part):
                    n = SUB * g + k
                    c, segs = TILES[k % NTL]
                    t = k % NTL
                    if part == 0:
                        if t in MASKED:
                            pe.wait_ge(S["masked"], 16 * g + 8 * (k // NTL) + 2 * MASKED[t] + 2)
                        else:
                            pe.wait_ge(S["exp_done"], 2 * n + 2)
                        if segs[0][0] == 0 and not (isinstance(g, int) and g == 0 and k == 0):
                            v = 4 * g + 2 * (k // NTL) + c
                            pe.wait_ge(S["y_copied"], v)
                    kb, q0, at = segs[part]
                    for o, rows in ((0, 2 * C0 * (k // NTL)), (C0, 2 * C0 * (1 - k // NTL))):
                        for x in range(2):
                            r = rows + C0 * x
                            m = mm(bankY[r:r + C0, q0:CH], latO[:, bg * QB + kb, o:o + C0],
                                   probs[:, k % 2, x, at:at + CH - q0], start=(kb == 0), stop=(kb == 4 * c + 3))
                    if part == 1:
                        m.then_inc(S["pv_done"], 1)

                def project(c):
                    pe.wait_ge(S["y_n_ready"], 2 * (s - 2) + c + 1)
                    if c == 0:
                        pe.wait_ge(S["vo_now_ready"], s - 1)
                        if be is not None:
                            pe.wait_ge(S["neg_max_ready"], 2 * s)
                    else:
                        pe.wait_ge(S["x_updated"], 2 * (s - 2) + 1)
                    mm(bankM[:, :], vo_now[:], y_n[:, c, :], start=True, stop=True).then_inc(S["proj_done"], 1)

                if bm is not None:
                    lots = {1: [1], 4: [3]}.get(s, []) if isinstance(s, int) else [2] if bm == 0 else []
                    for i in lots:
                        pe.wait_ge(q_placed[i], 16 * 3 * GR)
                if be is not None and isinstance(s, int) and s == 1:
                    pe.wait_ge(S["q_staged"], 2 * NG - 2)
                    pe.wait_ge(S["latO_ready"], 1)
                for k in range(SUB if bm is not None or be is not None else 5):
                    before = (k - 1, s - 1, be) if k else (SUB - 1, s - 2, bp)
                    if k and be is None:
                        before = None
                    if before and before[2] is None:
                        before = None
                    work = []
                    if be is not None:
                        work += [(scores_t, k, 0), (scores_t, k, 1)]
                    for pair, g, there in ((0, s, bm), (1, s - 1, be)):
                        if there is not None and k == TURN_AT[pair]:
                            work += [(turn_max, pair, g)]
                    if before:
                        work += [(values, *before, 0), (values, *before, 1)]
                    if first:
                        work += [(queries, *q) for q in later_q_of(k)]
                    fl = fills_of(k) if bm is not None else []
                    done = 0
                    for n, (product, *which) in enumerate(work):
                        upto = len(fl) * (n + 1) // (len(work) + 1)
                        for f in fl[done:upto]:
                            fill(f)
                        done = upto
                        product(*which)
                    for f in fl[done:]:
                        fill(f)
                    if bp is not None and k in (2, 4):
                        project(k // 2 - 1)
            steps(pe, body)

            pe.wait_ge(S["x_updated"], 2 * NG)
            norm(1, lambda e, c: None, True)
            pe.wait_ge(W["small_loaded"], 16 * 12)
            for i in range(NT):
                if i % 4 == 0:
                    pe.wait_ge(N["h"], norm_count(1, "h", i // 4 + 1))
                m = mm(bank[0][:, i * E0:(i + 1) * E0], hT[:, i * P:(i + 1) * P], rw[:], start=True, stop=True)
            m.then_inc(W["logits"], 1)
            lowb, outb = (bank[1], bankY), (bankM, bank[0])

            def low(c):
                if c >= 2:
                    pe.wait_ge(W["low_ready"], c - 1)
                mm(lowb[c % 2][0:NR, :], downT[:], hT[:, c * CH:(c + 1) * CH], start=True, stop=True)\
                    .then_inc(W["low_product"], 1)
            low(0)
            low(1)
            pe.wait_ge(W["weights_ready"], 1)
            for c in range(NC):
                for i in range(4):
                    m = pe.transpose(quad[c][0:NR, i * P:(i + 1) * P], wx[:, 4 * c + i, :], identf[:])
                m.then_inc(W["wx_turned"], 1)
            for c in range(NC):
                if c >= 2:
                    pe.wait_ge(W["ffn_ready"], c - 1)
                mm(outb[c % 2][:], bwT[:], hT[:, c * CH:(c + 1) * CH], start=True, stop=False)
                pe.wait_ge(W["low_ready"], c + 1)
                mm(outb[c % 2][:], up[:], lowr[:, c % 2, :], start=False, stop=True).then_inc(W["ffn_product"], 1)
                if c + 2 < NC:
                    low(c + 2)

            norm(2, lambda e, c: e.wait_ge(W["x_ffn"], c + 1), True)
            pe.wait_ge(W["pchain"], 14)
            mm(bank[0][:, 2 * P:2 * P + 1], owT[:], bqkv[:, 2:3], start=True, stop=True)\
                .then_inc(W["bias_product"], 1)
            for c in range(NC):
                pe.wait_ge(N["h"], norm_count(2, "h", (3, 3, h2_count, h2_count)[c]))
                need(pe, W["k_biased"], c - 1)
                mm((bankY, bankM)[c % 2][:], wqkv[:, D:2 * D], hT[:, c * CH:(c + 1) * CH], start=True, stop=True)\
                    .then_inc(W["k_product"], 1)

            def out_product(c):
                pe.wait_ge(W["o_ready"], 4 * (c + 1))
                if c >= 2:
                    pe.wait_ge(W["att_ready"], c - 1)
                mm(bank[c % 2][:], owT[:], oT[:, c * CH:(c + 1) * CH], start=True, stop=True)\
                    .then_inc(W["att_product"], 1)

            def window(j, stage):
                if stage(1):
                    i, q = stage(1)
                    pe.wait_ge(W["q_ready"], i + 1)
                    pe.wait_ge(W["k_ready"], 2 * i + 2)
                    need(pe, W["sub_ready"], i - 1)
                    for w in range(2):
                        m = mm(quad[q][WIN * w:WIN * w + WIN, :], qw[:, q, WIN * w:WIN * w + WIN],
                               kx[:, q, w].rearrange("p h k -> p (h k)"), start=True, stop=True)
                    m.then_inc(W["s_product"], 1)
                if stage(0):
                    i, q = stage(0)
                    need(pe, W["q_ready"], i)
                    mm(bank[0][:, 0:P], wqkv[:, 0:D], hT[:, bass.ds(i * P, P)], start=True, stop=True)\
                        .then_inc(W["q_product"], 1)
                if stage(3):
                    i, q = stage(3)
                    pe.wait_ge(W["exp_ready"], i + 1)
                    need(pe, W["pT_ready"], i - 1)
                    for r in range(NH // 2):
                        m = pe.transpose(quad[2 + q][:, r * P:(r + 1) * P],
                                         pw[:, q, 2 * r:2 * r + 2, :].rearrange("p h k -> p (h k)"), identf[:])
                    m.then_inc(W["p_turned"], 1)
                    pe.wait_ge(W["hwin_ready"], i + 1)
                    need(pe, W["v_ready"], i)
                    for w in range(2):
                        for e in range(2):
                            m = mm(bank[1][WIN * e:WIN * e + WIN, w * P:(w + 1) * P],
                                   hwin[:, q, WIN * w:WIN * w + WIN],
                                   wv_eo[:, e].rearrange("p n c -> p (n c)"), start=True, stop=True)
                    m.then_inc(W["v_product"], 1)
                if stage(4):
                    i, q = stage(4)
                    pe.wait_ge(W["pT_ready"], i + 1)
                    pe.wait_ge(W["v_ready"], i + 1)
                    need(pe, W["o_ready"], i - 1)
                    o = (bankY, bankM)[q]
                    for w in range(2):
                        for r in range(NH // 2):
                            mm(o[32 * r:32 * r + 32, w * WIN:(w + 1) * WIN], vw[:, q, w, 32 * r:32 * r + 32],
                               pT[:, q, r * P + w * WIN:r * P + (w + 1) * WIN], start=True, stop=True)
                    for r in range(NH // 2):
                        m = mm(o[32 * r:32 * r + 32, P:2 * P], ones_eo[:], pT[:, q, r * P:(r + 1) * P],
                               start=True, stop=True)
                    m.then_inc(W["o_product"], 1)
                if isinstance(j, int) and j == NT + 2:
                    out_product(0)
                if isinstance(j, int) and j == NT + 3:
                    out_product(1)
            pe.wait_ge(W["prep"], 2)
            windows(pe, window)
            out_product(2)
            out_product(3)

            def mean(c):
                pe.wait_ge(W["x_att"], (3, 3, 6, 6)[c])
                if c >= 2:
                    pe.wait_ge(N["centred"], norm_count(3, "centred", c - 1))
                mm(quad[c % 2], mean_w[:], xT[:, c * CH:(c + 1) * CH], start=True, stop=True).then_inc(N["mean"], 1)

            def var(k, c):
                pe.wait_ge(N["squared"], norm_count(k, "squared", c + 1))
                if k < 5:
                    pe.wait_ge(N["ln"], norm_count(k, "ln", c + 1) - 2)
                    to = quad[2 + c % 2]
                elif c % 2 == 0:
                    pe.wait_ge(E["c_lo"], NC + c)
                    to = bankM[:]
                else:
                    pe.wait_ge(E["z"], c + 1)
                    to = bank[1][:]
                mm(to, mean_w[:], sq[:, c * CH:(c + 1) * CH], start=True, stop=True).then_inc(N["var"], 1)

            def logits(k, h):
                pe.wait_ge(E["xn"], NC * k + 2 * h + 2)
                need(pe, E["c_lo"], NC * k + 2 * h)
                for i in range(NT // 2):
                    at = (NT // 2 * h + i) * P
                    m = mm(bankM[:, i * 12:(i + 1) * 12], xc[:, at:at + P], wrT[:], start=True, stop=True)
                m.then_inc(E["logits"], 1)

            def turn_weights(k, c):
                pe.wait_ge(E["weights_ready"], 2 * k + c // 2 + 1)
                if c % 2:
                    pe.wait_ge(E["c_lo"], NC * k + c)
                for i in range(4):
                    m = pe.transpose(bankM[0:E1, i * P:(i + 1) * P], wts[:, 4 * (c % 2) + i, :], identf[:])
                m.then_inc(E["cw_turned"], 1)

            def turn_out(c):
                pe.wait_ge(x_final, c + 1)
                need(pe, S["out_rows"], c)
                for i in range(4):
                    m = pe.transpose(bankM[:, i * P:(i + 1) * P], xT[:, (4 * c + i) * P:(4 * c + i + 1) * P],
                                     identf[:])
                m.then_inc(S["out_turned"], 1)

            def first_product(u):
                q, e = u // E1, u % E1
                cs = slice(q % NC * CH, (q % NC + 1) * CH)
                if e == 0:
                    pe.wait_ge(E["c_lo"], q + 1)
                    pe.wait_ge(E["xn_lo"], q + 1)
                need(pe, E["act"], u - 1)
                for f in range(2):
                    at = e * F1 + f * P
                    for t, (wp, xp) in enumerate(((0, 0), (0, 1), (1, 0))):
                        m = mm(stT[:, u % 2, f * CH:(f + 1) * CH], w1h[:, wp, at:at + P],
                               xnh[:, xp, cs], start=(t == 0), stop=(t == 2))
                m.then_inc(E["pre"], 1)
                need(pe, E["cw"], u)
                mm(bankY[:], spread[:, e, :], cT16[:, cs], start=True, stop=True).then_inc(E["cb"], 1)

            def second_product(u):
                q, e = u // E1, u % E1
                pe.wait_ge(E["hid_lo"], u + 1)
                if e == 0:
                    need(pe, E["z"], q - 1)
                    if q in (3, 5):
                        pe.wait_ge(N["ln"], norm_count(5, "ln", q - 1))
                for n, (f, wp, hp) in enumerate([(f, *p) for f in range(2) for p in ((0, 0), (0, 1), (1, 0))]):
                    at = (2 * e + f) * P
                    m = mm(bank[q % 2][:], w2h[:, wp, at:at + P], hidh[:, u % AHEAD, hp, f * CH:(f + 1) * CH],
                           start=(e == 0 and n == 0), stop=(e == E1 - 1 and n == 5))
                m.then_inc(E["y"], 1)

            mean(0)
            mean(1)
            var(3, 0)
            var(3, 1)
            mean(2)
            mean(3)
            var(4, 0)
            var(4, 1)
            logits(0, 0)
            var(3, 2)
            var(3, 3)
            var(4, 2)
            var(4, 3)
            turn_weights(0, 0)
            turn_weights(0, 1)
            pe.wait_ge(W["w_lo"], 2)
            pe.wait_ge(N["ln"], norm_count(4, "ln", NC))
            for u in range(AHEAD):
                first_product(u)
            for u in range(UNITS):
                k, h, s = next_half(u)
                if s == 1 and k == 1:
                    var(5, 2 * h)
                    var(5, 2 * h + 1)
                if s == 4:
                    logits(k, h)
                if u + AHEAD < UNITS:
                    first_product(u + AHEAD)
                if s in (11, 14):
                    turn_weights(k, 2 * h + s // 14)
                if u in OUT_AT:
                    turn_out(OUT_AT.index(u))
                second_product(u)
            turn_out(NC - 1)

        @block.scalar
        def _(act):
            A = nc.scalar.activation
            act.preload_act_table_set("natural_log_exp_and_others")
            act.wait_ge(S["c_loaded"], 64)
            A(csil[:, 0, :], cT[:].rearrange("p l b -> p (l b)"), ACT.Exp, scale=-1.0).then_inc(S["csil_step"], 1)
            for c in range(NC):
                act.wait_ge(S["x_turned"], c + 1)
                A(xT[:, c * CH:(c + 1) * CH], quad[c], ACT.Copy).then_inc(S["xT_ready"], 1)
            def norm(k, eps, centre):
                for i in range(NC + 1):
                    if i < NC:
                        cs = slice(i * CH, (i + 1) * CH)
                        act.wait_ge(N["centred"], norm_count(k, "centred", i + 1))
                        A(sq[:, cs], xc[:, cs], ACT.Square).then_inc(N["squared"], 1)
                    if i >= 1:
                        cs = slice((i - 1) * CH, i * CH)
                        act.wait_ge(N["var"], norm_count(k, "var", i))
                        A(rstd[:, cs], quad[2 + (i - 1) % 2], ACT.Ln, bias=epsc[:, eps:eps + 1]).then_inc(N["ln"], 1)
                        act.wait_ge(N["ln"], norm_count(k, "ln", i))
                        A(rstd[:, cs], rstd[:, cs], ACT.Exp, scale=-0.5).then_inc(N["rstd"], 1)

            norm(0, 0, True)
            act.wait_ge(S["qk_product"], 1)
            A(qk[:], bank[0][:], ACT.Copy, scale=HD0 ** -0.5).then_inc(S["qk_ready"], 1)

            def latents(c):
                act.wait_ge(S["lat_product"], c + 1)
                A(lat[0:96, c * CH:(c + 1) * CH], bank[c % 2][0:96, :], ACT.Copy).then_inc(S["lat_hi"], 1)

            def queries(g, c):
                n = 2 * g + c
                act.wait_ge(S["q_product"], n + 1)
                A(q_hi[g // GR][:, g % GR, c * CH:(c + 1) * CH], quad[n % 4], ACT.Copy).then_inc(S["q_hi_ready"], 1)
                if n >= 2:
                    need(act, S["q_lo_later"], n - 3)
                    A(q_stage[n % 2], quad[n % 4], ACT.Copy).then_inc(S["q_staged"], 1)

            queries(0, 0)
            queries(0, 1)
            for c in range(NC):
                latents(c)

            def body(s, bm, be, bp):
                if be is not None and isinstance(s, int) and s == 1:
                    act.wait_ge(S["q_lo_later"], 2 * NG - 2)

                def exps(k):
                    n = SUB * (s - 1) + k
                    c, segs = TILES[k % NTL]
                    width = segs[1][2] + CH - segs[1][1]
                    for x in range(2):
                        act.wait_ge(S["st_ready"], 2 * n + x + 1)
                        if x == 0 and not (isinstance(s, int) and s == 1 and k < 2):
                            act.wait_ge(S["pv_done"], n - 1)
                        A(probs[:, k % 2, x, 0:width], stT[:, x, 0:width], ACT.Exp).then_inc(S["exp_done"], 1)

                def logs(pair, c, g):
                    act.wait_ge(S["y_copied"], 4 * g + 2 * pair + c + 1)
                    if pair == 0 and not (isinstance(g, int) and g == 0):
                        act.wait_ge(S["y_n_ready"], 2 * (g - 1) + c + 1)
                    here, there = (slice(2 * C0 * p, 2 * C0 * p + 2 * C0) for p in (pair, 1 - pair))
                    A(ln_sum[here, c, :], y_part[there, c, :], ACT.Ln).then_inc(S["ln_done"], 1)
                    A(y_raw[here, c, :], y_part[here, c, :], ACT.Copy).then_inc(S["y_moved"], 1)
                    if pair == 1:
                        act.wait_ge(S["ln_done"], 4 * g + 3 + c)
                        if not (isinstance(g, int) and g == 0):
                            act.wait_ge(S["y_n_ready"], 2 * (g - 1) + c + 1)
                        A(inv_sum[:, c, :], ln_sum[:, c, :], ACT.Exp, scale=-1.0).then_inc(S["inv_ready"], 1)

                for k in range(SUB):
                    if be is not None:
                        exps(k)
                    if k == 0 and bp is not None:
                        logs(1, 1, s - 2)
                    if be is not None:
                        if k == 2:
                            logs(0, 0, s - 1)
                        if k == NTL:
                            logs(0, 1, s - 1)
                        if k == NTL + 2:
                            logs(1, 0, s - 1)
                    if isinstance(s, int) and s == 0:
                        for q in later_q_of(k):
                            queries(*q)
                    for pair, g, there in ((0, s, bm), (1, s - 1, be)):
                        if there is not None and k == TURN_AT[pair]:
                            act.wait_ge(S["max_turned"], 2 * g + pair + 1)
                            if not (isinstance(g, int) and g == 0):
                                act.wait_ge(max_placed[pair], 16 * g)
                            A(neg_max[:, pair, :], bankM[0:2 * QB, 0:P], ACT.Copy, scale=-1.0)\
                                .then_inc(S["neg_max_ready"], 1)
            steps(act, body)

            norm(1, 0, True)
            act.wait_ge(W["exp_in"], 1)
            A(pr[:, :, 0:E0], lg[:, :, 0:E0], ACT.Exp).then_inc(W["exp_out"], 1)
            act.wait_ge(W["w12_loaded"], 32)
            for dst, src in ((w1h, w1), (w2h, w2)):
                A(dst[:, 0, :], src[:], ACT.Copy, scale=UP).then_inc(W["w_hi"], 1)
            for c in range(NC):
                act.wait_ge(W["wx_turned"], c + 1)
                A(wxT[:, c * CH:(c + 1) * CH], quad[c][0:NR, :], ACT.Copy).then_inc(W["wxT_ready"], 1)
            outb = (bankM, bank[0])
            for c in range(NC):
                act.wait_ge(W["ffn_product"], c + 1)
                if c >= 2:
                    act.wait_ge(W["x_ffn"], c - 1)
                A(ffn[:, c % 2, :], outb[c % 2][:], ACT.Identity, bias=bb[:]).then_inc(W["ffn_ready"], 1)

            norm(2, 0, True)
            act.wait_ge(W["prep"], 1)
            for c in range(NC):
                act.wait_ge(W["k_product"], c + 1)
                A(kT[:, c * CH:(c + 1) * CH], (bankY, bankM)[c % 2][:], ACT.Identity, bias=bqkv[:, 1:2])\
                    .then_inc(W["k_biased"], 1)

            def window(j, stage):
                if stage(2):
                    i, q = stage(2)
                    act.wait_ge(W["sub_ready"], i + 1)
                    need(act, W["p_turned"], i - 1)
                    A(pw[:, q], sub[:, q], ACT.Exp).then_inc(W["exp_ready"], 1)
                if stage(0):
                    i, q = stage(0)
                    act.wait_ge(W["q_product"], i + 1)
                    need(act, W["s_product"], i - 1)
                    A(qw[:, q, :], bank[0][:, 0:P], ACT.Identity, bias=bq_s[:], scale=HD1 ** -0.5)\
                        .then_inc(W["q_ready"], 1)
                if stage(3):
                    i, q = stage(3)
                    act.wait_ge(W["p_turned"], i + 1)
                    need(act, W["o_product"], i - 1)
                    A(pT[:, q], quad[2 + q][:], ACT.Copy).then_inc(W["pT_ready"], 1)
                    act.wait_ge(W["v_product"], i + 1)
                    A(vw[:, q].rearrange("p w c -> p (w c)"), bank[1][:, 0:2 * P], ACT.Copy)\
                        .then_inc(W["v_ready"], 1)
            windows(act, window)
            act.wait_ge(W["prep"], 2)
            for c in range(NC):
                act.wait_ge(W["att_product"], c + 1)
                if c >= 2:
                    act.wait_ge(W["x_att"], (0, 1, 3, 4)[c - 1])
                A(ffn[:, c % 2, :], bank[c % 2][:], ACT.Identity, bias=ob_v[:]).then_inc(W["att_ready"], 1)

            def square(k, c):
                if k == 3:
                    act.wait_ge(N["centred"], norm_count(3, "centred", c + 1))
                elif k == 4:
                    act.wait_ge(N["h"], norm_count(3, "h", c + 1))
                else:
                    act.wait_ge(E["z"], c + 1)
                cs = slice(c * CH, (c + 1) * CH)
                A(sq[:, cs], (xc if k == 3 else z)[:, cs], ACT.Square).then_inc(N["squared"], 1)

            def inv_root(k, c):
                cs = slice(c * CH, (c + 1) * CH)
                bank_v = quad[2 + c % 2] if k < 5 else (bankM, bank[1])[c % 2][:]
                act.wait_ge(N["var"], norm_count(k, "var", c + 1))
                A(rstd[:, cs], bank_v, ACT.Ln, bias=epsc[:, min(k, 4) - 3:min(k, 4) - 2]).then_inc(N["ln"], 1)
                act.wait_ge(N["ln"], norm_count(k, "ln", c + 1))
                A(rstd[:, cs], rstd[:, cs], ACT.Exp, scale=-0.5).then_inc(N["rstd"], 1)

            def xn_high(k, c):
                act.wait_ge(E["xn"], NC * k + c + 1)
                if k:
                    act.wait_ge(E["pre"], E1 * (c + 1))
                A(xnh[:, 0, c * CH:(c + 1) * CH], xc[:, c * CH:(c + 1) * CH], ACT.Copy).then_inc(E["xn_hi"], 1)

            def exp_logits(k, h):
                act.wait_ge(E["exp_in"], 2 * k + h + 1)
                A(pr[:, 0:NT // 2], lg[:, 0:NT // 2], ACT.Exp).then_inc(E["exp_out"], 1)

            def weights_high(k, c):
                act.wait_ge(E["cw_turned"], NC * k + c + 1)
                A(cT16[0:E1, c * CH:(c + 1) * CH], bankM[0:E1, :], ACT.Copy).then_inc(E["c_hi"], 1)

            def rows_out(c):
                act.wait_ge(S["out_turned"], c + 1)
                A(x_rows[:, 4 * c:4 * c + 4, :].rearrange("p n d -> p (n d)"), bankM[:], ACT.Copy)\
                    .then_inc(S["out_rows"], 1)

            square(3, 0)
            square(3, 1)
            inv_root(3, 0)
            inv_root(3, 1)
            square(4, 0)
            square(4, 1)
            inv_root(4, 0)
            inv_root(4, 1)
            square(3, 2)
            square(3, 3)
            xn_high(0, 0)
            xn_high(0, 1)
            inv_root(3, 2)
            inv_root(3, 3)
            exp_logits(0, 0)
            square(4, 2)
            square(4, 3)
            inv_root(4, 2)
            inv_root(4, 3)
            act.wait_ge(W["consts_b"], 2)
            weights_high(0, 0)
            weights_high(0, 1)
            for u in range(UNITS):
                k, h, s = next_half(u - AHEAD)
                if s == 0 and k == 1:
                    square(5, 2 * h)
                    square(5, 2 * h + 1)
                if s == 2 and k == 1:
                    act.preload_act_table_set("natural_log_exp_and_others")
                    inv_root(5, 2 * h)
                    inv_root(5, 2 * h + 1)
                if s == 4:
                    xn_high(k, 2 * h)
                    xn_high(k, 2 * h + 1)
                if s == 6:
                    exp_logits(k, h)
                if s in (11, 14):
                    weights_high(k, 2 * h + s // 14)
                if u - AHEAD - 1 in OUT_AT:
                    rows_out(OUT_AT.index(u - AHEAD - 1))
                act.wait_ge(E["cb"], u + 1)
                need(act, E["hid_w"], u - AHEAD + 1)
                A(cw[:, u % AHEAD, :], bankY[:], ACT.Copy).then_inc(E["cw"], 1)
                act.wait_ge(E["pre"], u + 1)
                need(act, E["hid_lo"], u - AHEAD + 1)
                A(hid[:, u % AHEAD, :], stT[:, u % 2, :], ACT.Silu, scale=1.0 / UP).then_inc(E["act"], 1)
            rows_out(NC - 1)

        def add_ffn(dve, V, c):
            dve.wait_ge(W["ffn_ready"], c + 1)
            cs = slice(c * CH, (c + 1) * CH)
            V.scalar_tensor_tensor(out=xT[:, cs], in0=ffn[:, c % 2, :], scalar=mod[:, 0, 5, c // 2:c // 2 + 1],
                                   in1=xT[:, cs], op0=ALU.mult, op1=ALU.add).then_inc(W["x_ffn"], 1)

        def shifted_pieces_back(c):
            b = c // 2
            if c % 2 == 0:
                return [(b * L + SHIFT, 0, CH)]
            return [(b * L + CH + SHIFT, 0, CH - SHIFT), (b * L, CH - SHIFT, SHIFT)]

        @block.vector
        def _(dve):
            chain = [0]
            dch = S["gate_step"]

            def link(ins):
                chain[0] += 1
                ins.then_inc(dch, 1)
                dve.wait_ge(dch, chain[0])

            V = nc.vector
            dve.wait_ge(S["csil_step"], 1)
            link(V.tensor_scalar(csil[:, 1, :], csil[:, 0, :], 1.0, None, ALU.add))
            link(V.reciprocal(csil[:, 1, :], csil[:, 1, :]))
            V.tensor_tensor(csil[:, 2, :], cT[:].rearrange("p l b -> p (l b)"), csil[:, 1, :], ALU.mult)\
                .then_inc(S["silu_ready"], 1)
            def centre(k):
                for c in range(NC):
                    cs = slice(c * CH, (c + 1) * CH)
                    dve.wait_ge(N["mean"], norm_count(k, "mean", c + 1))
                    V.tensor_tensor(xc[:, cs], xT[:, cs], quad[c % 2], ALU.subtract).then_inc(N["centred"], 1)

            centre(0)
            dve.wait_ge(S["mod_product"], 1)
            link(V.tensor_copy(mod[:].rearrange("p l j b -> p (l j b)"), bankM[:, 0:12 * B]))
            for j in (1, 4):
                link(V.tensor_scalar(mod[:, :, j, :], mod[:, :, j, :], 1.0, None, ALU.add))
            for n, j in enumerate((2, 5)):
                gate = mod[:, :, j, :]
                link(V.tensor_scalar(sgn[:, n], gate, 0.0, 2.0, ALU.is_ge, ALU.mult))
                link(V.tensor_scalar(sgn[:, n], sgn[:, n], -1.0, None, ALU.add))
                link(V.tensor_tensor(gate, gate, sgn[:, n], ALU.mult))
                link(V.tensor_scalar(gate, gate, 0.25, None, ALU.max))
                link(V.tensor_tensor(gate, gate, sgn[:, n], ALU.mult))

            def norm(k, l, sh, sc, shifted=False):
                if k:
                    centre(k)
                for c in range(NC):
                    cs = slice(c * CH, (c + 1) * CH)
                    b = c // 2
                    dve.wait_ge(N["rstd"], norm_count(k, "rstd", c + 1))
                    V.scalar_tensor_tensor(out=xc[:, cs], in0=xc[:, cs], scalar=mod[:, l, sc, b:b + 1],
                                           in1=rstd[:, cs], op0=ALU.mult, op1=ALU.mult).then_inc(N["scaled"], 1)
                    dve.wait_ge(N["scaled"], norm_count(k, "scaled", c + 1))
                    for to, at, m in shifted_pieces(c) if shifted else [(c * CH, c * CH, CH)]:
                        V.tensor_scalar(hT[:, to:to + m], xc[:, at:at + m], mod[:, l, sh, b:b + 1], None, ALU.add)\
                            .then_inc(N["h"], 1)

            norm(0, 0, 0, 1)

            def latents(c):
                cs = slice(c * CH, (c + 1) * CH)
                dve.wait_ge(S["lat_hi"], c + 1)
                V.tensor_tensor(lat[64:96, cs], bank[c % 2][64:96, :], lat[64:96, cs], ALU.subtract)\
                    .then_inc(S["lat_ready"], 1)

            def queries(g, c):
                n = 2 * g + c
                dve.wait_ge(S["q_hi_ready"], n + 1)
                cs = slice(c * CH, (c + 1) * CH)
                V.tensor_tensor(q_lo[g // GR][:, g % GR, cs], quad[n % 4], q_hi[g // GR][:, g % GR, cs],
                                ALU.subtract).then_inc(S["q_lo_ready"], 1)

            queries(0, 0)
            queries(0, 1)
            for c in range(NC):
                latents(c)
            dve.wait_ge(S["vo_product"], 1)
            V.tensor_copy(vo[:].rearrange("p g d -> p (g d)"), bankM[:]).then_inc(S["vo_ready"], 1)
            dve.wait_ge(S["latO_product"], 1)
            V.tensor_copy(latO[:, :, 0:C0], bankY[:].rearrange("p (n c) -> p n c", c=C0)).then_inc(S["latO_ready"], 1)
            dve.wait_ge(S["consts"], 7)

            def body(s, bm, be, bp):
                def take(f):
                    j, i, half = FILLS[f]
                    width = min(CH, (i + 1) * P - half * CH)
                    dve.wait_ge(S["scores_ready"], NF * s + f + 1)
                    V.tensor_reduce(part_max[:, half, j, i:i + 1], bank[f % 2][:, 0:width], AX.X, ALU.max)\
                        .then_inc(S["max_taken"], 1)

                def copy_y(pair, c, g):
                    v = 4 * g + 2 * pair + c
                    dve.wait_ge(S["pv_done"], SUB * g + NTL * pair + (2 if c == 0 else NTL))
                    if not (isinstance(g, int) and v < 2):
                        dve.wait_ge(S["ln_done"], v - 1)
                        dve.wait_ge(S["y_moved"], v - 1)
                    V.tensor_copy(y_part[:, c, :], bankY[:, :]).then_inc(S["y_copied"], 1)

                def fold(pair, g):
                    dve.wait_ge(S["max_taken"], NF * g + NF // 2 * (pair + 1))
                    if not (isinstance(g, int) and g == 0):
                        dve.wait_ge(S["max_turned"], 2 * g + pair - 1)
                    hs = slice(2 * pair, 2 * pair + 2)
                    V.tensor_tensor(row_max[:].rearrange("p (j i) -> p j i", j=GR)[:, hs], part_max[:, 0, hs],
                                    part_max[:, 1, hs], ALU.max).then_inc(S["row_max_ready"], 1)

                def update(c):
                    dve.wait_ge(S["proj_done"], 2 * (s - 2) + c + 1)
                    cs = slice(bp * L + c * CH, bp * L + (c + 1) * CH)
                    V.scalar_tensor_tensor(out=xT[:, cs], in0=bankM[:, :], scalar=mod[:, 0, 2, bp:bp + 1],
                                           in1=xT[:, cs], op0=ALU.mult, op1=ALU.add).then_inc(S["x_updated"], 1)

                for k in range(SUB):
                    if k == 0 and be is not None:
                        fold(1, s - 1)
                    fl = fills_of(k) if bm is not None else []
                    for f in fl[:-1]:
                        take(f)
                    if k == 0 and bp is not None:
                        copy_y(1, 1, s - 2)
                    if be is not None:
                        if k == 2:
                            copy_y(0, 0, s - 1)
                        if k == NTL:
                            copy_y(0, 1, s - 1)
                        if k == NTL + 2:
                            copy_y(1, 0, s - 1)
                    for f in fl[-1:]:
                        take(f)
                    if bp is not None and k in (2, 4):
                        update(k // 2 - 1)
                    if bm is not None and k == NTL - 1:
                        fold(0, s)
                if bp is not None:
                    dve.wait_ge(S["x_updated"], 2 * (s - 1))
            steps(dve, body)

            chain2 = [0]

            def then(ins):
                chain2[0] += 1
                ins.then_inc(W["dchain"], 1)
                dve.wait_ge(W["dchain"], chain2[0])

            def softmax_in(x, k):
                g, n = x.shape[2], x.shape[3]
                m = st[:, k, :, 0:g]
                then(V.tensor_reduce(m, x, AX.X, ALU.max))
                then(V.tensor_tensor(x, x, m.unsqueeze(3).broadcast_to([P, NT, g, n]), ALU.subtract))

            def softmax_out(x, k):
                g, n = x.shape[2], x.shape[3]
                m = st[:, k, :, 0:g]
                then(V.tensor_reduce(m, x, AX.X, ALU.add))
                then(V.reciprocal(m, m))
                then(V.tensor_tensor(x, x, m.unsqueeze(3).broadcast_to([P, NT, g, n]), ALU.mult))

            def top_two(x, w, tiny):
                n = x.shape[2]
                g = gt[:, :, 0:n * n].rearrange("p t (e f) -> p t e f", e=n)
                q = eq[:, :, 0:n * n].rearrange("p t (e f) -> p t e f", e=n)
                other = x.unsqueeze(2).broadcast_to([P, NT, n, n])
                own = x.unsqueeze(3).broadcast_to([P, NT, n, n])
                then(V.tensor_tensor(g, other, own, ALU.is_gt))
                then(V.tensor_tensor(q, other, own, ALU.is_equal))
                then(V.tensor_tensor(q, q, earlier[:, 0:n, 0:n].unsqueeze(1).broadcast_to([P, NT, n, n]), ALU.mult))
                then(V.tensor_tensor(g, g, q, ALU.add))
                r = rank[:, :, 0:n]
                then(V.tensor_reduce(r, g, AX.X, ALU.add))
                then(V.tensor_scalar(r, r, 1.5, None, ALU.is_lt))
                then(V.tensor_tensor(w, x, r, ALU.mult))
                s1 = st[:, 4, :, 0:1]
                then(V.tensor_reduce(s1, w.unsqueeze(2), AX.X, ALU.add))
                then(V.tensor_scalar(s1, s1, tiny, None, ALU.add))
                then(V.reciprocal(s1, s1))
                then(V.tensor_tensor(w, w, s1.broadcast_to([P, NT, n]), ALU.mult))

            norm(1, 0, 3, 4)
            dve.wait_ge(W["logits"], 1)
            l0 = lg[:, :, 0:E0]
            then(V.tensor_tensor(l0, bank[0][:, 0:NT * E0].rearrange("p (t e) -> p t e", e=E0),
                                 rb[:].unsqueeze(1).broadcast_to([P, NT, E0]), ALU.add))
            softmax_in(l0.unsqueeze(2), 0)
            V.tensor_copy(st[:, 5, :, 0:1], st[:, 0, :, 0:1]).then_inc(W["exp_in"], 1)
            dve.wait_ge(W["exp_out"], 1)
            dve.wait_ge(W["pchain"], 14)
            softmax_out(pr[:, :, 0:E0].unsqueeze(2), 1)
            top_two(pr[:, :, 0:E0], wts[:, :, 0:E0], 1e-6)
            dve.wait_ge(W["consts_b"], 1)
            V.tensor_copy(wx[:, :, R0:NR].rearrange("p t (e r) -> p t e r", r=R0),
                          wts[:, :, 0:E0].unsqueeze(3).broadcast_to([P, NT, E0, R0])).then_inc(W["weights_ready"], 1)
            lowb = (bank[1], bankY)
            for c in range(NC):
                dve.wait_ge(W["low_product"], c + 1)
                dve.wait_ge(W["wxT_ready"], c + 1)
                if c >= 2:
                    dve.wait_ge(W["ffn_product"], c - 1)
                V.tensor_tensor(lowr[:, c % 2, :], lowb[c % 2][0:NR, :], wxT[:, c * CH:(c + 1) * CH], ALU.mult)\
                    .then_inc(W["low_ready"], 1)
                if c >= 1:
                    add_ffn(dve, V, c - 1)
            add_ffn(dve, V, NC - 1)
            then(V.tensor_scalar(bq_s[:], bqkv[:, 0:1], HD1 ** -0.5, None, ALU.mult))
            V.tensor_scalar(ga2[:], mod[:, 1, 2, :], 2.0, None, ALU.mult).then_inc(W["prep"], 1)

            norm(2, 1, 0, 1, shifted=True)

            dve.wait_ge(W["bias_product"], 1)
            V.tensor_tensor(ob_v[:], bank[0][:, 2 * P:2 * P + 1], ob[:], ALU.add).then_inc(W["prep"], 1)
            for n, (dst, src) in enumerate(((w1h, w1), (w2h, w2))):
                dve.wait_ge(W["w_hi"], n + 1)
                V.scalar_tensor_tensor(out=dst[:, 1, :], in0=src[:], scalar=UP, in1=dst[:, 0, :],
                                       op0=ALU.mult, op1=ALU.subtract).then_inc(W["w_lo"], 1)

            def window(j, stage):
                if stage(5):
                    i, q = stage(5)
                    dve.wait_ge(W["o_product"], i + 1)
                    o = (bankY, bankM)[q]
                    V.reciprocal(inv_w[:, q, :], o[:, P:2 * P]).then_inc(W["inv_ready"], 1)
                    dve.wait_ge(W["inv_ready"], i + 1)
                    V.tensor_tensor(oT[:, bass.ds(i * P, P)], o[:, 0:P], inv_w[:, q, :], ALU.mult)\
                        .then_inc(W["o_ready"], 1)
                if stage(1):
                    i, q = stage(1)
                    s4 = quad[q].rearrange("p (h k) -> p h k", h=NH)
                    dve.wait_ge(W["s_product"], i + 1)
                    V.tensor_reduce(mx[:, q, :], s4, AX.X, ALU.max).then_inc(W["max_ready"], 1)
                    dve.wait_ge(W["max_ready"], i + 1)
                    need(dve, W["exp_ready"], i - 1)
                    V.tensor_tensor(sub[:, q], s4, mx[:, q, :].unsqueeze(2).broadcast_to([P, NH, WIN]),
                                    ALU.subtract).then_inc(W["sub_ready"], 1)
            windows(dve, window)
            def add_attention(c):
                dve.wait_ge(W["att_ready"], c + 1)
                b = c // 2
                for to, at, m in shifted_pieces_back(c):
                    V.scalar_tensor_tensor(out=xT[:, to:to + m], in0=ffn[:, c % 2, at:at + m],
                                           scalar=ga2[:, b:b + 1], in1=xT[:, to:to + m], op0=ALU.mult,
                                           op1=ALU.add).then_inc(W["x_att"], 1)

            def centre_chunk(c):
                cs = slice(c * CH, (c + 1) * CH)
                dve.wait_ge(N["mean"], norm_count(3, "mean", c + 1))
                V.tensor_tensor(xc[:, cs], xT[:, cs], quad[c % 2], ALU.subtract).then_inc(N["centred"], 1)

            def modulate(c):
                cs, b = slice(c * CH, (c + 1) * CH), c // 2
                dve.wait_ge(N["rstd"], norm_count(3, "rstd", c + 1))
                V.scalar_tensor_tensor(out=xc[:, cs], in0=xc[:, cs], scalar=mod[:, 1, 4, b:b + 1],
                                       in1=rstd[:, cs], op0=ALU.mult, op1=ALU.mult).then_inc(N["scaled"], 1)
                dve.wait_ge(N["scaled"], norm_count(3, "scaled", c + 1))
                V.tensor_scalar(z[:, cs], xc[:, cs], mod[:, 1, 3, b:b + 1], None, ALU.add).then_inc(N["h"], 1)

            def rms(k, c):
                cs = slice(c * CH, (c + 1) * CH)
                dve.wait_ge(N["rstd"], norm_count(4 + k, "rstd", c + 1))
                V.scalar_tensor_tensor(out=xc[:, cs], in0=z[:, cs], scalar=nw[:], in1=rstd[:, cs],
                                       op0=ALU.mult, op1=ALU.mult).then_inc(E["xn"], 1)

            def xn_low(k, c):
                cs = slice(c * CH, (c + 1) * CH)
                dve.wait_ge(E["xn_hi"], NC * k + c + 1)
                V.tensor_tensor(xnh[:, 1, cs], xc[:, cs], xnh[:, 0, cs], ALU.subtract).then_inc(E["xn_lo"], 1)

            def weights_low(k, c):
                cs = slice(c * CH, (c + 1) * CH)
                dve.wait_ge(E["c_hi"], NC * k + c + 1)
                if k == 0 and c == 0:
                    dve.wait_ge(W["consts_b"], 2)
                V.tensor_tensor(cT16[96:104, cs], bankM[0:E1, :], cT16[0:E1, cs], ALU.subtract)\
                    .then_inc(E["c_lo"], 1)

            def both(*ins):
                chain2[0] += len(ins)
                for i in ins:
                    i.then_inc(W["dchain"], 1)
                dve.wait_ge(W["dchain"], chain2[0])

            HT = NT // 2
            lgh, prh = lg[:, 0:HT], pr[:, 0:HT]
            macro, micro = prh[:, :, 0:NGR], prh[:, :, NGR:12].rearrange("p t (g e) -> p t g e", e=2)
            stm, stu, best, den, first = st[:, 0, 0:HT, 0:1], st[:, 1, 0:HT], st[:, 2, 0:HT], st[:, 3, 0:HT], \
                st[:, 5, 0:HT]
            gth = gt[:, 0:HT, 0:NGR * NGR].rearrange("p t (e f) -> p t e f", e=NGR)
            eqh = eq[:, 0:HT, 0:NGR * NGR].rearrange("p t (e f) -> p t e f", e=NGR)
            rk, total = rank[:, 0:HT, 0:NGR], st[:, 4, 0:HT, 0:1]
            w4 = wts[:, 0:HT].rearrange("p t (g e) -> p t g e", e=2)
            wide = [P, HT, NGR, NGR]

            def route(k, h, step):
                if step == 0:
                    dve.wait_ge(E["logits"], 2 * k + h + 1)
                    both(V.tensor_copy(lgh, bankM[:, 0:HT * 12].rearrange("p (t e) -> p t e", e=12)))
                    lm, lu = lgh[:, :, 0:NGR], lgh[:, :, NGR:12].rearrange("p t (g e) -> p t g e", e=2)
                    both(V.tensor_reduce(stm, lm.unsqueeze(2), AX.X, ALU.max),
                         V.tensor_reduce(stu, lu, AX.X, ALU.max))
                    both(V.tensor_tensor(lm, lm, stm.broadcast_to([P, HT, NGR]), ALU.subtract))
                    V.tensor_tensor(lu, lu, stu.unsqueeze(3).broadcast_to([P, HT, NGR, 2]), ALU.subtract)\
                        .then_inc(E["exp_in"], 1)
                if step == 1:
                    dve.wait_ge(E["exp_out"], 2 * k + h + 1)
                    both(V.tensor_reduce(stm, macro.unsqueeze(2), AX.X, ALU.add),
                         V.tensor_reduce(stu, micro, AX.X, ALU.add))
                    both(V.reciprocal(stm, stm), V.reciprocal(stu, stu))
                    both(V.tensor_tensor(macro, macro, stm.broadcast_to([P, HT, NGR]), ALU.mult),
                         V.tensor_tensor(micro, micro, stu.unsqueeze(3).broadcast_to([P, HT, NGR, 2]), ALU.mult))
                if step == 2:
                    other, own = macro.unsqueeze(2).broadcast_to(wide), macro.unsqueeze(3).broadcast_to(wide)
                    both(V.tensor_tensor(gth, other, own, ALU.is_gt), V.tensor_tensor(eqh, other, own, ALU.is_equal),
                         V.tensor_reduce(best, micro, AX.X, ALU.max),
                         V.tensor_tensor(first, micro[:, :, :, 0], micro[:, :, :, 1], ALU.is_ge))
                    both(V.tensor_tensor(eqh, eqh, earlier[:, 0:NGR, 0:NGR].unsqueeze(1).broadcast_to(wide), ALU.mult),
                         V.tensor_scalar(den, best, 1e-9, None, ALU.add))
                    both(V.tensor_tensor(gth, gth, eqh, ALU.add), V.reciprocal(den, den))
                if step == 3:
                    both(V.tensor_reduce(rk, gth, AX.X, ALU.add), V.tensor_tensor(best, best, den, ALU.mult))
                    both(V.tensor_scalar(rk, rk, 1.5, None, ALU.is_lt))
                    both(V.tensor_tensor(macro, macro, rk, ALU.mult))
                    both(V.tensor_reduce(total, macro.unsqueeze(2), AX.X, ALU.add))
                if step == 4:
                    both(V.tensor_scalar(total, total, 1e-9, None, ALU.add))
                    both(V.reciprocal(total, total), V.tensor_tensor(best, best, macro, ALU.mult))
                    both(V.tensor_tensor(best, best, total.broadcast_to([P, HT, NGR]), ALU.mult))
                    both(V.tensor_tensor(w4[:, :, :, 0], best, first, ALU.mult))
                    V.tensor_tensor(w4[:, :, :, 1], best, w4[:, :, :, 0], ALU.subtract)\
                        .then_inc(E["weights_ready"], 1)

            def add_mixed(q):
                cs = slice(q % NC * CH, (q % NC + 1) * CH)
                dve.wait_ge(E["y"], E1 * (q + 1))
                V.scalar_tensor_tensor(out=z[:, cs], in0=bank[q % 2][:], scalar=1.0 / UP, in1=z[:, cs],
                                       op0=ALU.mult, op1=ALU.add).then_inc(E["z"], 1)

            def final(c):
                cs = slice(c * CH, (c + 1) * CH)
                dve.wait_ge(E["z"], NC + c + 1)
                V.scalar_tensor_tensor(out=xT[:, cs], in0=z[:, cs], scalar=mod[:, 1, 5, c // 2:c // 2 + 1],
                                       in1=xT[:, cs], op0=ALU.mult, op1=ALU.add).then_inc(x_final, 1)

            add_attention(0)
            add_attention(1)
            centre_chunk(0)
            centre_chunk(1)
            add_attention(2)
            add_attention(3)
            modulate(0)
            modulate(1)
            centre_chunk(2)
            centre_chunk(3)
            rms(0, 0)
            rms(0, 1)
            xn_low(0, 0)
            xn_low(0, 1)
            route(0, 0, 0)
            modulate(2)
            route(0, 0, 1)
            modulate(3)
            route(0, 0, 2)
            route(0, 0, 3)
            rms(0, 2)
            route(0, 0, 4)
            rms(0, 3)
            weights_low(0, 0)
            weights_low(0, 1)
            for u in range(UNITS):
                k, h, s = next_half(u - AHEAD + 1)
                at = u - AHEAD + 1
                if at % E1 == 0 and at > 0:
                    add_mixed(at // E1 - 1)
                if s == 3 and k == 1:
                    rms(k, 2 * h)
                    rms(k, 2 * h + 1)
                if s == 7:
                    xn_low(k, 2 * h)
                    xn_low(k, 2 * h + 1)
                if s in ROUTE_AT:
                    route(k, h, ROUTE_AT.index(s))
                if s in (12, 15):
                    weights_low(k, 2 * h + s // 15)
                if u in OUT_AT:
                    final(OUT_AT.index(u))
                dve.wait_ge(E["hid_w"], u + 1)
                need(dve, E["y"], u - AHEAD + 1)
                V.tensor_copy(hidh[:, u % AHEAD, 0, :], hid[:, u % AHEAD, :]).then_inc(E["hid_hi"], 1)
                dve.wait_ge(E["hid_hi"], u + 1)
                V.tensor_tensor(hidh[:, u % AHEAD, 1, :], hid[:, u % AHEAD, :], hidh[:, u % AHEAD, 0, :], ALU.subtract)\
                    .then_inc(E["hid_lo"], 1)
            add_mixed(2 * NC - 1)
            final(NC - 1)


def kernel(**inputs):
    import concourse.bacc as _bacc
    from concourse.bass_utils import run_bass_kernel_spmd as _run

    v = {k: np.asarray(x) for k, x in inputs.items()}
    lay = {
        "x": v["L0_attn_x_bld"],
        "c0T": v["L0_c"].T, "c1T": v["L1_c"].T, "wmod0": v["L0_wmod"], "wmod1": v["L1_wmod"],
        "wqT": v["L0_attn_Wq"].transpose(2, 1, 0), "wkT": v["L0_attn_Wk_up"].transpose(2, 1, 0),
        "wvT": v["L0_attn_Wv_up"].transpose(2, 1, 0), "wo": v["L0_attn_Wout"].transpose(1, 0, 2),
        "wkv": v["L0_attn_Wkv_down"],
        "bwT": v["L0_ffn_base_W"].T, "bb": v["L0_ffn_base_b"][:, None],
        "downT": np.concatenate([v["L0_ffn_shared_A"][None], v["L0_ffn_routed_A"]]).reshape(-1, D).T,
        "up": np.concatenate([v["L0_ffn_shared_B"][None], v["L0_ffn_routed_B"]]).transpose(0, 2, 1).reshape(-1, D),
        "rw": v["L0_ffn_router_W"].T, "rb": v["L0_ffn_router_b"],
        "wqkv": v["L1_attn_in_proj_w"].T, "bqkv": v["L1_attn_in_proj_b"].reshape(3, D).T,
        "owT": v["L1_attn_out_w"].T, "ob": v["L1_attn_out_b"][:, None],
        "nw": v["L1_ffn_norm_w"][:, None],
        "wrT": np.concatenate([v["L1_ffn_w_macro"], v["L1_ffn_w_micro"].reshape(E1, D)]).T,
        "w1": v["L1_ffn_w1"].transpose(2, 0, 1).reshape(D, E1 * F1),
        "w2": v["L1_ffn_w2"].reshape(E1, D, F1 // P, P).transpose(3, 0, 2, 1).reshape(P, E1 * F1),
    }
    nc = _bacc.Bacc("TRN2", target_bir_lowering=False, num_devices=1)
    arrays, args = {}, {}
    for name, x in lay.items():
        x = np.ascontiguousarray(x)
        arrays[f"in_{name}"] = x
        args[name] = nc.dram_tensor(f"in_{name}", x.shape, mybir.dt.from_np(x.dtype), kind="ExternalInput").ap()
    out = nc.dram_tensor("out", (B, L, D), F32, kind="ExternalOutput").ap()
    program(nc, args, out)
    r = _run(nc, [arrays], core_ids=[0])
    return r.results[0]["out"]
```
